# Optimizing a Trainium2 kernel written in Bass

```python
import numpy as np
import jax
import jax.numpy as jnp

def _softmax(x, axis=-1):
    return jax.nn.softmax(x, axis=axis)

def _gelu(x):
    return jax.nn.gelu(x, approximate=True)

def _silu(x):
    return jax.nn.silu(x)

def _sigmoid(x):
    return jax.nn.sigmoid(x)

def _layernorm(x, axis=-1, eps=1e-05):
    m = jnp.mean(x, axis=axis, keepdims=True)
    v = jnp.var(x, axis=axis, keepdims=True)
    return (x - m) / jnp.sqrt(v + eps)

def _scatter_add(tgt, idx, src, axis=0):
    return tgt.at[idx].add(src)

def _segment_sum(src, seg, n):
    return jax.ops.segment_sum(src, seg, n)
kernel_name = 'mk_macaron_d1_jaxref_r8_ea4a94'

def setup_inputs(seed: int=0):
    np.random.seed(seed)
    _w = jnp.asarray

    def _L0_attn_setup():
        import jax, jax.numpy as jnp
        import numpy as np
        B, S, D = (2, 256, 128)
        H, DH = (16, 64)
        DQL, DKVL = (64, 64)
        DR = 64
        TOPK = 64
        LN_EPS = 1e-05
        ROPE_BASE = 10000.0

        def _rope_tables(seq_len, dim):
            inv_freq = 1.0 / ROPE_BASE ** (np.arange(0, dim, 2, dtype=np.float32) / dim)
            t = np.arange(seq_len, dtype=np.float32)
            freqs = np.outer(t, inv_freq)
            cos = np.concatenate([np.cos(freqs), np.cos(freqs)], -1)[:, ::2]
            sin = np.concatenate([np.sin(freqs), np.sin(freqs)], -1)[:, ::2]
            return (jnp.asarray(cos), jnp.asarray(sin))

        def _apply_rope_subspace(x, d_rope):
            s = x.shape[-2]
            cos, sin = _rope_tables(s, d_rope)
            xr, xp = (x[..., :d_rope], x[..., d_rope:])
            e, o = (xr[..., 0::2], xr[..., 1::2])
            rot = jnp.stack([e * cos - o * sin, e * sin + o * cos], axis=-1).reshape(xr.shape)
            return jnp.concatenate([rot, xp], axis=-1)

        def _reference_tuple_inner(x, w_down_q, w_down_kv, w_up_q, w_up_k, w_up_v, w_out, ln_scale, ln_bias):
            b, s, d = x.shape
            residual = x
            mu = jnp.mean(x, axis=-1, keepdims=True)
            var = jnp.mean((x - mu) ** 2, axis=-1, keepdims=True)
            h = (x - mu) * jax.lax.rsqrt(var + LN_EPS) * ln_scale + ln_bias
            c_q = h @ w_down_q.T
            c_kv = h @ w_down_kv.T
            q = (c_q @ w_up_q.T).reshape(b, s, H, DH).transpose(0, 2, 1, 3)
            k = (c_kv @ w_up_k.T).reshape(b, s, H, DH).transpose(0, 2, 1, 3)
            v = (c_kv @ w_up_v.T).reshape(b, s, H, DH).transpose(0, 2, 1, 3)
            q = _apply_rope_subspace(q, DR)
            k = _apply_rope_subspace(k, DR)
            scale = 1.0 / np.sqrt(DH).astype(np.float32)
            scores = jnp.einsum('bhqd,bhkd->bhqk', q, k) * scale
            _, indices = jax.lax.top_k(scores, min(TOPK, s))
            attn = jax.nn.softmax(scores, axis=-1)
            out = jnp.einsum('bhqk,bhkd->bhqd', attn, v)
            out = out.transpose(0, 2, 1, 3).reshape(b, s, H * DH)
            out = out @ w_out.T + residual
            return (out, indices.astype(jnp.int64))
        key = jax.random.key(seed)
        ks = jax.random.split(key, 7)
        init = lambda k, shape: jax.random.normal(k, shape, jnp.float32) * 0.02
        return {'x': jax.random.normal(ks[0], (B, S, D), jnp.float32), 'w_down_q': init(ks[1], (DQL, D)), 'w_down_kv': init(ks[2], (DKVL, D)), 'w_up_q': init(ks[3], (H * DH, DQL)), 'w_up_k': init(ks[4], (H * DH, DKVL)), 'w_up_v': init(ks[5], (H * DH, DKVL)), 'w_out': init(ks[6], (D, H * DH)), 'ln_scale': jnp.ones((D,), jnp.float32), 'ln_bias': jnp.zeros((D,), jnp.float32)}
    _L0_attn_in = _L0_attn_setup()

    def _L0_ffn_setup():
        import jax, jax.numpy as jnp
        import numpy as np
        import math
        GOLDEN_CENTER = 1.0 / math.e
        GOLDEN_LOWER = 0.5 - math.log(4.0 / 3.0)
        GOLDEN_UPPER = 0.5
        B, T, D = (4, 256, 128)
        E = 8
        I = 512 // (E // 2)

        def _routing_weights(x, Wr, temperature):
            inh = jax.nn.sigmoid(x @ Wr / temperature)
            in_zone = (inh >= GOLDEN_LOWER) & (inh <= GOLDEN_UPPER)
            dist = jnp.abs(inh - GOLDEN_CENTER)
            w = jnp.exp(-dist / 0.1) * in_zone.astype(x.dtype)
            wsum = w.sum(axis=-1, keepdims=True)
            no_expert = wsum < 1e-08
            fb = jnp.exp(-dist / 0.3)
            _, top2 = jax.lax.top_k(fb, 2)
            fb_mask = jax.nn.one_hot(top2, E, dtype=x.dtype).sum(axis=-2)
            fb_w = fb * fb_mask
            fb_w = fb_w / jnp.clip(fb_w.sum(axis=-1, keepdims=True), 1e-08)
            w = jnp.where(no_expert, fb_w, w)
            wsum = w.sum(axis=-1, keepdims=True)
            return w / jnp.clip(wsum, 1e-08)
        key = jax.random.key(seed)
        k = jax.random.split(key, 6)
        s_d = 1.0 / math.sqrt(D)
        s_i = 1.0 / math.sqrt(I)
        return {'x': jax.random.normal(k[0], (B, T, D), jnp.float32), 'Wg': jax.random.normal(k[1], (E, D, I), jnp.float32) * s_d, 'Wu': jax.random.normal(k[2], (E, D, I), jnp.float32) * s_d, 'Wd': jax.random.normal(k[3], (E, I, D), jnp.float32) * s_i, 'Wr': jax.random.normal(k[4], (D, E), jnp.float32) * s_d, 'temperature': jnp.ones((1,), jnp.float32)}
    _L0_ffn_in = _L0_ffn_setup()
    _d = {'L0_attn_x': _L0_attn_in['x'], 'L0_attn_w_down_q': _L0_attn_in['w_down_q'], 'L0_attn_w_down_kv': _L0_attn_in['w_down_kv'], 'L0_attn_w_up_q': _L0_attn_in['w_up_q'], 'L0_attn_w_up_k': _L0_attn_in['w_up_k'], 'L0_attn_w_up_v': _L0_attn_in['w_up_v'], 'L0_attn_w_out': _L0_attn_in['w_out'], 'L0_attn_ln_scale': _L0_attn_in['ln_scale'], 'L0_attn_ln_bias': _L0_attn_in['ln_bias'], 'L0_ffn_Wg': _L0_ffn_in['Wg'], 'L0_ffn_Wu': _L0_ffn_in['Wu'], 'L0_ffn_Wd': _L0_ffn_in['Wd'], 'L0_ffn_Wr': _L0_ffn_in['Wr'], 'L0_ffn_temperature': _L0_ffn_in['temperature']}
    _x0 = _d['L0_attn_x']
    _d['L0_attn_x'] = jax.random.normal(jax.random.fold_in(jax.random.key(seed), 1), (4, 1024, 128), dtype=_x0.dtype)
    del _x0
    return _d

def reference(L0_attn_x, L0_attn_w_down_q, L0_attn_w_down_kv, L0_attn_w_up_q, L0_attn_w_up_k, L0_attn_w_up_v, L0_attn_w_out, L0_attn_ln_scale, L0_attn_ln_bias, L0_ffn_Wg, L0_ffn_Wu, L0_ffn_Wd, L0_ffn_Wr, L0_ffn_temperature):

    def _L0_attn_ref(x, w_down_q, w_down_kv, w_up_q, w_up_k, w_up_v, w_out, ln_scale, ln_bias):
        import jax, jax.numpy as jnp
        import numpy as np
        B, S, D = (2, 256, 128)
        H, DH = (16, 64)
        DQL, DKVL = (64, 64)
        DR = 64
        TOPK = 64
        LN_EPS = 1e-05
        ROPE_BASE = 10000.0

        def _rope_tables(seq_len, dim):
            inv_freq = 1.0 / ROPE_BASE ** (np.arange(0, dim, 2, dtype=np.float32) / dim)
            t = np.arange(seq_len, dtype=np.float32)
            freqs = np.outer(t, inv_freq)
            cos = np.concatenate([np.cos(freqs), np.cos(freqs)], -1)[:, ::2]
            sin = np.concatenate([np.sin(freqs), np.sin(freqs)], -1)[:, ::2]
            return (jnp.asarray(cos), jnp.asarray(sin))

        def _apply_rope_subspace(x, d_rope):
            s = x.shape[-2]
            cos, sin = _rope_tables(s, d_rope)
            xr, xp = (x[..., :d_rope], x[..., d_rope:])
            e, o = (xr[..., 0::2], xr[..., 1::2])
            rot = jnp.stack([e * cos - o * sin, e * sin + o * cos], axis=-1).reshape(xr.shape)
            return jnp.concatenate([rot, xp], axis=-1)

        def _reference_tuple_inner(x, w_down_q, w_down_kv, w_up_q, w_up_k, w_up_v, w_out, ln_scale, ln_bias):
            b, s, d = x.shape
            residual = x
            mu = jnp.mean(x, axis=-1, keepdims=True)
            var = jnp.mean((x - mu) ** 2, axis=-1, keepdims=True)
            h = (x - mu) * jax.lax.rsqrt(var + LN_EPS) * ln_scale + ln_bias
            c_q = h @ w_down_q.T
            c_kv = h @ w_down_kv.T
            q = (c_q @ w_up_q.T).reshape(b, s, H, DH).transpose(0, 2, 1, 3)
            k = (c_kv @ w_up_k.T).reshape(b, s, H, DH).transpose(0, 2, 1, 3)
            v = (c_kv @ w_up_v.T).reshape(b, s, H, DH).transpose(0, 2, 1, 3)
            q = _apply_rope_subspace(q, DR)
            k = _apply_rope_subspace(k, DR)
            scale = 1.0 / np.sqrt(DH).astype(np.float32)
            scores = jnp.einsum('bhqd,bhkd->bhqk', q, k) * scale
            _, indices = jax.lax.top_k(scores, min(TOPK, s))
            attn = jax.nn.softmax(scores, axis=-1)
            out = jnp.einsum('bhqk,bhkd->bhqd', attn, v)
            out = out.transpose(0, 2, 1, 3).reshape(b, s, H * DH)
            out = out @ w_out.T + residual
            return (out, indices.astype(jnp.int64))
        return _reference_tuple_inner(x, w_down_q, w_down_kv, w_up_q, w_up_k, w_up_v, w_out, ln_scale, ln_bias)[0]

    def _L0_ffn_ref(x, Wg, Wu, Wd, Wr, temperature):
        import jax, jax.numpy as jnp
        import numpy as np
        import math
        GOLDEN_CENTER = 1.0 / math.e
        GOLDEN_LOWER = 0.5 - math.log(4.0 / 3.0)
        GOLDEN_UPPER = 0.5
        B, T, D = (4, 256, 128)
        E = 8
        I = 512 // (E // 2)

        def _routing_weights(x, Wr, temperature):
            inh = jax.nn.sigmoid(x @ Wr / temperature)
            in_zone = (inh >= GOLDEN_LOWER) & (inh <= GOLDEN_UPPER)
            dist = jnp.abs(inh - GOLDEN_CENTER)
            w = jnp.exp(-dist / 0.1) * in_zone.astype(x.dtype)
            wsum = w.sum(axis=-1, keepdims=True)
            no_expert = wsum < 1e-08
            fb = jnp.exp(-dist / 0.3)
            _, top2 = jax.lax.top_k(fb, 2)
            fb_mask = jax.nn.one_hot(top2, E, dtype=x.dtype).sum(axis=-2)
            fb_w = fb * fb_mask
            fb_w = fb_w / jnp.clip(fb_w.sum(axis=-1, keepdims=True), 1e-08)
            w = jnp.where(no_expert, fb_w, w)
            wsum = w.sum(axis=-1, keepdims=True)
            return w / jnp.clip(wsum, 1e-08)
        weights = _routing_weights(x, Wr, temperature)
        gate = jnp.einsum('btd,edi->beti', x, Wg)
        up = jnp.einsum('btd,edi->beti', x, Wu)
        h = jax.nn.silu(gate) * up
        e_out = jnp.einsum('beti,eid->betd', h, Wd)
        out = jnp.einsum('bte,betd->btd', weights, e_out)
        return out
    x = L0_attn_x
    x = x + 0.5 * _L0_ffn_ref(_layernorm(x, axis=-1), L0_ffn_Wg, L0_ffn_Wu, L0_ffn_Wd, L0_ffn_Wr, L0_ffn_temperature)
    x = x + _L0_attn_ref(_layernorm(x, axis=-1), L0_attn_w_down_q, L0_attn_w_down_kv, L0_attn_w_up_q, L0_attn_w_up_k, L0_attn_w_up_v, L0_attn_w_out, L0_attn_ln_scale, L0_attn_ln_bias)
    x = x + 0.5 * _L0_ffn_ref(_layernorm(x, axis=-1), L0_ffn_Wg, L0_ffn_Wu, L0_ffn_Wd, L0_ffn_Wr, L0_ffn_temperature)
    return x

_drawn_inputs = setup_inputs


def setup_inputs(seed=0):
    import zlib

    import numpy as np

    out = dict(_drawn_inputs(seed))
    spreads = {'L0_attn_ln_scale': (1.0, 0.6), 'L0_attn_ln_bias': (0.0, 0.8)}
    factors = {'L0_attn_w_down_q': 8.0,
     'L0_attn_w_down_kv': 8.0,
     'L0_attn_w_up_q': 8.0,
     'L0_attn_w_up_k': 8.0,
     'L0_attn_w_up_v': 8.0,
     'L0_attn_w_out': 8.0}
    for name, (base, spread) in spreads.items():
        noise = np.random.default_rng([zlib.crc32(name.encode()), seed]).standard_normal(out[name].shape)
        drawn = base * np.exp(spread * noise) if base else spread * noise
        out[name] = jnp.asarray(drawn.astype(out[name].dtype))
    for name, factor in factors.items():
        out[name] = (out[name] * factor).astype(out[name].dtype)
    return out
```

```python
from contextlib import ExitStack

import numpy as np

import concourse.bass as bass
from concourse import mybir

F32 = mybir.dt.float32
F16 = mybir.dt.float16
ALU = mybir.AluOpType
ACT = mybir.ActivationFunctionType
AX = mybir.AxisListType

B, S, D = 4, 1024, 128
H, DH = 16, 64
E, I = 8, 128
P = 128
T = B * S
NT = T // P
NQ = T // 512
TB = S // P
PAIRS = H // 2
UNITS = B * PAIRS
EPS = 1e-5
ZONE_LOW = float(0.5 - np.log(4.0 / 3.0))
CENTER = float(1.0 / np.e)
Z_LOW = float(np.log(ZONE_LOW / (1.0 - ZONE_LOW)))
MAX_SCALE = 64.0


def rope_tables():
    inv_freq = 1.0 / 10000.0 ** (np.arange(0, DH, 2, dtype=np.float32) / DH)
    freqs = np.outer(np.arange(S, dtype=np.float32), inv_freq)
    cos = np.concatenate([np.cos(freqs), np.cos(freqs)], -1)[:, ::2]
    sin = np.concatenate([np.sin(freqs), np.sin(freqs)], -1)[:, ::2]
    sign = np.where(np.arange(DH) % 2 == 0, -1.0, 1.0)[:, None]
    c = np.repeat(cos.T, 2, axis=0)
    s = np.repeat(sin.T, 2, axis=0) * sign
    return np.stack([np.tile(c, (2, 1)), np.tile(s, (2, 1))], 1).astype(np.float32)


def build(nc, x, wg, wu, wd, wr, temp, wdq, wdkv, wuq, wuk, wuv, wo, lns, lnb, rope, out):
    with ExitStack() as ctx:
        def sb(name, shape, dt=F32):
            return ctx.enter_context(nc.sbuf_tensor(name, shape, dt))

        def sem(name):
            return ctx.enter_context(nc.semaphore(name))

        ps = ctx.enter_context(nc.psum_tensor("ps", [P, 8, 512], F32))

        xg = sb("xg", [P, B + 1, TB, D])
        xs = xg[:, 1:B + 1].rearrange("p b t d -> p (b t) d")
        ident = sb("ident", [P, P])
        ident16 = sb("ident16", [P, P], F16)
        xt_hi = sb("xt_hi", [P, T], F16)
        xt_lo = sb("xt_lo", [P, T], F16)
        w_ffn = {n: (sb(n + "_hi", [P, E, P], F16), sb(n + "_lo", [P, E, P], F16)) for n in ("wg", "wu", "wd")}
        wr_hi, wr_lo = sb("wr_hi", [P, E], F16), sb("wr_lo", [P, E], F16)
        rtemp = sb("rtemp", [P, 1])
        rev = sb("rev", [P, E])
        stat6 = sb("stat6", [P, NT, 6])
        mv = sb("mv", [P, NT, 2])
        half = sb("half", [P, NT])
        rs0 = sb("rs0", [P, NT])
        rs1 = sb("rs1", [P, NT])
        rstd = sb("rstd", [P, NT])
        cq_t, ckv_t = xt_hi, xt_lo
        CV = 2 * DH + 1
        cv_all = sb("cv_all", [P, NT, CV], F16)
        wc_hi = sb("wc_hi", [P, PAIRS, D], F16)
        wc_lo = sb("wc_lo", [P, PAIRS, D], F16)
        wup = sb("wup", [P, 4, 2, H * DH], F16)
        wd2 = sb("wd2", [P, 2, 3, P], F16)
        lnsb = sb("lnsb", [P, 2])
        cs = sb("cs", [P, 2, S])

        big = 26 * 1024
        area = sb("area", [P, big])
        area_at = [0]

        def carve(n, dt=F32):
            words = n if dt is F32 else n // 2
            a = area[:, area_at[0]:area_at[0] + words]
            area_at[0] += words
            assert area_at[0] <= big, area_at
            return a if dt is F32 else a.bitcast(dt)

        area_at[0] = 0
        st = {n: carve(E * P) for n in ("wg", "wu", "wd")}
        st_up = {n: carve(H * DH) for n in ("q", "k")}
        st_v = carve(PAIRS * DH)
        st_o = carve(PAIRS * D)
        st_dn = carve(2 * P)
        st_r = carve(E)
        s_x, s_w, s_up, s_small, s_rope = sem("x_loaded"), sem("ffn_w_loaded"), sem("up_w_loaded"), sem("small_loaded"), sem("rope_loaded")
        s_id, s_idz, s_c0 = sem("ident_ready"), sem("ident_zeroed"), sem("consts_ready")
        s_hi, s_lo, s_wc, s_sw = sem("w_hi_done"), sem("w_lo_done"), sem("wc_product"), sem("swap_done")
        s_wcr = sem("wc_read")
        s_rt = sem("rtemp_done")
        x_v = x.rearrange("(n p) d -> p n d", p=P)

        with nc.Block() as block:
            @block.sync
            def _(sp):
                for c in range(4):
                    sp.dma_start(xs[:, 8 * c:8 * c + 8, :], x_v[:, 8 * c:8 * c + 8, :]).then_inc(s_x, 16)
                sp.dma_start(st["wg"].rearrange("p (e i) -> p e i", e=E), wg.rearrange("e d i -> d e i")).then_inc(s_w, 16)
                sp.dma_start(st["wu"].rearrange("p (e i) -> p e i", e=E), wu.rearrange("e d i -> d e i")).then_inc(s_w, 16)
                sp.dma_start(st["wd"].rearrange("p (e i) -> p e i", e=E), wd.rearrange("e i d -> i e d")).then_inc(s_w, 16)
                sp.dma_start(st_r, wr).then_inc(s_w, 16)

            @block.scalar
            def _(act):
                for n, w in (("q", wuq), ("k", wuk)):
                    for r in range(2):
                        act.dma_start(st_up[n][64 * r:64 * r + 64, :], w).then_inc(s_up, 16)
                act.dma_start(st_v.rearrange("p (j r) -> p j r", j=PAIRS), wuv.rearrange("(j p) r -> p j r", p=P)).then_inc(s_small, 16)
                act.dma_start(st_o.rearrange("p (j d) -> p j d", j=PAIRS), wo.rearrange("(j p) d -> p j d", p=P)).then_inc(s_small, 16)
                act.dma_start(st_dn[:, 0:64], wdq).then_inc(s_small, 16)
                act.dma_start(st_dn[:, 64:128], wdkv).then_inc(s_small, 16)
                act.dma_start(lnsb[:, 0:1], lns.rearrange("(p a) -> p a", a=1)).then_inc(s_small, 16)
                act.dma_start(lnsb[:, 1:2], lnb.rearrange("(p a) -> p a", a=1)).then_inc(s_small, 16)
                act.dma_start(rtemp[:, 0:1], temp.rearrange("(p a) -> p a", a=1).broadcast_to([P, 1])).then_inc(s_small, 16)
                act.dma_start(cs[:], rope).then_inc(s_rope, 16)
                act.wait_ge(s_w, 64)
                for n in ("wg", "wu", "wd"):
                    nc.scalar.copy(w_ffn[n][0][:].rearrange("p e i -> p (e i)"), st[n]).then_inc(s_hi, 1)
                nc.scalar.copy(wr_hi[:], st_r).then_inc(s_hi, 1)
                act.wait_ge(s_up, 64)
                for k, n in ((0, "q"), (2, "k")):
                    nc.scalar.copy(wup[:, k, 0, :], st_up[n]).then_inc(s_hi, 1)
                act.wait_ge(s_rope, 16)
                act.wait_ge(s_small, 112)
                for k in range(2):
                    src = st_dn[:, 64 * k:64 * k + 64]
                    for r in range(2):
                        nc.scalar.copy(wd2[:, k, 0, 64 * r:64 * r + 64], src).then_inc(s_hi, 1)

            @block.vector
            def _(v):
                nc.vector.memset(half[:], -0.5).then_inc(s_c0, 1)
                nc.vector.memset(xg[:, 0], 0.0).then_inc(s_c0, 1)
                for e in range(E):
                    nc.vector.memset(rev[:, e:e + 1], float(E - e)).then_inc(s_c0, 1)
                v.wait_ge(s_w, 64)
                for k, n in enumerate(("wg", "wu", "wd")):
                    v.wait_ge(s_hi, k + 1)
                    nc.vector.tensor_tensor(w_ffn[n][1][:].rearrange("p e i -> p (e i)"), st[n],
                                            w_ffn[n][0][:].rearrange("p e i -> p (e i)"), ALU.subtract).then_inc(s_lo, 1)
                v.wait_ge(s_hi, 4)
                nc.vector.tensor_tensor(wr_lo[:], st_r, wr_hi[:], ALU.subtract).then_inc(s_lo, 1)
                v.wait_ge(s_up, 64)
                for j, (k, n) in enumerate(((0, "q"), (2, "k"))):
                    v.wait_ge(s_hi, 5 + j)
                    nc.vector.tensor_tensor(wup[:, k, 1, :], st_up[n], wup[:, k, 0, :], ALU.subtract).then_inc(s_lo, 1)
                v.wait_ge(s_small, 112)
                nc.vector.reciprocal(rtemp[:], rtemp[:]).then_inc(s_rt, 1)
                for k in range(2):
                    for r in range(2):
                        v.wait_ge(s_hi, 7 + 2 * k + r)
                        nc.vector.tensor_tensor(wd2[:, k, 1, 64 * r:64 * r + 64], st_dn[:, 64 * k:64 * k + 64],
                                                wd2[:, k, 0, 64 * r:64 * r + 64], ALU.subtract).then_inc(s_lo, 1)
                v.wait_ge(s_wc, 2 * PAIRS)
                for hh in range(2):
                    rows = slice(64 * hh, 64 * hh + 64)
                    for g in range(2):
                        bank = ps[rows, 2 * hh + g, :].rearrange("p (j d) -> p j d", d=D)
                        nc.vector.tensor_copy(wc_hi[rows, 4 * g:4 * g + 4, :], bank).then_inc(s_wcr, 1)
                        v.wait_ge(s_wcr, 2 * hh + g + 1)
                        nc.vector.tensor_tensor(wc_lo[rows, 4 * g:4 * g + 4, :], bank,
                                                wc_hi[rows, 4 * g:4 * g + 4, :], ALU.subtract).then_inc(s_lo, 1)

            @block.tensor
            def _(pe):
                pe.wait_ge(s_small, 112)
                for hh in range(2):
                    rows = slice(64 * hh, 64 * hh + 64)
                    for j in range(PAIRS):
                        nc.tensor.matmul(ps[rows, 2 * hh + j // 4, D * (j % 4):D * (j % 4) + D],
                                         st_v[rows, DH * j:DH * j + DH], st_o[rows, D * j:D * j + D],
                                         start=True, stop=True).then_inc(s_wc, 1)

            @block.gpsimd
            def _(pool):
                nc.gpsimd.memset(ident[:], 0.0).then_inc(s_idz, 1)
                nc.gpsimd.memset(ident16[:], 0.0).then_inc(s_idz, 1)
                pool.wait_ge(s_idz, 2)
                for m in (ident, ident16):
                    nc.gpsimd.affine_select(out=m[:], in_=m[:], compare_op=ALU.not_equal, fill=1.0, base=0,
                                            pattern=[[-1, P]], channel_multiplier=1).then_inc(s_id, 1)
                pool.wait_ge(s_lo, 6)
                for k in (0, 2):
                    for hl in range(2):
                        src = wup[:, k, hl, :].rearrange("p (n two) -> p n two", two=2)
                        dst = wup[:, k + 1, hl, :].rearrange("p (n two) -> p n two", two=2)
                        for a in range(2):
                            nc.gpsimd.tensor_copy(dst[:, :, a], src[:, :, 1 - a]).then_inc(s_sw, 1)

        def norm_stats(v, src, chain, s_var, s_pow):
            for n in range(NT):
                nc.vector.bn_stats(stat6[:, n, :], src[:, n, :]).then_inc(chain, 1)
            for n in range(NT):
                if n in (0, NT // 2):
                    v.wait_ge(chain, n + NT // 2)
                nc.vector.bn_aggr(mv[:, n, :], stat6[:, n, :]).then_inc(chain, 1)
            v.wait_ge(chain, 2 * NT)
            nc.vector.tensor_scalar(rs0[:], mv[:, :, 1], EPS, None, ALU.add).then_inc(s_var, 1)
            v.wait_ge(s_pow, 1)
            done = 2 * NT
            v.wait_ge(s_var, 1)
            for f in (lambda: nc.vector.tensor_tensor(rstd[:], rs1[:], rs1[:], ALU.mult),
                      lambda: nc.vector.tensor_tensor(rstd[:], rstd[:], rs0[:], ALU.mult),
                      lambda: nc.vector.tensor_scalar(rstd[:], rstd[:], -0.5, 1.5, ALU.mult, ALU.add),
                      lambda: nc.vector.tensor_tensor(rstd[:], rstd[:], rs1[:], ALU.mult)):
                f().then_inc(chain, 1)
                done += 1
                v.wait_ge(chain, done)
            return done

        def ffn(name):
            area_at[0] = 0
            xn = carve(2 * 512).rearrange("p (s j d) -> p s j d", s=2, j=4)
            gate = carve(2 * 512).rearrange("p (s n) -> p s n", s=2)
            gu = carve(2 * 512).rearrange("p (s n) -> p s n", s=2)
            hw = carve(2 * 512).rearrange("p (s n) -> p s n", s=2)
            h_hi = carve(2 * 512, F16).rearrange("p (s n) -> p s n", s=2)
            h_lo = carve(2 * 512, F16).rearrange("p (s n) -> p s n", s=2)
            r3 = [carve(NT * E).rearrange("p (t e) -> p t e", e=E) for _ in range(9)]
            z, inh, dist, w, fb, t0, t1, oh, fbm = r3
            r2 = [carve(NT) for _ in range(4)]
            w_hi = carve(NT * E, F16).rearrange("p (t e) -> p t e", e=E)
            w_lo = carve(NT * E, F16).rearrange("p (t e) -> p t e", e=E)
            s_ch, s_var, s_pow = sem(name + "_stats_chain"), sem(name + "_var"), sem(name + "_pow")
            s_xn, s_xT, s_xhi, s_xlo, s_xnf = (sem(name + n) for n in ("_xn", "_xT", "_xT_hi", "_xT_lo", "_xn_free"))
            s_z, s_zr, s_inh, s_dist, s_ex = (sem(name + n) for n in ("_logits", "_logits_read", "_inh", "_dist", "_exps"))
            s_rc, s_routed = sem(name + "_route_chain"), sem(name + "_route_done")

            with nc.Block() as block:
                @block.vector
                def _(v):
                    if name == "f1":
                        v.wait_ge(s_x, 64)
                    norm_stats(v, xs, s_ch, s_var, s_pow)
                    for q in range(NQ):
                        if q >= 2:
                            v.wait_ge(s_xT, 4 * (q - 1))
                        for j in range(4):
                            n = 4 * q + j
                            nc.vector.tensor_scalar(xn[:, q % 2, j, :], xs[:, n, :], mv[:, n, 0:1], rstd[:, n:n + 1],
                                                    ALU.subtract, ALU.mult).then_inc(s_xn, 1)
                        v.wait_ge(s_xhi, q + 1)
                        nc.vector.tensor_tensor(xt_lo[:, 512 * q:512 * q + 512], ps[:, q % 2, :],
                                                xt_hi[:, 512 * q:512 * q + 512], ALU.subtract).then_inc(s_xlo, 1)
                    v.wait_ge(s_z, 1)
                    v.wait_ge(s_rt, 1)
                    nc.vector.tensor_scalar(z, ps[:, 2, 0:NT * E].rearrange("p (t e) -> p t e", e=E), rtemp[:, 0:1],
                                            None, ALU.mult).then_inc(s_zr, 1)
                    v.wait_ge(s_inh, 1)
                    step = [0]

                    def link(ins):
                        step[0] += 1
                        ins.then_inc(s_rc, 1)
                        v.wait_ge(s_rc, step[0])

                    def wide(t):
                        return t.unsqueeze(2).broadcast_to([P, NT, E])
                    link(nc.vector.tensor_scalar(t0, inh, CENTER, None, ALU.subtract))
                    link(nc.vector.scalar_tensor_tensor(dist, t0, -1.0, t0, ALU.mult, ALU.max))
                    nc.vector.tensor_scalar(t1, dist, 1.0, None, ALU.mult).then_inc(s_dist, 1)
                    v.wait_ge(s_ex, 2)
                    v.wait_ge(s_dist, 1)
                    v.wait_ge(s_zr, 1)
                    link(nc.vector.tensor_scalar(t0, z, Z_LOW, None, ALU.is_ge))
                    link(nc.vector.scalar_tensor_tensor(t0, z, 0.0, t0, ALU.is_le, ALU.mult))
                    link(nc.vector.tensor_tensor(w, w, t0, ALU.mult))
                    link(nc.vector.tensor_reduce(r2[0], w, AX.X, ALU.add))
                    link(nc.vector.tensor_scalar(r2[1], r2[0], 1e-8, None, ALU.is_lt))
                    link(nc.vector.tensor_copy(fbm, fb))
                    for k in range(2):
                        link(nc.vector.tensor_reduce(r2[2], fbm, AX.X, ALU.max))
                        link(nc.vector.tensor_tensor(t0, fbm, wide(r2[2]), ALU.is_equal))
                        link(nc.vector.tensor_tensor(t0, t0, rev[:].unsqueeze(1).broadcast_to([P, NT, E]), ALU.mult))
                        link(nc.vector.tensor_reduce(r2[2], t0, AX.X, ALU.max))
                        dst = oh if k == 0 else t1
                        link(nc.vector.tensor_tensor(dst, t0, wide(r2[2]), ALU.is_equal))
                        if k == 0:
                            link(nc.vector.scalar_tensor_tensor(fbm, oh, -4.0, fbm, ALU.mult, ALU.add))
                    link(nc.vector.tensor_tensor(oh, oh, t1, ALU.add))
                    link(nc.vector.tensor_tensor(fb, fb, oh, ALU.mult))
                    link(nc.vector.tensor_reduce(r2[2], fb, AX.X, ALU.add))
                    link(nc.vector.tensor_scalar(r2[2], r2[2], 1e-8, None, ALU.max))
                    link(nc.vector.reciprocal(r2[3], r2[2]))
                    link(nc.vector.tensor_tensor(r2[3], r2[3], r2[1], ALU.mult))
                    link(nc.vector.tensor_tensor(fb, fb, wide(r2[3]), ALU.mult))
                    link(nc.vector.tensor_scalar(r2[1], r2[1], -1.0, 1.0, ALU.mult, ALU.add))
                    link(nc.vector.tensor_tensor(w, w, wide(r2[1]), ALU.mult))
                    link(nc.vector.tensor_tensor(w, w, fb, ALU.add))
                    link(nc.vector.tensor_reduce(r2[2], w, AX.X, ALU.add))
                    link(nc.vector.tensor_scalar(r2[2], r2[2], 1e-8, None, ALU.max))
                    link(nc.vector.reciprocal(r2[3], r2[2]))
                    link(nc.vector.tensor_tensor(w, w, wide(r2[3]), ALU.mult))
                    link(nc.vector.tensor_copy(w_hi, w))
                    nc.vector.tensor_tensor(w_lo, w, w_hi, ALU.subtract).then_inc(s_routed, 1)

                @block.gpsimd
                def _(pool):
                    pool.wait_ge(s_var, 1)
                    if name == "f1":
                        pool.wait_ge(s_c0, 10)
                    nc.gpsimd.tensor_tensor(rs1[:], rs0[:], half[:], ALU.pow).then_inc(s_pow, 1)

                @block.scalar
                def _(act):
                    for q in range(NQ):
                        act.wait_ge(s_xT, 4 * (q + 1))
                        nc.scalar.copy(xt_hi[:, 512 * q:512 * q + 512], ps[:, q % 2, :]).then_inc(s_xhi, 1)
                    act.wait_ge(s_zr, 1)
                    nc.scalar.activation(inh, z, ACT.Sigmoid).then_inc(s_inh, 1)
                    act.wait_ge(s_dist, 1)
                    nc.scalar.activation(w, dist, ACT.Exp, scale=-1.0 / 0.1).then_inc(s_ex, 1)
                    nc.scalar.activation(fb, dist, ACT.Exp, scale=-1.0 / 0.3).then_inc(s_ex, 1)

                @block.tensor
                def _(pe):
                    pe.wait_ge(s_id, 2)

                    def route(q):
                        pe.wait_ge(s_xlo, q + 1)
                        for j in range(4):
                            n = 4 * q + j
                            cols = slice(P * n, P * n + P)
                            for k, (a, b) in enumerate(((xt_hi, wr_hi), (xt_hi, wr_lo), (xt_lo, wr_hi))):
                                last = nc.tensor.matmul(ps[:, 2, E * n:E * n + E], a[:, cols], b[:],
                                                        start=(n == 0 and k == 0), stop=(k == 2), skip_group_check=True)
                        return last
                    for q in range(NQ):
                        pe.wait_ge(s_xn, 4 * (q + 1))
                        if q >= 2:
                            pe.wait_ge(s_xlo, q - 1)
                        for j in range(4):
                            nc.tensor.transpose(ps[:, q % 2, P * j:P * j + P], xn[:, q % 2, j, :], ident[:]).then_inc(s_xT, 1)
                        if q >= 1:
                            route(q - 1)
                    route(NQ - 1).then_inc(s_z, 1)

            s_g, s_u, s_wb = (sem(name + n) for n in ("_gate", "_up", "_wbcast"))
            s_si, s_gu, s_hw = sem(name + "_silu"), sem(name + "_gate_up"), sem(name + "_h")
            s_hh, s_hl, s_dn = sem(name + "_h_hi"), sem(name + "_h_lo"), sem(name + "_down")
            s_y0 = sem(name + "_y_zeroed")
            s_wcur, s_y = sem(name + "_w_current"), sem(name + "_y_added")
            (g_hi, g_lo), (u_hi, u_lo), (d_hi, d_lo) = (w_ffn[n] for n in ("wg", "wu", "wd"))
            w_cur = carve(2 * 2 * 4 * E, F16).rearrange("p (s h j e) -> p s h j e", s=2, h=2, j=4)

            def turns(eng, body):
                with eng.Fori(0, NQ // 2 - 1) as it:
                    body(it * 16, it * 2, False)
                body((NQ // 2 - 1) * 16, NQ - 2, True)

            with nc.Block() as block:
                @block.tensor
                def _(pe):
                    def up_part(i, q, k):
                        e, b = k % E, k % 2
                        cols = bass.ds(q * 512, 512)
                        for w_h, w_l, bank, read, done in ((g_hi, g_lo, 0, s_si, s_g), (u_hi, u_lo, 2, s_gu, s_u)):
                            if k >= 2:
                                pe.wait_ge(read, i - 1 if read is s_si else i)
                            o = ps[:, bank + b, :]
                            nc.tensor.matmul(o, w_h[:, e, :], xt_hi[:, cols], start=True, stop=False)
                            nc.tensor.matmul(o, w_h[:, e, :], xt_lo[:, cols], start=False, stop=False)
                            nc.tensor.matmul(o, w_l[:, e, :], xt_hi[:, cols], start=False, stop=True).then_inc(done, 1)
                        if k >= 2:
                            pe.wait_ge(s_hw, i - 1)
                        if e == 0:
                            pe.wait_ge(s_wcur, q + 1)
                        for j in range(4):
                            for h in range(2):
                                col = w_cur[:, (k // E) % 2, h, j, e:e + 1].broadcast_to([P, P])
                                last = nc.tensor.matmul(ps[:, 4 + b, P * j:P * j + P], col, ident16[:],
                                                        start=(h == 0 and j == 0), stop=(h == 1), skip_group_check=True)
                        last.then_inc(s_wb, 1)

                    def down_part(i, q, k):
                        e, b = k % E, k % 2
                        pe.wait_ge(s_hh, i + 1)
                        pe.wait_ge(s_hl, i + 3)
                        if e == 0:
                            pe.wait_ge(s_y, q + 1)
                        for j in range(4):
                            o = ps[:, 6 + (k // E) % 2, P * j:P * j + P]
                            cols = slice(P * j, P * j + P)
                            nc.tensor.matmul(o, h_hi[:, b, cols], d_hi[:, e, :], start=(e == 0 and j == 0), stop=False,
                                             skip_group_check=True)
                            nc.tensor.matmul(o, h_hi[:, b, cols], d_lo[:, e, :], start=False, stop=False, skip_group_check=True)
                            last = nc.tensor.matmul(o, h_lo[:, b, cols], d_hi[:, e, :], start=False, stop=(e == E - 1),
                                                    skip_group_check=True)
                        last.then_inc(s_dn, 1)

                    def turn(base, q0, last):
                        for k in range(16):
                            if not (last and k >= 14):
                                up_part(base + (k + 2), q0 + (k + 2) // E, k + 2)
                            down_part(base + k, q0 + k // E, k)
                    pe.sem_inc(s_dn, 2)
                    up_part(0, 0, 0)
                    up_part(1, 0, 1)
                    turns(pe, turn)

                @block.scalar
                def _(act):
                    def silu(i, k):
                        act.wait_ge(s_g, i + 1)
                        if k:
                            act.wait_ge(s_gu, i)
                        nc.scalar.activation(gate[:, k % 2, :], ps[:, k % 2, :], ACT.Silu).then_inc(s_si, 1)

                    def turn(base, q0, last):
                        for k in range(16):
                            if not (last and k == 15):
                                silu(base + (k + 1), k + 1)
                            act.wait_ge(s_hw, base + (k + 1))
                            act.wait_ge(s_dn, base + (k + 1))
                            nc.scalar.copy(h_hi[:, k % 2, :], hw[:, k % 2, :]).then_inc(s_hh, 1)
                    silu(0, 0)
                    turns(act, turn)

                @block.gpsimd
                def _(pool):
                    def turn(base, q0, last):
                        for k in range(16):
                            pool.wait_ge(s_hh, base + (k + 1))
                            pool.wait_ge(s_dn, base + (k + 1))
                            nc.gpsimd.tensor_tensor(h_lo[:, k % 2, :], hw[:, k % 2, :], h_hi[:, k % 2, :],
                                                    ALU.subtract).then_inc(s_hl, 1)
                    pool.sem_inc(s_hl, 2)
                    turns(pool, turn)

                @block.vector
                def _(v):
                    def weights(q, slot):
                        for h, src in enumerate((w_hi, w_lo)):
                            ins = nc.vector.tensor_copy(w_cur[:, slot, h], src[:, bass.ds(q * 4, 4), :])
                        ins.then_inc(s_wcur, 1)

                    def add_y(q, slot):
                        v.wait_ge(s_dn, q * E + 2)
                        xq = xg[:].rearrange("p b t d -> p (b t) d")[:, bass.ds(q * 4 + (TB - 4), 4), :]
                        y = ps[:, 6 + slot, :].rearrange("p (t d) -> p t d", d=D)
                        nc.vector.scalar_tensor_tensor(xq, y, 0.5, xq, ALU.mult, ALU.add).then_inc(s_y, 1)

                    def turn(base, q0, last):
                        for k in range(16):
                            i, q, b, e = base + k, q0 + k // E, k % 2, k % E
                            v.wait_ge(s_si, i + 1)
                            v.wait_ge(s_u, i + 1)
                            nc.vector.tensor_tensor(gu[:, b, :], gate[:, b, :], ps[:, 2 + b, :], ALU.mult).then_inc(s_gu, 1)
                            v.wait_ge(s_gu, i + 2)
                            v.wait_ge(s_wb, i + 1)
                            v.wait_ge(s_hl, i + 1)
                            nc.vector.tensor_tensor(hw[:, b, :], gu[:, b, :], ps[:, 4 + b, :], ALU.mult).then_inc(s_hw, 1)
                            if e == 3:
                                add_y(q, (k // E + 1) % 2)
                            if e == 4 and not (last and k > E):
                                weights(q + 1, (k // E + 1) % 2)
                    v.sem_inc(s_gu, 1)
                    v.sem_inc(s_y, 1)
                    nc.vector.memset(ps[:, 7, :], 0.0).then_inc(s_y0, 1)
                    v.wait_ge(s_y0, 1)
                    weights(0, 0)
                    turns(v, turn)
                    add_y(NQ, 1)

        ffn("f1")
        area_at[0] = 0
        y = carve(NT * D).rearrange("p (t d) -> p t d", d=D)
        yn = carve(2 * 512).rearrange("p (s j d) -> p s j d", s=2, j=4)
        h32 = carve(2 * 512).rearrange("p (s n) -> p s n", s=2)
        hh_hi = carve(2 * 512, F16).rearrange("p (s n) -> p s n", s=2)
        hh_lo = carve(2 * 512, F16).rearrange("p (s n) -> p s n", s=2)
        s_ch, s_var, s_pow = sem("a1_chain"), sem("a1_var"), sem("a1_pow")
        s_ch2, s_var2, s_pow2 = sem("a2_chain"), sem("a2_var"), sem("a2_pow")
        s_yy, s_yr, s_yn, s_yT = sem("y_done"), sem("y_residual"), sem("yn_done"), sem("yT_done")
        s_h32, s_hhi, s_hlo = sem("h32_done"), sem("hT_hi"), sem("hT_lo")
        s_lat, s_lhi, s_llo, s_one = sem("latents_product"), sem("latents_hi"), sem("latents_lo"), sem("cv_ones")
        with nc.Block() as block:
            @block.gpsimd
            def _(pool):
                pool.wait_ge(s_var, 1)
                nc.gpsimd.tensor_tensor(rs1[:], rs0[:], half[:], ALU.pow).then_inc(s_pow, 1)
                pool.wait_ge(s_var2, 1)
                nc.gpsimd.tensor_tensor(rs1[:], rs0[:], half[:], ALU.pow).then_inc(s_pow2, 1)

            @block.vector
            def _(v):
                norm_stats(v, xs, s_ch, s_var, s_pow)
                nc.vector.memset(cv_all[:, :, DH:DH + 1], 1.0).then_inc(s_one, 1)
                for n in range(NT):
                    nc.vector.tensor_scalar(y[:, n, :], xs[:, n, :], mv[:, n, 0:1], rstd[:, n:n + 1],
                                            ALU.subtract, ALU.mult).then_inc(s_yy, 1)
                v.wait_ge(s_yy, NT)
                norm_stats(v, y, s_ch2, s_var2, s_pow2)
                for b in range(B):
                    nc.vector.tensor_tensor(xs[:, TB * b:TB * b + TB, :], xs[:, TB * b:TB * b + TB, :],
                                            y[:, TB * b:TB * b + TB, :], ALU.add).then_inc(s_yr, 1)
                for q in range(NQ + 1):
                    if q < NQ:
                        if q >= 2:
                            v.wait_ge(s_yT, 4 * (q - 1))
                        for j in range(4):
                            n = 4 * q + j
                            nc.vector.tensor_scalar(yn[:, q % 2, j, :], y[:, n, :], mv[:, n, 0:1], rstd[:, n:n + 1],
                                                    ALU.subtract, ALU.mult).then_inc(s_yn, 1)
                        v.wait_ge(s_hhi, q + 1)
                        if q >= 2:
                            v.wait_ge(s_lat, 3 * (q - 1))
                        nc.vector.tensor_tensor(hh_lo[:, q % 2, :], h32[:, q % 2, :], hh_hi[:, q % 2, :],
                                                ALU.subtract).then_inc(s_hlo, 1)
                    if q >= 1:
                        p, cols = q - 1, slice(512 * q - 512, 512 * q)
                        for k, dst in enumerate((cq_t, ckv_t)):
                            v.wait_ge(s_lhi, 3 * p + k + 1)
                            nc.vector.tensor_tensor(dst[64:128, cols], ps[64:128, 2 + k, :], dst[64:128, cols],
                                                    ALU.subtract).then_inc(s_llo, 1)
                        v.wait_ge(s_lhi, 3 * p + 3)
                        cvt = cv_all[:, 4 * p:4 * p + 4, :]
                        nc.vector.tensor_tensor(cvt[:, :, DH + 1:CV], ps[:, 4, 0:256].rearrange("p (t r) -> p t r", r=DH),
                                                cvt[:, :, 0:DH], ALU.subtract).then_inc(s_llo, 1)

            @block.scalar
            def _(act):
                def latents(q):
                    cols = slice(512 * q, 512 * q + 512)
                    for k, dst in enumerate((cq_t, ckv_t)):
                        act.wait_ge(s_lat, 3 * q + k + 1)
                        nc.scalar.copy(dst[:, cols], ps[:, 2 + k, :]).then_inc(s_lhi, 1)
                    act.wait_ge(s_lat, 3 * q + 3)
                    nc.scalar.copy(cv_all[:, 4 * q:4 * q + 4, 0:DH], ps[:, 4, 0:256].rearrange("p (t r) -> p t r", r=DH)).then_inc(s_lhi, 1)
                for q in range(NQ):
                    act.wait_ge(s_yT, 4 * (q + 1))
                    if q >= 2:
                        act.wait_ge(s_hlo, q - 1)
                    nc.scalar.activation(h32[:, q % 2, :], ps[:, q % 2, :], ACT.Identity, scale=lnsb[:, 0:1],
                                         bias=lnsb[:, 1:2]).then_inc(s_h32, 1)
                    act.wait_ge(s_h32, q + 1)
                    if q >= 2:
                        act.wait_ge(s_lat, 3 * (q - 1))
                    nc.scalar.copy(hh_hi[:, q % 2, :], h32[:, q % 2, :]).then_inc(s_hhi, 1)
                    if q >= 1:
                        latents(q - 1)
                latents(NQ - 1)

            @block.tensor
            def _(pe):
                for q in range(NQ):
                    pe.wait_ge(s_yn, 4 * (q + 1))
                    if q >= 2:
                        pe.wait_ge(s_h32, q - 1)
                    for j in range(4):
                        nc.tensor.transpose(ps[:, q % 2, P * j:P * j + P], yn[:, q % 2, j, :], ident[:]).then_inc(s_yT, 1)
                    pe.wait_ge(s_hlo, q + 1)
                    if q >= 1:
                        pe.wait_ge(s_llo, 3 * q)
                    a_hi, a_lo = hh_hi[:, q % 2, :], hh_lo[:, q % 2, :]
                    for k in range(2):
                        for m, (w_, a_) in enumerate(((0, a_hi), (0, a_lo), (1, a_hi))):
                            last = nc.tensor.matmul(ps[:, 2 + k, :], wd2[:, k, w_, :], a_, start=(m == 0), stop=(m == 2))
                        last.then_inc(s_lat, 1)
                    for j in range(4):
                        cols = slice(P * j, P * j + P)
                        for m, (a_, w_) in enumerate(((a_hi, 0), (a_hi, 1), (a_lo, 0))):
                            last = nc.tensor.matmul(ps[:, 4, DH * j:DH * j + DH], a_[:, cols], wd2[:, 1, w_, 0:DH],
                                                    start=(j == 0 and m == 0), stop=(m == 2), skip_group_check=True)
                    last.then_inc(s_lat, 1)

        area_at[0] = 0
        qk = {n: carve(4 * S, F16).rearrange("p (u h n) -> p u h n", u=2, h=2) for n in ("Q1", "Q2", "K1", "K2")}
        p32 = carve(2 * 1024).rearrange("p (s n) -> p s n", s=2)
        p_hi = carve(4 * 1024, F16).rearrange("p (s n) -> p s n", s=4)
        p_lo = carve(4 * 1024, F16).rearrange("p (s n) -> p s n", s=4)
        ra = carve(2 * 512).rearrange("p (s n) -> p s n", s=2)
        rb = carve(2 * 512).rearrange("p (s n) -> p s n", s=2)
        rc = carve(2 * 512).rearrange("p (s n) -> p s n", s=2)
        r_hi = carve(4 * 512, F16).rearrange("p (c n) -> p c n", c=4)
        r_lo = carve(4 * 512, F16).rearrange("p (c n) -> p c n", c=4)
        cx = carve(TB * P).rearrange("p (t n) -> p t n", t=TB)
        cxt_hi = carve(S, F16).rearrange("p (t n) -> p t n", t=TB)
        cxt_lo = carve(S, F16).rearrange("p (t n) -> p t n", t=TB)
        lat = carve(2 * S, F16).rearrange("p (k n) -> p k n", k=2)
        wu_cur = carve(8 * P, F16).rearrange("p (w h n) -> p w h n", w=4, h=2)
        cv_cur = carve(2 * TB * CV, F16).rearrange("p (s t r) -> p s t r", s=2, t=TB)
        wc_cur = carve(2 * 2 * D, F16).rearrange("p (s h d) -> p s h d", s=2, h=2)
        mx = carve(2 * 16).rearrange("p (a k q) -> p a k q", a=2, k=2)
        mm = carve(2 * 8).rearrange("p (a q) -> p a q", a=2)
        m16 = carve(2 * 8, F16).rearrange("p (a q) -> p a q", a=2)
        mt = carve(2 * P, F16).rearrange("p (a n) -> p a n", a=2)
        rsum = carve(4)
        s_qz = sem("qk_zeroed")
        s_op = sem("operands_loaded")
        s_cv, s_wcc = ([sem(f"{n}_loaded_{k}") for k in range(2)] for n in ("cv", "wc"))
        s_mf, s_mr = sem("misc_filled"), sem("misc_read")
        s_rc, s_rh, s_rl = sem("rotated_sum"), sem("rotated_hi"), sem("rotated_lo")
        s_sq, s_sk = sem("q_stacked"), sem("k_stacked")
        s_mch, s_m16, s_mrow = sem("max_chain"), sem("max_f16"), sem("max_row_stored")
        s_s, s_e32, s_e16 = sem("scores"), sem("exp_f32"), sem("exp_hi")
        s_pd, s_pp = sem("p_lo_dve"), sem("p_lo_pool")
        s_pv, s_rs, s_cx = sem("pv"), sem("row_sums_inverted"), sem("context")
        s_oh = sem("context_T_hi")
        DC = 416
        ROT_SUM, ROT_HI, ROT_LO = 7, 8, 9
        STEPS = 16
        IT = UNITS // 2

        plan = {s: [] for s in range(STEPS)}
        for kind, of_step in ((("A", 0, 1), {0: 3, 1: 3, 2: 2}),
                              (("A", 1, 0), {3: 1, 4: 2, 5: 2, 6: 2, 7: 2, 8: 2, 9: 2, 10: 2, 11: 1}),
                              (("A", 1, 1), {12: 1, 13: 3, 14: 2, 15: 2})):
            i = 8 if kind == ("A", 0, 1) else 0
            for s, n in of_step.items():
                plan[s] += [(*kind, i + m) for m in range(n)]
                i += n
        plan[2] += [("OT", -1, 0, 0), ("OT", -1, 0, 1)]
        plan[3] = [plan[3][0], ("M", 0, 1, 0), ("OP", -1, 0, 0)]
        plan[4].append(("OP", -1, 0, 1))
        for i in range(8):
            plan[5 + i].append(("R", 2, 0, i))
        plan[12].append(("M", 1, 0, 0))
        before = ([("R", 0, 0, i) for i in range(8)] + [("R", 1, 0, i) for i in range(8)]
                  + [("A", 0, 0, i) for i in range(16)] + [("M", 0, 0, 0)] + [("A", 0, 1, i) for i in range(8)])

        after = [("OT", -1, 0, 0), ("OT", -1, 0, 1), ("OP", -1, 0, 0), ("OP", -1, 0, 1)]

        def items(s, left):
            return [i for i in plan[s] if i[1] <= left]
        per_unit = sum(len(p) for p in plan.values())

        def read_by(item, left=9):
            return [i for s in range(STEPS) for i in items(s, left)].index(item) + 1

        def run_units(eng, prologue, unit):
            prologue()
            n0 = len(before)
            with eng.Fori(0, IT - 1) as it:
                for k in range(2):
                    unit(it * 2 + k, k, 9, it * (2 * per_unit) + (n0 + k * per_unit), (n0 + k * per_unit) % 2)
            n = n0 + (IT - 1) * 2 * per_unit
            for k in range(2):
                unit(UNITS - 2 + k, k, 1 - k, n, n % 2)
                n += sum(len(items(s, 1 - k)) for s in range(STEPS))
            return n

        with nc.Block() as block:
            @block.tensor
            def _(pe):
                def misc(item, u, k, n, par, ot_read=None):
                    kind, off, hd, i = item
                    w, slot = u + off, (k + off) % 2
                    bank = ps[:, 6 + par, :]
                    if not (isinstance(n, int) and n < 2):
                        pe.wait_ge(s_mr, n - 1)
                    if kind == "R":
                        c, half_, sw = i // 2, (i // 2) % 2, i % 2
                        if i == 0:
                            pe.wait_ge(s_op, (w + 1) * 48)
                        which = 2 * (c // 2) + sw
                        src = lat[:, c // 2, 512 * half_:512 * half_ + 512]
                        nc.tensor.matmul(bank, wu_cur[:, which, 0, :], src, start=True, stop=False)
                        last = nc.tensor.matmul(bank, wu_cur[:, which, 1, :], src, start=False, stop=True)
                    elif kind == "A":
                        if i == 0 and hd == 0:
                            pe.wait_ge(s_sq, (w + 1) * 96)
                            pe.wait_ge(s_sk, (w + 1) * 96)
                        qt, kh = i // 2, i % 2
                        last = nc.tensor.matmul(bank, qk["Q1"][:, slot, hd, P * qt:P * qt + P],
                                                qk["K1"][:, slot, hd, 512 * kh:512 * kh + 512], start=True, stop=True)
                    elif kind == "M":
                        pe.wait_ge(s_m16, w * 2 + (hd + 1))
                        last = nc.tensor.matmul(bank[0:8, 0:P], m16[:, hd, :], ident16[:], start=True, stop=True)
                    elif kind == "OT":
                        pe.wait_ge(s_cx, u * 4 + 2)
                        for t in range(4):
                            last = nc.tensor.transpose(bank[:, P * t:P * t + P], cx[:, 4 * i + t, :], ident[:])
                    else:
                        pe.wait_ge(s_oh, u * 2 + (i + 1))
                        pe.wait_ge(s_mr, ot_read[i])
                        if i == 0:
                            pe.wait_ge(s_wcc[slot], (u + (2 - k)) * 16)
                        for t in range(4):
                            a = [c_[:, 4 * i + t, :] for c_ in (cxt_hi, cxt_lo)]
                            for m, (x_, y_) in enumerate(((0, 0), (0, 1), (1, 0))):
                                last = nc.tensor.matmul(bank[:, P * t:P * t + P], a[x_], wc_cur[:, slot, y_, :],
                                                        start=(t == 0 and m == 0), stop=(m == 2), skip_group_check=True)
                    last.then_inc(s_mf, 1)

                def scores(u, k, s, kk):
                    hd, qh, kt = s // 8, (s // 4) % 2, 2 * (s % 4) + kk
                    if s % 8 == 0 and kk == 0:
                        pe.wait_ge(s_mrow, (u * 2 + (hd + 2)) * 16)
                    o = ps[:, 2 * (s % 2) + kk, :]
                    keys, qs = slice(P * kt, P * kt + P), slice(512 * qh, 512 * qh + 512)
                    nc.tensor.matmul(o, qk["K1"][:, k, hd, keys], qk["Q1"][:, k, hd, qs], start=True, stop=False)
                    return nc.tensor.matmul(o, qk["K2"][:, k, hd, keys], qk["Q2"][:, k, hd, qs], start=False, stop=True)

                def pv(u, k, s, kk):
                    kt = 2 * (s % 4) + kk
                    g = u * STEPS + s
                    if kk == 0:
                        if s == 0:
                            pe.wait_ge(s_cv[k], (u + (2 - k)) * 8)
                        if s % 4 == 0:
                            pe.wait_ge(s_cx, u * 4 + (s // 4 + 1))
                        pe.wait_ge(s_pd, g + 2)
                        pe.wait_ge(s_pp, g + 2)
                    for j in range(4):
                        c = 512 * kk + P * j
                        o = ps[:, 4 + (s // 4) % 2, (DH + 1) * j:(DH + 1) * (j + 1)]
                        first = kt == 0 and j == 0
                        nc.tensor.matmul(o, p_hi[:, s % 4, c:c + P], cv_cur[:, k, kt, 0:DH + 1], start=first, stop=False,
                                         skip_group_check=True)
                        nc.tensor.matmul(o[:, 0:DH], p_hi[:, s % 4, c:c + P], cv_cur[:, k, kt, DH + 1:CV], start=False,
                                         stop=False, skip_group_check=True)
                        last = nc.tensor.matmul(o, p_lo[:, s % 4, c:c + P], cv_cur[:, k, kt, 0:DH + 1], start=False,
                                                stop=(kt == 7), skip_group_check=True)
                    return last

                def prologue():
                    pe.sem_inc(s_pv, 3)
                    for n, item in enumerate(before):
                        misc(item, 0, 0, n, n % 2)
                    for s in range(2):
                        scores(0, 0, s, 0)
                        scores(0, 0, s, 1).then_inc(s_s, 1)

                def unit(u, k, left, n, par):
                    ot_read = [n + read_by(("OT", -1, 0, i), left) for i in range(2)]
                    for s in range(STEPS):
                        work = []
                        if s + 2 < STEPS or left >= 1:
                            t, v_, k_ = ((s + 2), u, k) if s + 2 < STEPS else (s + 2 - STEPS, u + 1, 1 - k)

                            def half0(t=t, v_=v_, k_=k_, s=s):
                                pe.wait_ge(s_e16, u * STEPS + (s + 1))
                                scores(v_, k_, t, 0)

                            def half1(t=t, v_=v_, k_=k_):
                                scores(v_, k_, t, 1).then_inc(s_s, 1)
                            work += [half0, half1]
                        work += [lambda s=s: pv(u, k, s, 0), lambda s=s: pv(u, k, s, 1).then_inc(s_pv, 1)]
                        todo = items(s, left)
                        todo = list(todo)
                        for c in "wiwiwiwiii":
                            if c == "i" and todo:
                                misc(todo.pop(0), u, k, n, par, ot_read)
                                n, par = n + 1, 1 - par
                            if c == "w" and work:
                                work.pop(0)()
                n = run_units(pe, prologue, unit)
                for m, item in enumerate(after):
                    misc(item, UNITS, 0, n + m, (n + m) % 2, [n + 1, n + 2])

            @block.vector
            def _(v):
                def misc(item, u, k, n, par):
                    kind, off, hd, i = item
                    w = u + off
                    bank = ps[:, 6 + par, :]
                    v.wait_ge(s_mf, n + 1)
                    if kind == "R":
                        c, half_, sw = i // 2, (i // 2) % 2, i % 2
                        if not (isinstance(w, int) and w == 0 and c < 2):
                            v.wait_ge(s_rc, w * 4 + (c - 1))
                        nc.vector.tensor_tensor((ra, rb)[sw][:, c % 2, :], bank, cs[:, sw, 512 * half_:512 * half_ + 512],
                                                ALU.mult).then_inc(s_mr, 1)
                    elif kind == "A":
                        qt, kh = i // 2, i % 2
                        nc.vector.tensor_reduce(mx[:, hd, kh, qt:qt + 1], bank, AX.X, ALU.max).then_inc(s_mr, 1)
                        if i == 15:
                            v.wait_ge(s_mr, n + 1)
                            nc.vector.tensor_tensor(mm[:, hd, :], mx[:, hd, 0, :], mx[:, hd, 1, :], ALU.max).then_inc(s_mch, 1)
                            v.wait_ge(s_mch, w * 2 + (hd + 1))
                            nc.vector.tensor_scalar(m16[:, hd, :], mm[:, hd, :], 1.0 / MAX_SCALE, None, ALU.mult).then_inc(s_m16, 1)
                    elif kind == "M":
                        if not (isinstance(w, int) and w == 0):
                            v.wait_ge(s_mrow, (w * 2 + hd) * 16)
                        nc.vector.tensor_copy(mt[0:8, hd, :], bank[0:8, 0:P]).then_inc(s_mr, 1)
                    elif kind == "OT":
                        v.wait_ge(s_oh, u * 2 + (i + 1))
                        c_ = slice(4 * i, 4 * i + 4)
                        nc.vector.tensor_tensor(cxt_lo[:, c_, :], bank.rearrange("p (t n) -> p t n", t=4), cxt_hi[:, c_, :],
                                                ALU.subtract).then_inc(s_mr, 1)
                    else:
                        grp = (u + (off + PAIRS)) // PAIRS
                        xo = xg[:, bass.ds(grp, 1), 4 * i:4 * i + 4, :].rearrange("p b t d -> p (b t) d")
                        nc.vector.tensor_tensor(xo, xo, bank.rearrange("p (t d) -> p t d", d=D), ALU.add).then_inc(s_mr, 1)

                def low(g, s):
                    v.wait_ge(s_e32, g + 1)
                    v.wait_ge(s_e16, g + 1)
                    if not (isinstance(g, int) and g == 0):
                        v.wait_ge(s_pv, g)
                    nc.vector.tensor_tensor(p_lo[:, s % 4, 0:DC], p32[:, s % 2, 0:DC], p_hi[:, s % 4, 0:DC],
                                            ALU.subtract).then_inc(s_pd, 1)

                def prologue():
                    v.sem_inc(s_cx, 2)
                    v.sem_inc(s_pd, 1)
                    for n_ in ("Q1", "Q2", "K1", "K2"):
                        nc.vector.memset(qk[n_], 0.0).then_inc(s_qz, 1)
                    nc.vector.memset(cx, 0.0).then_inc(s_qz, 1)
                    v.wait_ge(s_qz, 5)
                    nc.vector.memset(qk["K2"][64:65], -MAX_SCALE).then_inc(s_qz, 1)
                    for n, item in enumerate(before):
                        misc(item, 0, 0, n, n % 2)
                    low(0, 0)

                def unit(u, k, left, n, par):
                    for s in range(STEPS):
                        todo = items(s, left)
                        for m, item in enumerate(todo):
                            misc(item, u, k, n, par)
                            n, par = n + 1, 1 - par
                            if m == 1 and (s + 1 < STEPS or left >= 1):
                                low(u * STEPS + (s + 1), (s + 1) % STEPS)
                        if len(todo) < 2 and (s + 1 < STEPS or left >= 1):
                            low(u * STEPS + (s + 1), (s + 1) % STEPS)
                        if s % 4 == 3:
                            hd, qh = s // 8, (s // 4) % 2
                            o = ps[:, 4 + (s // 4) % 2, 0:4 * (DH + 1)].rearrange("p (t r) -> p t r", r=DH + 1)
                            v.wait_ge(s_pv, u * STEPS + (s + 4))
                            nc.vector.reciprocal(rsum, o[:, :, DH]).then_inc(s_rs, 1)
                            v.wait_ge(s_rs, u * 4 + (s // 4 + 1))
                            nc.vector.tensor_tensor(cx[:, 4 * qh:4 * qh + 4, DH * hd:DH * hd + DH], o[:, :, 0:DH],
                                                    rsum.unsqueeze(2).broadcast_to([P, 4, DH]), ALU.mult).then_inc(s_cx, 1)
                n = run_units(v, prologue, unit)
                for m, item in enumerate(after):
                    misc(item, UNITS, 0, n + m, (n + m) % 2)

            @block.scalar
            def _(act):
                def exps(g, s):
                    act.wait_ge(s_s, g + 1)
                    if not (isinstance(g, int) and g == 0):
                        act.wait_ge(s_pd, g)
                        act.wait_ge(s_pp, g)
                    sc = ps[:, 2 * (s % 2):2 * (s % 2) + 2, :].rearrange("p b n -> p (b n)")
                    nc.scalar.activation(p32[:, s % 2, :], sc, ACT.Exp, scale=0.125).then_inc(s_e32, 1)
                    if not (isinstance(g, int) and g == 0):
                        act.wait_ge(s_pv, g)
                    nc.scalar.activation(p_hi[:, s % 4, :], sc, ACT.Exp, scale=0.125).then_inc(s_e16, 1)

                def rot_hi(w, c):
                    act.wait_ge(s_rc, w * 4 + (c + 1))
                    if not (isinstance(w, int) and w == 0):
                        act.wait_ge((s_sq, s_sk)[c // 2], w * 96)
                    nc.scalar.copy(r_hi[:, c, :], rc[:, c % 2, :]).then_inc(s_rh, 1)

                def context_hi(i, n, par):
                    act.wait_ge(s_mf, n + 1)
                    bank = ps[:, 6 + par, :].rearrange("p (t n) -> p t n", t=4)
                    nc.scalar.copy(cxt_hi[:, 4 * i:4 * i + 4, :], bank).then_inc(s_oh, 1)

                def prologue():
                    for w in range(2):
                        for c in range(4):
                            rot_hi(w, c)
                    exps(0, 0)

                def unit(u, k, left, n, par):
                    for s in range(STEPS):
                        if s + 1 < STEPS or left >= 1:
                            exps(u * STEPS + (s + 1), (s + 1) % STEPS)
                        for item in items(s, left):
                            if item[0] == "OT":
                                context_hi(item[3], n, par)
                            n, par = n + 1, 1 - par
                        if left >= 2 and s >= ROT_HI and (s - ROT_HI) % 2 == 0 and s < ROT_HI + 8:
                            rot_hi(u + 2, (s - ROT_HI) // 2)
                n = run_units(act, prologue, unit)
                for i in range(2):
                    context_hi(i, n + i, (n + i) % 2)

            @block.gpsimd
            def _(pool):
                def low(g, s):
                    pool.wait_ge(s_e32, g + 1)
                    pool.wait_ge(s_e16, g + 1)
                    if not (isinstance(g, int) and g == 0):
                        pool.wait_ge(s_pv, g)
                    nc.gpsimd.tensor_tensor(p_lo[:, s % 4, DC:], p32[:, s % 2, DC:], p_hi[:, s % 4, DC:],
                                            ALU.subtract).then_inc(s_pp, 1)

                def rot_sum(w, c, read):
                    pool.wait_ge(s_mr, read)
                    if not (isinstance(w, int) and w == 0 and c < 2):
                        pool.wait_ge(s_rl, w * 4 + (c - 1))
                    nc.gpsimd.tensor_tensor(rc[:, c % 2, :], ra[:, c % 2, :], rb[:, c % 2, :], ALU.add).then_inc(s_rc, 1)

                def rot_lo(w, c):
                    pool.wait_ge(s_rh, w * 4 + (c + 1))
                    nc.gpsimd.tensor_tensor(r_lo[:, c, :], rc[:, c % 2, :], r_hi[:, c, :], ALU.subtract).then_inc(s_rl, 1)

                def prologue():
                    pool.sem_inc(s_pp, 1)
                    for w in range(2):
                        for c in range(4):
                            rot_sum(w, c, 8 * w + 2 * c + 2)
                            rot_lo(w, c)
                    low(0, 0)

                def unit(u, k, left, n, par):
                    for s in range(STEPS):
                        if s + 1 < STEPS or left >= 1:
                            low(u * STEPS + (s + 1), (s + 1) % STEPS)
                        if left >= 2:
                            if s >= ROT_SUM and (s - ROT_SUM) % 2 == 0 and s < ROT_SUM + 8:
                                c = (s - ROT_SUM) // 2
                                rot_sum(u + 2, c, n + read_by(("R", 2, 0, 2 * c + 1), left))
                            if s >= ROT_LO and (s - ROT_LO) % 2 == 0 and s < ROT_LO + 8:
                                rot_lo(u + 2, (s - ROT_LO) // 2)
                run_units(pool, prologue, unit)

            @block.sync
            def _(sp):
                def operands(w):
                    b_, j_ = w // PAIRS, w % PAIRS
                    sp.dma_start(lat[:, 0, :], cq_t[:, bass.ds(b_ * S, S)]).then_inc(s_op, 16)
                    sp.dma_start(lat[:, 1, :], ckv_t[:, bass.ds(b_ * S, S)]).then_inc(s_op, 16)
                    sp.dma_start(wu_cur.rearrange("p w h n -> p (w h) n"),
                                 wup[:].rearrange("p w h n -> p (w h) n")[:, :, bass.ds(j_ * P, P)]).then_inc(s_op, 16)

                def latent_rows(w, slot):
                    sp.dma_start(cv_cur[:, slot].rearrange("p t r -> p (t r)"),
                                 cv_all[:].rearrange("p t r -> p (t r)")[:, bass.ds((w // PAIRS) * (TB * CV), TB * CV)]).then_inc(s_cv[slot], 16)

                def out_weights(w, slot):
                    j_ = w % PAIRS
                    sp.dma_start(wc_cur[:, slot, 0, :], wc_hi[:].rearrange("p j d -> p (j d)")[:, bass.ds(j_ * D, D)]).then_inc(s_wcc[slot], 16)
                    sp.dma_start(wc_cur[:, slot, 1, :], wc_lo[:].rearrange("p j d -> p (j d)")[:, bass.ds(j_ * D, D)]).then_inc(s_wcc[slot], 16)

                def stack(w, slot):
                    for kind, done in ((0, s_sq), (2, s_sk)):
                        for sm in (s_rh, s_rl):
                            sp.wait_ge(sm, w * 4 + (kind + 2))
                        for hd in range(2):
                            rows = slice(64 * hd, 64 * hd + 64)
                            hi, lo = (t[rows, kind:kind + 2, :].rearrange("p c n -> p (c n)") for t in (r_hi, r_lo))
                            if kind == 0:
                                moves = (("Q1", 0, hi), ("Q1", 64, lo), ("Q2", 0, hi))
                            else:
                                moves = (("K1", 0, hi), ("K1", 64, hi), ("K2", 0, lo))
                            for name_, row, src in moves:
                                sp.dma_start(qk[name_][row:row + 64, slot, hd, :], src).then_inc(done, 16)

                def max_row(slot, hd, read):
                    sp.wait_ge(s_mr, read)
                    sp.dma_start(qk["Q2"][64:65, slot, hd, :], mt[0:8, hd, :]).then_inc(s_mrow, 16)

                def prologue():
                    sp.sem_inc(s_mrow, 16)
                    operands(0)
                    latent_rows(0, 0)
                    out_weights(0, 1)
                    sp.wait_ge(s_mr, 8)
                    operands(1)
                    sp.wait_ge(s_qz, 6)
                    stack(0, 0)
                    stack(1, 1)
                    max_row(0, 0, before.index(("M", 0, 0, 0)) + 1)

                def unit(u, k, left, n, par):
                    sp.wait_ge(s_mr, n)
                    if left >= 2:
                        operands(u + 2)
                    out_weights(u, k)
                    if left >= 1:
                        sp.wait_ge(s_pv, u * STEPS + 3)
                        latent_rows(u + 1, 1 - k)
                    max_row(k, 1, n + read_by(("M", 0, 1, 0), left))
                    if left >= 1:
                        max_row(1 - k, 0, n + read_by(("M", 1, 0, 0), left))
                    if left >= 2:
                        sp.wait_ge(s_s, (u + 1) * STEPS)
                        stack(u + 2, k)
                run_units(sp, prologue, unit)
        ffn("f2")
        s_out = sem("out_written")
        with nc.Block() as block:
            @block.sync
            def _(sp):
                o_v = out.rearrange("(n p) d -> p n d", p=P)
                for c in range(4):
                    sp.dma_start(o_v[:, 8 * c:8 * c + 8, :], xs[:, 8 * c:8 * c + 8, :]).then_inc(s_out, 16)
                sp.wait_ge(s_out, 64)


_INS = ["x", "wg", "wu", "wd", "wr", "temp", "wdq", "wdkv", "wuq", "wuk", "wuv", "wo", "lns", "lnb", "rope"]


def kernel(L0_attn_x, L0_attn_w_down_q, L0_attn_w_down_kv, L0_attn_w_up_q, L0_attn_w_up_k, L0_attn_w_up_v, L0_attn_w_out,
           L0_attn_ln_scale, L0_attn_ln_bias, L0_ffn_Wg, L0_ffn_Wu, L0_ffn_Wd, L0_ffn_Wr, L0_ffn_temperature):
    import concourse.bacc as bacc
    from concourse.bass_utils import run_bass_kernel_spmd

    given = {
        "x": np.reshape(L0_attn_x, (T, D)), "wg": L0_ffn_Wg, "wu": L0_ffn_Wu, "wd": L0_ffn_Wd, "wr": L0_ffn_Wr,
        "temp": L0_ffn_temperature, "wdq": np.transpose(L0_attn_w_down_q), "wdkv": np.transpose(L0_attn_w_down_kv),
        "wuq": np.transpose(L0_attn_w_up_q), "wuk": np.transpose(L0_attn_w_up_k), "wuv": L0_attn_w_up_v,
        "wo": np.transpose(L0_attn_w_out), "lns": L0_attn_ln_scale, "lnb": L0_attn_ln_bias, "rope": rope_tables(),
    }
    nc = bacc.Bacc("TRN2", target_bir_lowering=False, num_devices=1)
    arrays, args = {}, []
    for n in _INS:
        a = np.ascontiguousarray(given[n])
        arrays["in_" + n] = a
        args.append(nc.dram_tensor("in_" + n, a.shape, mybir.dt.from_np(a.dtype), kind="ExternalInput").ap())
    args.append(nc.dram_tensor("out_x", (T, D), F32, kind="ExternalOutput").ap())
    build(nc, *args)
    r = run_bass_kernel_spmd(nc, [arrays], core_ids=[0])
    return np.reshape(r.results[0]["out_x"], (B, S, D))
```

```python
from contextlib import ExitStack

import numpy as np

import concourse.bass as bass
from concourse import mybir

F32 = mybir.dt.float32
F16 = mybir.dt.float16
ALU = mybir.AluOpType
ACT = mybir.ActivationFunctionType
AX = mybir.AxisListType

B, S, D = 4, 1024, 128
H, DH = 16, 64
E, I = 8, 128
P = 128
T = B * S
NT = T // P
NQ = T // 512
TB = S // P
PAIRS = H // 2
UNITS = B * PAIRS
EPS = 1e-5
ZONE_LOW = float(0.5 - np.log(4.0 / 3.0))
CENTER = float(1.0 / np.e)
Z_LOW = float(np.log(ZONE_LOW / (1.0 - ZONE_LOW)))
MAX_SCALE = 64.0


def rope_tables():
    inv_freq = 1.0 / 10000.0 ** (np.arange(0, DH, 2, dtype=np.float32) / DH)
    freqs = np.outer(np.arange(S, dtype=np.float32), inv_freq)
    cos = np.concatenate([np.cos(freqs), np.cos(freqs)], -1)[:, ::2]
    sin = np.concatenate([np.sin(freqs), np.sin(freqs)], -1)[:, ::2]
    sign = np.where(np.arange(DH) % 2 == 0, -1.0, 1.0)[:, None]
    c = np.repeat(cos.T, 2, axis=0)
    s = np.repeat(sin.T, 2, axis=0) * sign
    return np.stack([np.tile(c, (2, 1)), np.tile(s, (2, 1))], 1).astype(np.float32)


def build(nc, x, wg, wu, wd, wr, temp, wdq, wdkv, wuq, wuk, wuv, wo, lns, lnb, rope, out):
    with ExitStack() as ctx:
        def sb(name, shape, dt=F32):
            return ctx.enter_context(nc.sbuf_tensor(name, shape, dt))

        def sem(name):
            return ctx.enter_context(nc.semaphore(name))

        ps = ctx.enter_context(nc.psum_tensor("ps", [P, 8, 512], F32))

        xg = sb("xg", [P, B + 2, TB, D])
        xs = xg[:, 1:B + 1].rearrange("p b t d -> p (b t) d")
        ident = sb("ident", [P, P])
        ident16 = sb("ident16", [P, P], F16)
        rows_sum = sb("rows_sum", [P, E], F16)
        xt_hi = sb("xt_hi", [P, T], F16)
        xt_lo = sb("xt_lo", [P, T], F16)
        w_ffn = {n: (sb(n + "_hi", [P, E, P], F16), sb(n + "_lo", [P, E, P], F16)) for n in ("wg", "wu", "wd")}
        wr_hi, wr_lo = sb("wr_hi", [P, E], F16), sb("wr_lo", [P, E], F16)
        rtemp = sb("rtemp", [P, 1])
        rev = sb("rev", [P, E])
        GT = (B + 2) * TB
        stat6 = sb("stat6", [P, 2, TB, 6])
        mean, var, m_sum, m_dif, v_sum = (sb(n, [P, 2, TB]) for n in ("mean", "var", "mean_sum", "mean_dif", "var_sum"))
        tanh_bias = sb("tanh_bias", [P, 2])
        rs0, rs1, root_tmp, rstd, nmr, rstd2, rr, nmrr, rstd_1 = (
            sb(n, [P, GT]) for n in ("var_eps", "minus_half_var", "root_tmp", "rstd", "minus_mean_rstd", "rstd2", "rstd_both",
                                     "minus_mean_both", "rstd_plus_1"))
        cq_t, ckv_t = xt_hi, xt_lo
        CV = 2 * DH + 1
        cv_all = sb("cv_all", [P, NT, CV], F16)
        wc_hi = sb("wc_hi", [P, PAIRS, D], F16)
        wc_lo = sb("wc_lo", [P, PAIRS, D], F16)
        wup = sb("wup", [P, 4, 2, H * DH], F16)
        wd2 = sb("wd2", [P, 2, 3, P], F16)
        lnsb = sb("lnsb", [P, 2])
        cs = sb("cs", [P, 2, S])

        big = 26 * 1024
        area = sb("area", [P, big])
        area_at = [0]

        def carve(n, dt=F32):
            words = n if dt is F32 else n // 2
            a = area[:, area_at[0]:area_at[0] + words]
            area_at[0] += words
            assert area_at[0] <= big, area_at
            return a if dt is F32 else a.bitcast(dt)

        area_at[0] = 0
        st = {n: carve(E * P) for n in ("wg", "wu", "wd")}
        st_up = {n: carve(H * DH) for n in ("q", "k")}
        st_v = carve(PAIRS * DH)
        st_o = carve(PAIRS * D)
        st_dn = carve(2 * P)
        st_r = carve(E)
        s_x, s_w, s_up, s_small, s_rope = sem("x_loaded"), sem("ffn_w_loaded"), sem("up_w_loaded"), sem("small_loaded"), sem("rope_loaded")
        s_id, s_idz, s_c0 = sem("ident_ready"), sem("ident_zeroed"), sem("consts_ready")
        s_hi, s_lo, s_wc, s_sw = sem("w_hi_done"), sem("w_lo_done"), sem("wc_product"), sem("swap_done")
        s_wcr = sem("wc_read")
        s_rt = sem("rtemp_done")
        x_v = x.rearrange("(n p) d -> p n d", p=P)

        with nc.Block() as block:
            @block.sync
            def _(sp):
                for c in range(4):
                    sp.dma_start(xs[:, 8 * c:8 * c + 8, :], x_v[:, 8 * c:8 * c + 8, :]).then_inc(s_x, 16)
                sp.dma_start(st["wg"].rearrange("p (e i) -> p e i", e=E), wg.rearrange("e d i -> d e i")).then_inc(s_w, 16)
                sp.dma_start(st["wu"].rearrange("p (e i) -> p e i", e=E), wu.rearrange("e d i -> d e i")).then_inc(s_w, 16)
                sp.dma_start(st["wd"].rearrange("p (e i) -> p e i", e=E), wd.rearrange("e i d -> i e d")).then_inc(s_w, 16)
                sp.dma_start(st_r, wr).then_inc(s_w, 16)

            @block.scalar
            def _(act):
                for n, w in (("q", wuq), ("k", wuk)):
                    for r in range(2):
                        act.dma_start(st_up[n][64 * r:64 * r + 64, :], w).then_inc(s_up, 16)
                act.dma_start(st_v.rearrange("p (j r) -> p j r", j=PAIRS), wuv.rearrange("(j p) r -> p j r", p=P)).then_inc(s_small, 16)
                act.dma_start(st_o.rearrange("p (j d) -> p j d", j=PAIRS), wo.rearrange("(j p) d -> p j d", p=P)).then_inc(s_small, 16)
                act.dma_start(st_dn[:, 0:64], wdq).then_inc(s_small, 16)
                act.dma_start(st_dn[:, 64:128], wdkv).then_inc(s_small, 16)
                act.dma_start(lnsb[:, 0:1], lns.rearrange("(p a) -> p a", a=1)).then_inc(s_small, 16)
                act.dma_start(lnsb[:, 1:2], lnb.rearrange("(p a) -> p a", a=1)).then_inc(s_small, 16)
                act.dma_start(rtemp[:, 0:1], temp.rearrange("(p a) -> p a", a=1).broadcast_to([P, 1])).then_inc(s_small, 16)
                act.dma_start(cs[:], rope).then_inc(s_rope, 16)
                act.wait_ge(s_w, 64)
                for n in ("wg", "wu", "wd"):
                    nc.scalar.copy(w_ffn[n][0][:].rearrange("p e i -> p (e i)"), st[n]).then_inc(s_hi, 1)
                nc.scalar.copy(wr_hi[:], st_r).then_inc(s_hi, 1)
                act.wait_ge(s_up, 64)
                for k, n in ((0, "q"), (2, "k")):
                    nc.scalar.copy(wup[:, k, 0, :], st_up[n]).then_inc(s_hi, 1)
                act.wait_ge(s_rope, 16)
                act.wait_ge(s_small, 112)
                for k in range(2):
                    src = st_dn[:, 64 * k:64 * k + 64]
                    for r in range(2):
                        nc.scalar.copy(wd2[:, k, 0, 64 * r:64 * r + 64], src).then_inc(s_hi, 1)

            @block.vector
            def _(v):
                nc.vector.memset(tanh_bias[:, 0:1], (0.5 - CENTER) * 0.5 / 0.1).then_inc(s_c0, 1)
                nc.vector.memset(tanh_bias[:, 1:2], (0.5 - CENTER) * 0.5 / 0.3).then_inc(s_c0, 1)
                nc.vector.memset(xg[:, 0], 0.0).then_inc(s_c0, 1)
                nc.vector.memset(xg[:, B + 1], 0.0).then_inc(s_c0, 1)
                for e in range(E):
                    nc.vector.memset(rev[:, e:e + 1], float(E - e)).then_inc(s_c0, 1)
                v.wait_ge(s_w, 64)
                for k, n in enumerate(("wg", "wu", "wd")):
                    v.wait_ge(s_hi, k + 1)
                    nc.vector.tensor_tensor(w_ffn[n][1][:].rearrange("p e i -> p (e i)"), st[n],
                                            w_ffn[n][0][:].rearrange("p e i -> p (e i)"), ALU.subtract).then_inc(s_lo, 1)
                v.wait_ge(s_hi, 4)
                nc.vector.tensor_tensor(wr_lo[:], st_r, wr_hi[:], ALU.subtract).then_inc(s_lo, 1)
                v.wait_ge(s_up, 64)
                for j, (k, n) in enumerate(((0, "q"), (2, "k"))):
                    v.wait_ge(s_hi, 5 + j)
                    nc.vector.tensor_tensor(wup[:, k, 1, :], st_up[n], wup[:, k, 0, :], ALU.subtract).then_inc(s_lo, 1)
                v.wait_ge(s_small, 112)
                nc.vector.reciprocal(rtemp[:], rtemp[:]).then_inc(s_rt, 1)
                for k in range(2):
                    for r in range(2):
                        v.wait_ge(s_hi, 7 + 2 * k + r)
                        nc.vector.tensor_tensor(wd2[:, k, 1, 64 * r:64 * r + 64], st_dn[:, 64 * k:64 * k + 64],
                                                wd2[:, k, 0, 64 * r:64 * r + 64], ALU.subtract).then_inc(s_lo, 1)
                v.wait_ge(s_wc, 2 * PAIRS)
                for hh in range(2):
                    rows = slice(64 * hh, 64 * hh + 64)
                    for g in range(2):
                        bank = ps[rows, 2 * hh + g, :].rearrange("p (j d) -> p j d", d=D)
                        nc.vector.tensor_copy(wc_hi[rows, 4 * g:4 * g + 4, :], bank).then_inc(s_wcr, 1)
                        v.wait_ge(s_wcr, 2 * hh + g + 1)
                        nc.vector.tensor_tensor(wc_lo[rows, 4 * g:4 * g + 4, :], bank,
                                                wc_hi[rows, 4 * g:4 * g + 4, :], ALU.subtract).then_inc(s_lo, 1)

            @block.tensor
            def _(pe):
                pe.wait_ge(s_small, 112)
                for hh in range(2):
                    rows = slice(64 * hh, 64 * hh + 64)
                    for j in range(PAIRS):
                        nc.tensor.matmul(ps[rows, 2 * hh + j // 4, D * (j % 4):D * (j % 4) + D],
                                         st_v[rows, DH * j:DH * j + DH], st_o[rows, D * j:D * j + D],
                                         start=True, stop=True).then_inc(s_wc, 1)

            @block.gpsimd
            def _(pool):
                nc.gpsimd.memset(ident[:], 0.0).then_inc(s_idz, 1)
                nc.gpsimd.memset(ident16[:], 0.0).then_inc(s_idz, 1)
                pool.wait_ge(s_idz, 2)
                for m in (ident, ident16):
                    nc.gpsimd.affine_select(out=m[:], in_=m[:], compare_op=ALU.not_equal, fill=1.0, base=0,
                                            pattern=[[-1, P]], channel_multiplier=1).then_inc(s_id, 1)
                pool.wait_ge(s_id, 2)
                nc.gpsimd.tensor_tensor(rows_sum[:], ident16[:, 0:E], ident16[:, E:2 * E], ALU.add).then_inc(s_id, 1)
                pool.wait_ge(s_lo, 6)
                for k in (0, 2):
                    for hl in range(2):
                        src = wup[:, k, hl, :].rearrange("p (n two) -> p n two", two=2)
                        dst = wup[:, k + 1, hl, :].rearrange("p (n two) -> p n two", two=2)
                        for a in range(2):
                            nc.gpsimd.tensor_copy(dst[:, :, a], src[:, :, 1 - a]).then_inc(s_sw, 1)

        def inverse_root(link, v_eps, minus_half, root, tmp):
            i32 = mybir.dt.int32
            link(lambda: nc.vector.tensor_scalar(root.bitcast(i32), v_eps.bitcast(i32), -0.5, float(0x5F3759DF), ALU.mult, ALU.add))
            link(lambda: nc.vector.tensor_scalar(minus_half, v_eps, -0.5, None, ALU.mult))
            for _ in range(3):
                link(lambda: nc.vector.tensor_tensor(tmp, root, root, ALU.mult))
                link(lambda: nc.vector.tensor_tensor(tmp, tmp, minus_half, ALU.mult))
                link(lambda: nc.vector.scalar_tensor_tensor(root, tmp, 1.5, root, ALU.add, ALU.mult))

        NORM_LINKS, NORM2_LINKS = 26, 42

        def chain(v, s, p, count):
            at = [0]

            def link(make, back=1):
                done = p * count + (at[0] + 1 - back)
                if not isinstance(done, int) or done > 0:
                    v.wait_ge(s, done)
                make().then_inc(s, 1)
                at[0] += 1
            return link, at

        def norm(v, g, s_chain, s_done, twice=False):
            count = NORM2_LINKS if twice else NORM_LINKS
            link, at = chain(v, s_chain, g, count)
            at_g = bass.ds(g * TB, TB)
            v_e, m_h, rt, tm, nm, rt2, both, nmb, plus1 = (
                t[:, at_g] for t in (rs0, rs1, rstd, root_tmp, nmr, rstd2, rr, nmrr, rstd_1))
            kind = 1 if twice else 0
            m_, var_, ms, md, vs = (t[:, kind, :] for t in (mean, var, m_sum, m_dif, v_sum))
            m_e, v_e_, m_o, v_o_ = (stat6[:, kind, :, c] for c in (1, 2, 4, 5))

            def stats(n):
                xj = xg[:, bass.ds(g, 1), n, :].rearrange("p b d -> p (b d)")
                at[0] += 1
                nc.vector.bn_stats(stat6[:, kind, n, :], xj).then_inc(s_chain, 1)

            made = [lambda: nc.vector.tensor_tensor(ms, m_e, m_o, ALU.add),
                    lambda: nc.vector.tensor_tensor(md, m_e, m_o, ALU.subtract),
                    lambda: nc.vector.tensor_tensor(vs, v_e_, v_o_, ALU.add),
                    lambda: nc.vector.scalar_tensor_tensor(md, md, 0.25, md, ALU.mult, ALU.mult),
                    lambda: nc.vector.tensor_scalar(m_, ms, 0.5, None, ALU.mult),
                    lambda: nc.vector.scalar_tensor_tensor(var_, vs, 1.0 / D, md, ALU.mult, ALU.add)]
            backs = [1, 2, 3, 2, 2, 2]
            made.append(lambda: nc.vector.tensor_scalar(v_e, var_, EPS, None, ALU.add))
            inverse_root(made.append, v_e, m_h, rt, tm)
            if twice:
                made += [lambda: nc.vector.tensor_tensor(v_e, var_, rt, ALU.mult),
                         lambda: nc.vector.tensor_tensor(v_e, v_e, rt, ALU.mult),
                         lambda: nc.vector.tensor_scalar(v_e, v_e, EPS, None, ALU.add)]
                inverse_root(made.append, v_e, m_h, rt2, tm)
                made += [lambda: nc.vector.tensor_tensor(both, rt, rt2, ALU.mult),
                         lambda: nc.vector.scalar_tensor_tensor(nmb, m_, -1.0, both, ALU.mult, ALU.mult)]

            def last():
                assert at[0] == count, at
                v.wait_ge(s_chain, g * count + count)
                if twice:
                    nc.vector.tensor_scalar(plus1, rt, 1.0, None, ALU.add)
                nc.vector.scalar_tensor_tensor(nm, m_, -1.0, rt, ALU.mult, ALU.mult).then_inc(s_done, 1)
            backs += [1] * (len(made) - len(backs))
            return ([lambda n=n: stats(n) for n in range(TB)]
                    + [lambda make=make, back=back: link(make, back) for make, back in zip(made, backs)] + [last])

        def ffn(name):
            area_at[0] = 0
            xn = carve(2 * 512).rearrange("p (s j d) -> p s j d", s=2, j=4)
            gate = carve(2 * 512).rearrange("p (s n) -> p s n", s=2)
            gu = carve(2 * 512).rearrange("p (s n) -> p s n", s=2)
            hw = carve(2 * 512).rearrange("p (s n) -> p s n", s=2)
            h_hi = carve(2 * 512, F16).rearrange("p (s n) -> p s n", s=2)
            h_lo = carve(2 * 512, F16).rearrange("p (s n) -> p s n", s=2)
            wt = carve(2 * 512, F16).rearrange("p (s n) -> p s n", s=2)
            z, th, w, fb, t0, t1, oh, fbm = (
                carve(TB * E).rearrange("p (t e) -> p t e", e=E) for _ in range(8))
            t01 = carve(2 * TB * E).rearrange("p (a n) -> p a n", a=2)
            ex = carve(2 * TB * E).rearrange("p (a n) -> p a n", a=2)
            abs01 = carve(2 * TB * E).rearrange("p (a n) -> p a n", a=2)
            r0, r1, r2, r3, r4, r5, r6, r7 = (carve(TB) for _ in range(8))
            whl = carve(TB * 2 * E, F16).rearrange("p (t h e) -> p t h e", h=2, e=E)
            s_ch, s_rstd = sem(name + "_norm_chain"), sem(name + "_rstd")
            s_xn, s_xT, s_xhi, s_xlo = (sem(name + n) for n in ("_xn", "_xT", "_xT_hi", "_xT_lo"))
            s_z, s_zr, s_th, s_tt, s_ex = (sem(name + n) for n in ("_logits", "_logits_read", "_tanh", "_tanh_dist", "_abs_tanh"))
            s_rc, s_routed = sem(name + "_route_chain"), sem(name + "_route_done")
            s_wr, s_wt, s_wz = sem(name + "_w_rows"), sem(name + "_w_rows_stored"), sem(name + "_w_rows_zeroed")
            s_g, s_u, s_wb = (sem(name + n) for n in ("_gate", "_up", "_wbcast"))
            s_si, s_gu, s_hw = sem(name + "_silu"), sem(name + "_gate_up"), sem(name + "_h")
            s_hh, s_hl, s_dn = sem(name + "_h_hi"), sem(name + "_h_lo"), sem(name + "_down")
            s_y0, s_y = sem(name + "_y_zeroed"), sem(name + "_y_added")
            s_out_ = sem(name + "_written")
            (g_hi, g_lo), (u_hi, u_lo), (d_hi, d_lo) = (w_ffn[n] for n in ("wg", "wu", "wd"))
            ROUTE_LINKS = 27

            def turns(eng, body):
                with eng.Fori(0, B - 1) as it:
                    body(it, False)
                body(B - 1, True)

            with nc.Block() as block:
                @block.tensor
                def _(pe):
                    def transpose(p, a):
                        pe.wait_ge(s_xn, 2 * p + (a + 1))
                        if a == 1:
                            pe.wait_ge(s_xlo, 2 * p + 1)
                        elif not isinstance(p, int):
                            pe.wait_ge(s_y, 2 * p - 1)
                        for j in range(4):
                            last = nc.tensor.transpose(ps[:, 7, P * j:P * j + P], xn[:, a, j, :], ident[:])
                        last.then_inc(s_xT, 1)

                    def router(p):
                        pe.wait_ge(s_xlo, 2 * p + 2)
                        for j in range(TB):
                            cols = bass.ds(p * S + P * j, P)
                            for k, (a, b) in enumerate(((xt_hi, wr_hi), (xt_hi, wr_lo), (xt_lo, wr_hi))):
                                last = nc.tensor.matmul(ps[:, 7, E * j:E * j + E], a[:, cols], b[:],
                                                        start=(j == 0 and k == 0), stop=(k == 2), skip_group_check=True)
                        last.then_inc(s_z, 1)

                    def weight_rows(p, a):
                        if a == 0:
                            pe.wait_ge(s_routed, p + 1)
                            if not isinstance(p, int):
                                pe.wait_ge(s_y, 2 * p)
                        else:
                            pe.wait_ge(s_wt, 2 * p + 1)
                        for j in range(4):
                            last = nc.tensor.matmul(ps[0:2 * E, 6, P * j:P * j + P],
                                                    whl[:, 4 * a + j].rearrange("p h e -> p (h e)"), ident16[:],
                                                    start=(j == 0), stop=True, skip_group_check=True)
                        last.then_inc(s_wr, 1)

                    def gate_up(i, t, k):
                        e, b = k % E, k % 2
                        cols = bass.ds(t * S + 512 * (k // E), 512)
                        for w_h, w_l, bank, read, done in ((g_hi, g_lo, 0, s_si, s_g), (u_hi, u_lo, 2, s_gu, s_u)):
                            if not (isinstance(t, int) and t == 0 and k < 2):
                                pe.wait_ge(read, i - 1 if read is s_si else i)
                            o = ps[:, bank + b, :]
                            nc.tensor.matmul(o, w_h[:, e, :], xt_hi[:, cols], start=True, stop=False)
                            nc.tensor.matmul(o, w_h[:, e, :], xt_lo[:, cols], start=False, stop=False)
                            nc.tensor.matmul(o, w_l[:, e, :], xt_hi[:, cols], start=False, stop=True).then_inc(done, 1)

                    def weight(i, t, k):
                        if not (isinstance(t, int) and t == 0 and k < 2):
                            pe.wait_ge(s_hw, i - 1)
                        if k % E == 0:
                            pe.wait_ge(s_wt, 2 * t + (k // E + 1))
                        nc.tensor.matmul(ps[:, 4 + k % 2, :], rows_sum[:, k % E:k % E + 1].broadcast_to([P, P]),
                                         wt[:, k // E, :], start=True, stop=True).then_inc(s_wb, 1)

                    def down(i, t, k, last_turn):
                        e, b = k % E, k % 2
                        if k == 0:
                            pe.wait_ge(s_wt, 2 * t + 2)
                        if k == E:
                            if last_turn:
                                pe.wait_ge(s_y, 2 * t + 1)
                            else:
                                pe.wait_ge(s_zr, t + 2)
                        pe.wait_ge(s_hh, i + 1)
                        pe.wait_ge(s_hl, i + 3)
                        for j in range(4):
                            o = ps[:, 6 + k // E, P * j:P * j + P]
                            cols = slice(P * j, P * j + P)
                            nc.tensor.matmul(o, h_hi[:, b, cols], d_hi[:, e, :], start=(e == 0 and j == 0), stop=False,
                                             skip_group_check=True)
                            nc.tensor.matmul(o, h_hi[:, b, cols], d_lo[:, e, :], start=False, stop=False, skip_group_check=True)
                            last = nc.tensor.matmul(o, h_lo[:, b, cols], d_hi[:, e, :], start=False, stop=(e == E - 1),
                                                    skip_group_check=True)
                        last.then_inc(s_dn, 1)

                    def turn(t, last):
                        for k in range(16):
                            i = t * 16 + k
                            t2, k2 = (t, k + 2) if k < 14 else (t + 1, k - 14)
                            ahead = k < 14 or not last
                            if ahead:
                                gate_up(i + 2, t2, k2)
                            if not last and k == 5:
                                router(t + 1)
                            down(i, t, k, last)
                            if not last and k in (1, 3):
                                transpose(t + 1, (k - 1) // 2)
                            if not last and k in (13, 14):
                                weight_rows(t + 1, k - 13)
                            if ahead:
                                weight(i + 2, t2, k2)
                    pe.sem_inc(s_dn, 2)
                    if name == "f1":
                        pe.wait_ge(s_id, 3)
                    transpose(0, 0)
                    transpose(0, 1)
                    router(0)
                    gate_up(0, 0, 0)
                    gate_up(1, 0, 1)
                    weight_rows(0, 0)
                    weight_rows(0, 1)
                    pe.wait_ge(s_wz, 1)
                    weight(0, 0, 0)
                    weight(1, 0, 1)
                    turns(pe, turn)

                @block.scalar
                def _(act):
                    def normed(p, a):
                        act.wait_ge(s_rstd, p + 1)
                        if not isinstance(p, int):
                            act.wait_ge(s_xT, 2 * p + (a - 1))
                        for j in range(4):
                            n = 4 * a + j
                            xj = xg[:, bass.ds(p + 1, 1), n, :].rearrange("p b d -> p (b d)")
                            at_n = bass.ds((p + 1) * TB + n, 1)
                            last = nc.scalar.activation(xn[:, a, j, :], xj, ACT.Identity, scale=rstd[:, at_n], bias=nmr[:, at_n])
                        last.then_inc(s_xn, 1)

                    def hi(p, a):
                        act.wait_ge(s_xT, 2 * p + (a + 1))
                        nc.scalar.copy(xt_hi[:, bass.ds(p * S + 512 * a, 512)], ps[:, 7, :]).then_inc(s_xhi, 1)

                    def tanh_z(p):
                        act.wait_ge(s_zr, p + 1)
                        nc.scalar.activation(th, z, ACT.Tanh, scale=0.5).then_inc(s_th, 1)

                    def tanh_dist(p):
                        act.wait_ge(s_th, p + 1)
                        th_ = th.rearrange("p t e -> p (t e)")
                        for m, width in enumerate((0.1, 0.3)):
                            nc.scalar.activation(t01[:, m], th_, ACT.Tanh, scale=0.5 * 0.5 / width,
                                                 bias=tanh_bias[:, m:m + 1]).then_inc(s_tt, 1)
                        act.wait_ge(s_tt, 2 * p + 2)
                        nc.scalar.activation(abs01, t01, ACT.Abs, scale=0.5).then_inc(s_ex, 1)

                    def rows(p, a):
                        act.wait_ge(s_wr, 2 * p + (a + 1))
                        nc.scalar.copy(wt[0:2 * E, a, :], ps[0:2 * E, 6, :]).then_inc(s_wt, 1)

                    def silu(i, t, k):
                        act.wait_ge(s_g, i + 1)
                        if not (isinstance(t, int) and t == 0 and k == 0):
                            act.wait_ge(s_gu, i)
                        nc.scalar.activation(gate[:, k % 2, :], ps[:, k % 2, :], ACT.Silu).then_inc(s_si, 1)

                    def turn(t, last):
                        for k in range(16):
                            i = t * 16 + k
                            if not (last and k == 15):
                                silu(i + 1, *((t, k + 1) if k < 15 else (t + 1, 0)))
                            act.wait_ge(s_hw, i + 1)
                            act.wait_ge(s_dn, i + 1)
                            nc.scalar.copy(h_hi[:, k % 2, :], hw[:, k % 2, :]).then_inc(s_hh, 1)
                            if not last:
                                if k in (0, 1):
                                    normed(t + 1, k)
                                if k in (2, 4):
                                    hi(t + 1, (k - 2) // 2)
                                if k == 6:
                                    tanh_z(t + 1)
                                    tanh_dist(t + 1)
                                if k in (14, 15):
                                    rows(t + 1, k - 14)
                    act.wait_ge(s_wz, 1)
                    normed(0, 0)
                    normed(0, 1)
                    hi(0, 0)
                    hi(0, 1)
                    tanh_z(0)
                    tanh_dist(0)
                    silu(0, 0, 0)
                    rows(0, 0)
                    rows(0, 1)
                    turns(act, turn)

                @block.gpsimd
                def _(pool):
                    def turn(t, last):
                        for k in range(16):
                            i = t * 16 + k
                            pool.wait_ge(s_hh, i + 1)
                            pool.wait_ge(s_dn, i + 1)
                            nc.gpsimd.tensor_tensor(h_lo[:, k % 2, :], hw[:, k % 2, :], h_hi[:, k % 2, :],
                                                    ALU.subtract).then_inc(s_hl, 1)
                    nc.gpsimd.memset(wt, 0.0).then_inc(s_wz, 1)
                    pool.sem_inc(s_hl, 2)
                    turns(pool, turn)

                @block.vector
                def _(v):
                    def lo(p, a):
                        v.wait_ge(s_xhi, 2 * p + (a + 1))
                        cols = bass.ds(p * S + 512 * a, 512)
                        nc.vector.tensor_tensor(xt_lo[:, cols], ps[:, 7, :], xt_hi[:, cols], ALU.subtract).then_inc(s_xlo, 1)

                    def logits(p):
                        v.wait_ge(s_z, p + 1)
                        nc.vector.tensor_scalar(z, ps[:, 7, 0:TB * E].rearrange("p (t e) -> p t e", e=E), rtemp[:, 0:1],
                                                None, ALU.mult).then_inc(s_zr, 1)

                    def wide(t):
                        return t.unsqueeze(2).broadcast_to([P, TB, E])

                    def flat(t):
                        return t.rearrange("p t e -> p (t e)")

                    def route(p):
                        link, at = chain(v, s_rc, p, ROUTE_LINKS)
                        tt, stt, ts, tr = (nc.vector.tensor_tensor, nc.vector.scalar_tensor_tensor,
                                           nc.vector.tensor_scalar, nc.vector.tensor_reduce)
                        w_all, fb_all = (ex[:, m].rearrange("p (t e) -> p t e", e=E) for m in range(2))
                        idx = rev[:].unsqueeze(1).broadcast_to([P, TB, E])
                        parts = []

                        def do(make, back=1):
                            parts.append(lambda: link(make, back))
                        parts.append(lambda: v.wait_ge(s_ex, p + 1))
                        do(lambda: ts(abs01, abs01, 0.5, None, ALU.add))
                        do(lambda: nc.vector.reciprocal(ex, abs01))
                        do(lambda: ts(ex, ex, -1.0, None, ALU.add))
                        parts.append(lambda: v.wait_ge(s_zr, p + 1))
                        do(lambda: tr(r2, fb_all, AX.X, ALU.max))
                        do(lambda: stt(w, z, Z_LOW, w_all, ALU.is_ge, ALU.mult), 2)
                        do(lambda: tt(t0, fb_all, wide(r2), ALU.is_equal), 2)
                        do(lambda: stt(w, z, 0.0, w, ALU.is_le, ALU.mult), 2)
                        do(lambda: tt(t0, t0, idx, ALU.mult), 2)
                        do(lambda: tr(r0, w, AX.X, ALU.add), 2)
                        do(lambda: tr(r3, t0, AX.X, ALU.max), 2)
                        do(lambda: ts(r1, r0, 1e-8, None, ALU.is_lt), 2)
                        do(lambda: tt(oh, t0, wide(r3), ALU.is_equal), 2)
                        do(lambda: stt(fbm, oh, -4.0, fb_all, ALU.mult, ALU.add))
                        do(lambda: tr(r4, fbm, AX.X, ALU.max))
                        do(lambda: tt(fb, fb_all, wide(r1), ALU.mult), 2)
                        do(lambda: tt(t1, fbm, wide(r4), ALU.is_equal), 2)
                        do(lambda: tt(t1, t1, idx, ALU.mult))
                        do(lambda: tr(r5, t1, AX.X, ALU.max))
                        do(lambda: tt(t1, t1, wide(r5), ALU.is_equal))
                        do(lambda: tt(oh, oh, t1, ALU.add))
                        do(lambda: tt(fb, fb, oh, ALU.mult))
                        do(lambda: tt(w, w, fb, ALU.add))
                        do(lambda: tr(r6, w, AX.X, ALU.add))
                        do(lambda: ts(r6, r6, 1e-8, None, ALU.max))
                        do(lambda: nc.vector.reciprocal(r7, r6))
                        do(lambda: tt(w, w, wide(r7), ALU.mult))
                        do(lambda: nc.vector.tensor_copy(whl[:, :, 0, :], w))

                        def low_half():
                            assert at[0] == ROUTE_LINKS, at
                            v.wait_ge(s_rc, p * ROUTE_LINKS + ROUTE_LINKS)
                            tt(whl[:, :, 1, :], w, whl[:, :, 0, :], ALU.subtract).then_inc(s_routed, 1)
                        return parts + [low_half]

                    def add_y(t, a):
                        v.wait_ge(s_dn, t * 16 + (10 if a == 0 else 2))
                        xq = xg[:, bass.ds(t + (1 - a), 1), 4 * a:4 * a + 4, :].rearrange("p b t d -> p (b t) d")
                        y_ = ps[:, 6 + a, :].rearrange("p (t d) -> p t d", d=D)
                        nc.vector.scalar_tensor_tensor(xq, y_, 0.5, xq, ALU.mult, ALU.add).then_inc(s_y, 1)

                    def turn(t, last):
                        spread = [0] * 16
                        between, after_ = ({k: [] for k in range(16)} for _ in range(2))
                        after_[1].append(lambda: add_y(t, 1))
                        after_[9].append(lambda: add_y(t, 0))
                        if not last:
                            between[3].append(lambda: lo(t + 1, 0))
                            between[5].append(lambda: lo(t + 1, 1))
                            after_[6].append(lambda: logits(t + 1))
                            for parts, n_between, n_after in (
                                    (norm(v, t + 3, s_ch, s_rstd), {k: 1 for k in (2, 3, 4, 5, 6, 7, 14, 15)}, {k: 4 for k in range(2, 8)}),
                                    (route(t + 1), {k: 1 for k in range(8, 13)}, {k: 5 for k in range(8, 13)})):
                                for k in range(16):
                                    for part_list, count in ((between, n_between), (after_, n_after)):
                                        for _ in range(count.get(k, 0)):
                                            if parts:
                                                part_list[k].append(parts.pop(0))
                                assert not parts, len(parts)
                        if name == "f1":
                            parts = norm(v, t + 0, s_an, s_ann, True)
                            for k in [2, 3, 4, 5, 6, 7] * 4 + [13, 14, 15] * 7:
                                spread[k] += 1
                            for k in range(16):
                                for _ in range(min(spread[k], len(parts))):
                                    after_[k].append(parts.pop(0))
                        for k in range(16):
                            i, b = t * 16 + k, k % 2
                            v.wait_ge(s_si, i + 1)
                            v.wait_ge(s_u, i + 1)
                            nc.vector.tensor_tensor(gu[:, b, :], gate[:, b, :], ps[:, 2 + b, :], ALU.mult).then_inc(s_gu, 1)
                            for f in between[k]:
                                f()
                            v.wait_ge(s_gu, i + 2)
                            v.wait_ge(s_wb, i + 1)
                            v.wait_ge(s_hl, i + 1)
                            nc.vector.tensor_tensor(hw[:, b, :], gu[:, b, :], ps[:, 4 + b, :], ALU.mult).then_inc(s_hw, 1)
                            for f in after_[k]:
                                f()
                    v.sem_inc(s_gu, 1)
                    if name == "f1":
                        v.wait_ge(s_x, 64)
                        v.wait_ge(s_rt, 1)
                    v.sem_inc(s_ch, NORM_LINKS)
                    for g in (1, 2):
                        for f in norm(v, g, s_ch, s_rstd):
                            f()
                    lo(0, 0)
                    lo(0, 1)
                    logits(0)
                    v.wait_ge(s_zr, 1)
                    nc.vector.memset(ps[:, 7, :], 0.0).then_inc(s_y0, 1)
                    v.wait_ge(s_y0, 1)
                    for f in route(0):
                        f()
                    turns(v, turn)
                    add_y(B, 1)

        s_an, s_ann = sem("attention_norm_chain"), sem("attention_norms")
        ffn("f1")
        area_at[0] = 0
        yn = carve(2 * 512).rearrange("p (s j d) -> p s j d", s=2, j=4)
        h32 = carve(2 * 512).rearrange("p (s n) -> p s n", s=2)
        hh_hi = carve(2 * 512, F16).rearrange("p (s n) -> p s n", s=2)
        hh_lo = carve(2 * 512, F16).rearrange("p (s n) -> p s n", s=2)
        s_yr, s_yn, s_yT = sem("y_residual"), sem("yn_done"), sem("yT_done")
        s_h32, s_hhi, s_hlo = sem("h32_done"), sem("hT_hi"), sem("hT_lo")
        s_lat, s_lhi, s_llo, s_one = sem("latents_product"), sem("latents_hi"), sem("latents_lo"), sem("cv_ones")
        with nc.Block() as block:
            @block.vector
            def _(v):
                for f in norm(v, B, s_an, s_ann, True):
                    f()
                for q in range(NQ + 1):
                    if q < NQ:
                        v.wait_ge(s_yT, q + 1)
                        if q >= 2:
                            v.wait_ge(s_hlo, q - 1)
                        nc.vector.tensor_scalar(h32[:, q % 2, :], ps[:, q % 2, :], lnsb[:, 0:1], lnsb[:, 1:2],
                                                ALU.mult, ALU.add).then_inc(s_h32, 1)
                        v.wait_ge(s_yn, q + 1)
                        for n in range(4 * q, 4 * q + 4):
                            nc.vector.tensor_scalar(xs[:, n, :], xs[:, n, :], rstd_1[:, TB + n:TB + n + 1], nmr[:, TB + n:TB + n + 1],
                                                    ALU.mult, ALU.add).then_inc(s_yr, 1)
                    if q >= 1:
                        p, cols, bank = q - 1, slice(512 * q - 512, 512 * q), 2 + 3 * ((q - 1) % 2)
                        for k, dst in enumerate((cq_t, ckv_t)):
                            v.wait_ge(s_lhi, 3 * p + k + 1)
                            nc.vector.tensor_tensor(dst[64:128, cols], ps[64:128, bank + k, :], dst[64:128, cols],
                                                    ALU.subtract).then_inc(s_llo, 1)
                        v.wait_ge(s_lhi, 3 * p + 3)
                        cvt = cv_all[:, 4 * p:4 * p + 4, :]
                        nc.vector.tensor_tensor(cvt[:, :, DH + 1:CV], ps[:, bank + 2, 0:256].rearrange("p (t r) -> p t r", r=DH),
                                                cvt[:, :, 0:DH], ALU.subtract).then_inc(s_llo, 1)

            @block.gpsimd
            def _(pool):
                nc.gpsimd.memset(cv_all[:, :, DH:DH + 1], 1.0).then_inc(s_one, 1)
                for q in range(NQ):
                    pool.wait_ge(s_h32, q + 1)
                    pool.wait_ge(s_hhi, q + 1)
                    if q >= 2:
                        pool.wait_ge(s_lat, 3 * (q - 1))
                    nc.gpsimd.tensor_tensor(hh_lo[:, q % 2, :], h32[:, q % 2, :], hh_hi[:, q % 2, :],
                                            ALU.subtract).then_inc(s_hlo, 1)

            @block.scalar
            def _(act):
                def normed(q):
                    if q >= 2:
                        act.wait_ge(s_yT, q - 1)
                    if q == NQ - 2:
                        act.wait_ge(s_ann, B + 1)
                    for j in range(4):
                        n = 4 * q + j
                        last = nc.scalar.activation(yn[:, q % 2, j, :], xs[:, n, :], ACT.Identity,
                                                    scale=rr[:, TB + n:TB + n + 1], bias=nmrr[:, TB + n:TB + n + 1])
                    last.then_inc(s_yn, 1)

                def latents(q):
                    cols, bank = slice(512 * q, 512 * q + 512), 2 + 3 * (q % 2)
                    for k, dst in enumerate((cq_t, ckv_t)):
                        act.wait_ge(s_lat, 3 * q + k + 1)
                        nc.scalar.copy(dst[:, cols], ps[:, bank + k, :]).then_inc(s_lhi, 1)
                    act.wait_ge(s_lat, 3 * q + 3)
                    nc.scalar.copy(cv_all[:, 4 * q:4 * q + 4, 0:DH],
                                   ps[:, bank + 2, 0:256].rearrange("p (t r) -> p t r", r=DH)).then_inc(s_lhi, 1)
                normed(0)
                for q in range(NQ):
                    if q + 1 < NQ:
                        normed(q + 1)
                    act.wait_ge(s_h32, q + 1)
                    if q >= 2:
                        act.wait_ge(s_lat, 3 * (q - 1))
                    nc.scalar.copy(hh_hi[:, q % 2, :], h32[:, q % 2, :]).then_inc(s_hhi, 1)
                    if q >= 1:
                        latents(q - 1)
                latents(NQ - 1)

            @block.tensor
            def _(pe):
                def transposes(q):
                    pe.wait_ge(s_yn, q + 1)
                    if q >= 2:
                        pe.wait_ge(s_h32, q - 1)
                    for j in range(4):
                        last = nc.tensor.transpose(ps[:, q % 2, P * j:P * j + P], yn[:, q % 2, j, :], ident[:])
                    last.then_inc(s_yT, 1)
                transposes(0)
                for q in range(NQ):
                    if q + 1 < NQ:
                        transposes(q + 1)
                    bank = 2 + 3 * (q % 2)
                    pe.wait_ge(s_hlo, q + 1)
                    if q >= 2:
                        pe.wait_ge(s_llo, 3 * (q - 1))
                    a_hi, a_lo = hh_hi[:, q % 2, :], hh_lo[:, q % 2, :]
                    for k in range(2):
                        for m, (w_, a_) in enumerate(((0, a_hi), (0, a_lo), (1, a_hi))):
                            last = nc.tensor.matmul(ps[:, bank + k, :], wd2[:, k, w_, :], a_, start=(m == 0), stop=(m == 2))
                        last.then_inc(s_lat, 1)
                    for j in range(4):
                        cols = slice(P * j, P * j + P)
                        for m, (a_, w_) in enumerate(((a_hi, 0), (a_hi, 1), (a_lo, 0))):
                            last = nc.tensor.matmul(ps[:, bank + 2, DH * j:DH * j + DH], a_[:, cols], wd2[:, 1, w_, 0:DH],
                                                    start=(j == 0 and m == 0), stop=(m == 2), skip_group_check=True)
                    last.then_inc(s_lat, 1)

        area_at[0] = 0
        qk = {n: carve(4 * S, F16).rearrange("p (u h n) -> p u h n", u=2, h=2) for n in ("Q1", "Q2", "K1", "K2")}
        p32 = carve(2 * 1024).rearrange("p (s n) -> p s n", s=2)
        p_hi = carve(4 * 1024, F16).rearrange("p (s n) -> p s n", s=4)
        p_lo = carve(4 * 1024, F16).rearrange("p (s n) -> p s n", s=4)
        ra = carve(2 * 512).rearrange("p (s n) -> p s n", s=2)
        rb = carve(2 * 512).rearrange("p (s n) -> p s n", s=2)
        rc = carve(2 * 512).rearrange("p (s n) -> p s n", s=2)
        r_hi = carve(4 * 512, F16).rearrange("p (c n) -> p c n", c=4)
        r_lo = carve(4 * 512, F16).rearrange("p (c n) -> p c n", c=4)
        cx = carve(TB * P).rearrange("p (t n) -> p t n", t=TB)
        cxt_hi = carve(S, F16).rearrange("p (t n) -> p t n", t=TB)
        cxt_lo = carve(S, F16).rearrange("p (t n) -> p t n", t=TB)
        lat = carve(2 * S, F16).rearrange("p (k n) -> p k n", k=2)
        wu_cur = carve(8 * P, F16).rearrange("p (w h n) -> p w h n", w=4, h=2)
        cv_cur = carve(2 * TB * CV, F16).rearrange("p (s t r) -> p s t r", s=2, t=TB)
        wc_cur = carve(2 * 2 * D, F16).rearrange("p (s h d) -> p s h d", s=2, h=2)
        mx = carve(2 * 16).rearrange("p (a k q) -> p a k q", a=2, k=2)
        mm = carve(2 * 8).rearrange("p (a q) -> p a q", a=2)
        m16 = carve(2 * 8, F16).rearrange("p (a q) -> p a q", a=2)
        mt = carve(2 * P, F16).rearrange("p (a n) -> p a n", a=2)
        rsum = carve(4)
        s_qz = sem("qk_zeroed")
        s_op = sem("operands_loaded")
        s_cv, s_wcc = ([sem(f"{n}_loaded_{k}") for k in range(2)] for n in ("cv", "wc"))
        s_mf, s_mr = sem("misc_filled"), sem("misc_read")
        s_rc, s_rh, s_rl = sem("rotated_sum"), sem("rotated_hi"), sem("rotated_lo")
        s_sq, s_sk = sem("q_stacked"), sem("k_stacked")
        s_mch, s_m16, s_mrow = sem("max_chain"), sem("max_f16"), sem("max_row_stored")
        s_s, s_e32, s_e16 = sem("scores"), sem("exp_f32"), sem("exp_hi")
        s_pd, s_pp = sem("p_lo_dve"), sem("p_lo_pool")
        s_pv, s_rs, s_cx = sem("pv"), sem("row_sums_inverted"), sem("context")
        s_oh = sem("context_T_hi")
        DC = 416
        ROT_SUM, ROT_HI, ROT_LO = 7, 8, 9
        STEPS = 16
        IT = UNITS // 2

        plan = {s: [] for s in range(STEPS)}
        for kind, of_step in ((("A", 0, 1), {0: 3, 1: 3, 2: 2}),
                              (("A", 1, 0), {3: 1, 4: 2, 5: 2, 6: 2, 7: 2, 8: 2, 9: 2, 10: 2, 11: 1}),
                              (("A", 1, 1), {12: 1, 13: 3, 14: 2, 15: 2})):
            i = 8 if kind == ("A", 0, 1) else 0
            for s, n in of_step.items():
                plan[s] += [(*kind, i + m) for m in range(n)]
                i += n
        plan[2] += [("OT", -1, 0, 0), ("OT", -1, 0, 1)]
        plan[3] = [plan[3][0], ("M", 0, 1, 0), ("OP", -1, 0, 0)]
        plan[4].append(("OP", -1, 0, 1))
        for i in range(8):
            plan[5 + i].append(("R", 2, 0, i))
        plan[12].append(("M", 1, 0, 0))
        before = ([("R", 0, 0, i) for i in range(8)] + [("R", 1, 0, i) for i in range(8)]
                  + [("A", 0, 0, i) for i in range(16)] + [("M", 0, 0, 0)] + [("A", 0, 1, i) for i in range(8)])

        after = [("OT", -1, 0, 0), ("OT", -1, 0, 1), ("OP", -1, 0, 0), ("OP", -1, 0, 1)]

        def items(s, left):
            return [i for i in plan[s] if i[1] <= left]
        per_unit = sum(len(p) for p in plan.values())

        def read_by(item, left=9):
            return [i for s in range(STEPS) for i in items(s, left)].index(item) + 1

        def run_units(eng, prologue, unit):
            prologue()
            n0 = len(before)
            with eng.Fori(0, IT - 1) as it:
                for k in range(2):
                    unit(it * 2 + k, k, 9, it * (2 * per_unit) + (n0 + k * per_unit), (n0 + k * per_unit) % 2)
            n = n0 + (IT - 1) * 2 * per_unit
            for k in range(2):
                unit(UNITS - 2 + k, k, 1 - k, n, n % 2)
                n += sum(len(items(s, 1 - k)) for s in range(STEPS))
            return n

        with nc.Block() as block:
            @block.tensor
            def _(pe):
                def misc(item, u, k, n, par, ot_read=None):
                    kind, off, hd, i = item
                    w, slot = u + off, (k + off) % 2
                    bank = ps[:, 6 + par, :]
                    if not (isinstance(n, int) and n < 2):
                        pe.wait_ge(s_mr, n - 1)
                    if kind == "R":
                        c, half_, sw = i // 2, (i // 2) % 2, i % 2
                        if i == 0:
                            pe.wait_ge(s_op, (w + 1) * 48)
                        which = 2 * (c // 2) + sw
                        src = lat[:, c // 2, 512 * half_:512 * half_ + 512]
                        nc.tensor.matmul(bank, wu_cur[:, which, 0, :], src, start=True, stop=False)
                        last = nc.tensor.matmul(bank, wu_cur[:, which, 1, :], src, start=False, stop=True)
                    elif kind == "A":
                        if i == 0 and hd == 0:
                            pe.wait_ge(s_sq, (w + 1) * 96)
                            pe.wait_ge(s_sk, (w + 1) * 96)
                        qt, kh = i // 2, i % 2
                        last = nc.tensor.matmul(bank, qk["Q1"][:, slot, hd, P * qt:P * qt + P],
                                                qk["K1"][:, slot, hd, 512 * kh:512 * kh + 512], start=True, stop=True)
                    elif kind == "M":
                        pe.wait_ge(s_m16, w * 2 + (hd + 1))
                        last = nc.tensor.matmul(bank[0:8, 0:P], m16[:, hd, :], ident16[:], start=True, stop=True)
                    elif kind == "OT":
                        pe.wait_ge(s_cx, u * 4 + 2)
                        for t in range(4):
                            last = nc.tensor.transpose(bank[:, P * t:P * t + P], cx[:, 4 * i + t, :], ident[:])
                    else:
                        pe.wait_ge(s_oh, u * 2 + (i + 1))
                        pe.wait_ge(s_mr, ot_read[i])
                        if i == 0:
                            pe.wait_ge(s_wcc[slot], (u + (2 - k)) * 16)
                        for t in range(4):
                            a = [c_[:, 4 * i + t, :] for c_ in (cxt_hi, cxt_lo)]
                            for m, (x_, y_) in enumerate(((0, 0), (0, 1), (1, 0))):
                                last = nc.tensor.matmul(bank[:, P * t:P * t + P], a[x_], wc_cur[:, slot, y_, :],
                                                        start=(t == 0 and m == 0), stop=(m == 2), skip_group_check=True)
                    last.then_inc(s_mf, 1)

                def scores(u, k, s, kk):
                    hd, qh, kt = s // 8, (s // 4) % 2, 2 * (s % 4) + kk
                    if s % 8 == 0 and kk == 0:
                        pe.wait_ge(s_mrow, (u * 2 + (hd + 2)) * 16)
                    o = ps[:, 2 * (s % 2) + kk, :]
                    keys, qs = slice(P * kt, P * kt + P), slice(512 * qh, 512 * qh + 512)
                    nc.tensor.matmul(o, qk["K1"][:, k, hd, keys], qk["Q1"][:, k, hd, qs], start=True, stop=False)
                    return nc.tensor.matmul(o, qk["K2"][:, k, hd, keys], qk["Q2"][:, k, hd, qs], start=False, stop=True)

                def pv(u, k, s, kk):
                    kt = 2 * (s % 4) + kk
                    g = u * STEPS + s
                    if kk == 0:
                        if s == 0:
                            pe.wait_ge(s_cv[k], (u + (2 - k)) * 8)
                        if s % 4 == 0:
                            pe.wait_ge(s_cx, u * 4 + (s // 4 + 1))
                        pe.wait_ge(s_pd, g + 2)
                        pe.wait_ge(s_pp, g + 2)
                    for j in range(4):
                        c = 512 * kk + P * j
                        o = ps[:, 4 + (s // 4) % 2, (DH + 1) * j:(DH + 1) * (j + 1)]
                        first = kt == 0 and j == 0
                        nc.tensor.matmul(o, p_hi[:, s % 4, c:c + P], cv_cur[:, k, kt, 0:DH + 1], start=first, stop=False,
                                         skip_group_check=True)
                        nc.tensor.matmul(o[:, 0:DH], p_hi[:, s % 4, c:c + P], cv_cur[:, k, kt, DH + 1:CV], start=False,
                                         stop=False, skip_group_check=True)
                        last = nc.tensor.matmul(o, p_lo[:, s % 4, c:c + P], cv_cur[:, k, kt, 0:DH + 1], start=False,
                                                stop=(kt == 7), skip_group_check=True)
                    return last

                def prologue():
                    pe.sem_inc(s_pv, 3)
                    for n, item in enumerate(before):
                        misc(item, 0, 0, n, n % 2)
                    for s in range(2):
                        scores(0, 0, s, 0)
                        scores(0, 0, s, 1).then_inc(s_s, 1)

                def unit(u, k, left, n, par):
                    ot_read = [n + read_by(("OT", -1, 0, i), left) for i in range(2)]
                    for s in range(STEPS):
                        work = []
                        if s + 2 < STEPS or left >= 1:
                            t, v_, k_ = ((s + 2), u, k) if s + 2 < STEPS else (s + 2 - STEPS, u + 1, 1 - k)

                            def half0(t=t, v_=v_, k_=k_, s=s):
                                pe.wait_ge(s_e16, u * STEPS + (s + 1))
                                scores(v_, k_, t, 0)

                            def half1(t=t, v_=v_, k_=k_):
                                scores(v_, k_, t, 1).then_inc(s_s, 1)
                            work += [half0, half1]
                        work += [lambda s=s: pv(u, k, s, 0), lambda s=s: pv(u, k, s, 1).then_inc(s_pv, 1)]
                        todo = items(s, left)
                        todo = list(todo)
                        for c in "wiwiwiwiii":
                            if c == "i" and todo:
                                misc(todo.pop(0), u, k, n, par, ot_read)
                                n, par = n + 1, 1 - par
                            if c == "w" and work:
                                work.pop(0)()
                n = run_units(pe, prologue, unit)
                for m, item in enumerate(after):
                    misc(item, UNITS, 0, n + m, (n + m) % 2, [n + 1, n + 2])

            @block.vector
            def _(v):
                def misc(item, u, k, n, par):
                    kind, off, hd, i = item
                    w = u + off
                    bank = ps[:, 6 + par, :]
                    v.wait_ge(s_mf, n + 1)
                    if kind == "R":
                        c, half_, sw = i // 2, (i // 2) % 2, i % 2
                        if not (isinstance(w, int) and w == 0 and c < 2):
                            v.wait_ge(s_rc, w * 4 + (c - 1))
                        nc.vector.tensor_tensor((ra, rb)[sw][:, c % 2, :], bank, cs[:, sw, 512 * half_:512 * half_ + 512],
                                                ALU.mult).then_inc(s_mr, 1)
                    elif kind == "A":
                        qt, kh = i // 2, i % 2
                        nc.vector.tensor_reduce(mx[:, hd, kh, qt:qt + 1], bank, AX.X, ALU.max).then_inc(s_mr, 1)
                        if i == 15:
                            v.wait_ge(s_mr, n + 1)
                            nc.vector.tensor_tensor(mm[:, hd, :], mx[:, hd, 0, :], mx[:, hd, 1, :], ALU.max).then_inc(s_mch, 1)
                            v.wait_ge(s_mch, w * 2 + (hd + 1))
                            nc.vector.tensor_scalar(m16[:, hd, :], mm[:, hd, :], 1.0 / MAX_SCALE, None, ALU.mult).then_inc(s_m16, 1)
                    elif kind == "M":
                        if not (isinstance(w, int) and w == 0):
                            v.wait_ge(s_mrow, (w * 2 + hd) * 16)
                        nc.vector.tensor_copy(mt[0:8, hd, :], bank[0:8, 0:P]).then_inc(s_mr, 1)
                    elif kind == "OT":
                        v.wait_ge(s_oh, u * 2 + (i + 1))
                        c_ = slice(4 * i, 4 * i + 4)
                        nc.vector.tensor_tensor(cxt_lo[:, c_, :], bank.rearrange("p (t n) -> p t n", t=4), cxt_hi[:, c_, :],
                                                ALU.subtract).then_inc(s_mr, 1)
                    else:
                        grp = (u + (off + PAIRS)) // PAIRS
                        xo = xg[:, bass.ds(grp, 1), 4 * i:4 * i + 4, :].rearrange("p b t d -> p (b t) d")
                        nc.vector.tensor_tensor(xo, xo, bank.rearrange("p (t d) -> p t d", d=D), ALU.add).then_inc(s_mr, 1)

                def low(g, s):
                    v.wait_ge(s_e32, g + 1)
                    v.wait_ge(s_e16, g + 1)
                    if not (isinstance(g, int) and g == 0):
                        v.wait_ge(s_pv, g)
                    nc.vector.tensor_tensor(p_lo[:, s % 4, 0:DC], p32[:, s % 2, 0:DC], p_hi[:, s % 4, 0:DC],
                                            ALU.subtract).then_inc(s_pd, 1)

                def prologue():
                    v.sem_inc(s_cx, 2)
                    v.sem_inc(s_pd, 1)
                    for n_ in ("Q1", "Q2", "K1", "K2"):
                        nc.vector.memset(qk[n_], 0.0).then_inc(s_qz, 1)
                    nc.vector.memset(cx, 0.0).then_inc(s_qz, 1)
                    v.wait_ge(s_qz, 5)
                    nc.vector.memset(qk["K2"][64:65], -MAX_SCALE).then_inc(s_qz, 1)
                    for n, item in enumerate(before):
                        misc(item, 0, 0, n, n % 2)
                    low(0, 0)

                def unit(u, k, left, n, par):
                    for s in range(STEPS):
                        todo = items(s, left)
                        for m, item in enumerate(todo):
                            misc(item, u, k, n, par)
                            n, par = n + 1, 1 - par
                            if m == 1 and (s + 1 < STEPS or left >= 1):
                                low(u * STEPS + (s + 1), (s + 1) % STEPS)
                        if len(todo) < 2 and (s + 1 < STEPS or left >= 1):
                            low(u * STEPS + (s + 1), (s + 1) % STEPS)
                        if s % 4 == 3:
                            hd, qh = s // 8, (s // 4) % 2
                            o = ps[:, 4 + (s // 4) % 2, 0:4 * (DH + 1)].rearrange("p (t r) -> p t r", r=DH + 1)
                            v.wait_ge(s_pv, u * STEPS + (s + 4))
                            nc.vector.reciprocal(rsum, o[:, :, DH]).then_inc(s_rs, 1)
                            v.wait_ge(s_rs, u * 4 + (s // 4 + 1))
                            nc.vector.tensor_tensor(cx[:, 4 * qh:4 * qh + 4, DH * hd:DH * hd + DH], o[:, :, 0:DH],
                                                    rsum.unsqueeze(2).broadcast_to([P, 4, DH]), ALU.mult).then_inc(s_cx, 1)
                n = run_units(v, prologue, unit)
                for m, item in enumerate(after):
                    misc(item, UNITS, 0, n + m, (n + m) % 2)

            @block.scalar
            def _(act):
                def exps(g, s):
                    act.wait_ge(s_s, g + 1)
                    if not (isinstance(g, int) and g == 0):
                        act.wait_ge(s_pd, g)
                        act.wait_ge(s_pp, g)
                    sc = ps[:, 2 * (s % 2):2 * (s % 2) + 2, :].rearrange("p b n -> p (b n)")
                    nc.scalar.activation(p32[:, s % 2, :], sc, ACT.Exp, scale=0.125).then_inc(s_e32, 1)
                    if not (isinstance(g, int) and g == 0):
                        act.wait_ge(s_pv, g)
                    nc.scalar.activation(p_hi[:, s % 4, :], sc, ACT.Exp, scale=0.125).then_inc(s_e16, 1)

                def rot_hi(w, c):
                    act.wait_ge(s_rc, w * 4 + (c + 1))
                    if not (isinstance(w, int) and w == 0):
                        act.wait_ge((s_sq, s_sk)[c // 2], w * 96)
                    nc.scalar.copy(r_hi[:, c, :], rc[:, c % 2, :]).then_inc(s_rh, 1)

                def context_hi(i, n, par):
                    act.wait_ge(s_mf, n + 1)
                    bank = ps[:, 6 + par, :].rearrange("p (t n) -> p t n", t=4)
                    nc.scalar.copy(cxt_hi[:, 4 * i:4 * i + 4, :], bank).then_inc(s_oh, 1)

                def prologue():
                    for w in range(2):
                        for c in range(4):
                            rot_hi(w, c)
                    exps(0, 0)

                def unit(u, k, left, n, par):
                    for s in range(STEPS):
                        if s + 1 < STEPS or left >= 1:
                            exps(u * STEPS + (s + 1), (s + 1) % STEPS)
                        for item in items(s, left):
                            if item[0] == "OT":
                                context_hi(item[3], n, par)
                            n, par = n + 1, 1 - par
                        if left >= 2 and s >= ROT_HI and (s - ROT_HI) % 2 == 0 and s < ROT_HI + 8:
                            rot_hi(u + 2, (s - ROT_HI) // 2)
                n = run_units(act, prologue, unit)
                for i in range(2):
                    context_hi(i, n + i, (n + i) % 2)

            @block.gpsimd
            def _(pool):
                def low(g, s):
                    pool.wait_ge(s_e32, g + 1)
                    pool.wait_ge(s_e16, g + 1)
                    if not (isinstance(g, int) and g == 0):
                        pool.wait_ge(s_pv, g)
                    nc.gpsimd.tensor_tensor(p_lo[:, s % 4, DC:], p32[:, s % 2, DC:], p_hi[:, s % 4, DC:],
                                            ALU.subtract).then_inc(s_pp, 1)

                def rot_sum(w, c, read):
                    pool.wait_ge(s_mr, read)
                    if not (isinstance(w, int) and w == 0 and c < 2):
                        pool.wait_ge(s_rl, w * 4 + (c - 1))
                    nc.gpsimd.tensor_tensor(rc[:, c % 2, :], ra[:, c % 2, :], rb[:, c % 2, :], ALU.add).then_inc(s_rc, 1)

                def rot_lo(w, c):
                    pool.wait_ge(s_rh, w * 4 + (c + 1))
                    nc.gpsimd.tensor_tensor(r_lo[:, c, :], rc[:, c % 2, :], r_hi[:, c, :], ALU.subtract).then_inc(s_rl, 1)

                def prologue():
                    pool.sem_inc(s_pp, 1)
                    for w in range(2):
                        for c in range(4):
                            rot_sum(w, c, 8 * w + 2 * c + 2)
                            rot_lo(w, c)
                    low(0, 0)

                def unit(u, k, left, n, par):
                    for s in range(STEPS):
                        if s + 1 < STEPS or left >= 1:
                            low(u * STEPS + (s + 1), (s + 1) % STEPS)
                        if left >= 2:
                            if s >= ROT_SUM and (s - ROT_SUM) % 2 == 0 and s < ROT_SUM + 8:
                                c = (s - ROT_SUM) // 2
                                rot_sum(u + 2, c, n + read_by(("R", 2, 0, 2 * c + 1), left))
                            if s >= ROT_LO and (s - ROT_LO) % 2 == 0 and s < ROT_LO + 8:
                                rot_lo(u + 2, (s - ROT_LO) // 2)
                run_units(pool, prologue, unit)

            @block.sync
            def _(sp):
                def operands(w):
                    b_, j_ = w // PAIRS, w % PAIRS
                    sp.dma_start(lat[:, 0, :], cq_t[:, bass.ds(b_ * S, S)]).then_inc(s_op, 16)
                    sp.dma_start(lat[:, 1, :], ckv_t[:, bass.ds(b_ * S, S)]).then_inc(s_op, 16)
                    sp.dma_start(wu_cur.rearrange("p w h n -> p (w h) n"),
                                 wup[:].rearrange("p w h n -> p (w h) n")[:, :, bass.ds(j_ * P, P)]).then_inc(s_op, 16)

                def latent_rows(w, slot):
                    sp.dma_start(cv_cur[:, slot].rearrange("p t r -> p (t r)"),
                                 cv_all[:].rearrange("p t r -> p (t r)")[:, bass.ds((w // PAIRS) * (TB * CV), TB * CV)]).then_inc(s_cv[slot], 16)

                def out_weights(w, slot):
                    j_ = w % PAIRS
                    sp.dma_start(wc_cur[:, slot, 0, :], wc_hi[:].rearrange("p j d -> p (j d)")[:, bass.ds(j_ * D, D)]).then_inc(s_wcc[slot], 16)
                    sp.dma_start(wc_cur[:, slot, 1, :], wc_lo[:].rearrange("p j d -> p (j d)")[:, bass.ds(j_ * D, D)]).then_inc(s_wcc[slot], 16)

                def stack(w, slot):
                    for kind, done in ((0, s_sq), (2, s_sk)):
                        for sm in (s_rh, s_rl):
                            sp.wait_ge(sm, w * 4 + (kind + 2))
                        for hd in range(2):
                            rows = slice(64 * hd, 64 * hd + 64)
                            hi, lo = (t[rows, kind:kind + 2, :].rearrange("p c n -> p (c n)") for t in (r_hi, r_lo))
                            if kind == 0:
                                moves = (("Q1", 0, hi), ("Q1", 64, lo), ("Q2", 0, hi))
                            else:
                                moves = (("K1", 0, hi), ("K1", 64, hi), ("K2", 0, lo))
                            for name_, row, src in moves:
                                sp.dma_start(qk[name_][row:row + 64, slot, hd, :], src).then_inc(done, 16)

                def max_row(slot, hd, read):
                    sp.wait_ge(s_mr, read)
                    sp.dma_start(qk["Q2"][64:65, slot, hd, :], mt[0:8, hd, :]).then_inc(s_mrow, 16)

                def prologue():
                    sp.sem_inc(s_mrow, 16)
                    operands(0)
                    latent_rows(0, 0)
                    out_weights(0, 1)
                    sp.wait_ge(s_mr, 8)
                    operands(1)
                    sp.wait_ge(s_qz, 6)
                    stack(0, 0)
                    stack(1, 1)
                    max_row(0, 0, before.index(("M", 0, 0, 0)) + 1)

                def unit(u, k, left, n, par):
                    sp.wait_ge(s_mr, n)
                    if left >= 2:
                        operands(u + 2)
                    out_weights(u, k)
                    if left >= 1:
                        sp.wait_ge(s_pv, u * STEPS + 3)
                        latent_rows(u + 1, 1 - k)
                    max_row(k, 1, n + read_by(("M", 0, 1, 0), left))
                    if left >= 1:
                        max_row(1 - k, 0, n + read_by(("M", 1, 0, 0), left))
                    if left >= 2:
                        sp.wait_ge(s_s, (u + 1) * STEPS)
                        stack(u + 2, k)
                run_units(sp, prologue, unit)
        ffn("f2")
        s_out = sem("out_written")
        with nc.Block() as block:
            @block.sync
            def _(sp):
                o_v = out.rearrange("(n p) d -> p n d", p=P)
                for c in range(4):
                    sp.dma_start(o_v[:, 8 * c:8 * c + 8, :], xs[:, 8 * c:8 * c + 8, :]).then_inc(s_out, 16)
                sp.wait_ge(s_out, 64)


_INS = ["x", "wg", "wu", "wd", "wr", "temp", "wdq", "wdkv", "wuq", "wuk", "wuv", "wo", "lns", "lnb", "rope"]


def kernel(L0_attn_x, L0_attn_w_down_q, L0_attn_w_down_kv, L0_attn_w_up_q, L0_attn_w_up_k, L0_attn_w_up_v, L0_attn_w_out,
           L0_attn_ln_scale, L0_attn_ln_bias, L0_ffn_Wg, L0_ffn_Wu, L0_ffn_Wd, L0_ffn_Wr, L0_ffn_temperature):
    import concourse.bacc as bacc
    from concourse.bass_utils import run_bass_kernel_spmd

    given = {
        "x": np.reshape(L0_attn_x, (T, D)), "wg": L0_ffn_Wg, "wu": L0_ffn_Wu, "wd": L0_ffn_Wd, "wr": L0_ffn_Wr,
        "temp": L0_ffn_temperature, "wdq": np.transpose(L0_attn_w_down_q), "wdkv": np.transpose(L0_attn_w_down_kv),
        "wuq": np.transpose(L0_attn_w_up_q), "wuk": np.transpose(L0_attn_w_up_k), "wuv": L0_attn_w_up_v,
        "wo": np.transpose(L0_attn_w_out), "lns": L0_attn_ln_scale, "lnb": L0_attn_ln_bias, "rope": rope_tables(),
    }
    nc = bacc.Bacc("TRN2", target_bir_lowering=False, num_devices=1)
    arrays, args = {}, []
    for n in _INS:
        a = np.ascontiguousarray(given[n])
        arrays["in_" + n] = a
        args.append(nc.dram_tensor("in_" + n, a.shape, mybir.dt.from_np(a.dtype), kind="ExternalInput").ap())
    args.append(nc.dram_tensor("out_x", (T, D), F32, kind="ExternalOutput").ap())
    build(nc, *args)
    r = run_bass_kernel_spmd(nc, [arrays], core_ids=[0])
    return np.reshape(r.results[0]["out_x"], (B, S, D))
```

```python
from contextlib import ExitStack

import numpy as np

import concourse.bass as bass
from concourse import mybir

F32 = mybir.dt.float32
F16 = mybir.dt.float16
ALU = mybir.AluOpType
ACT = mybir.ActivationFunctionType
AX = mybir.AxisListType

B, S, D = 4, 1024, 128
H, DH = 16, 64
E, I = 8, 128
P = 128
T = B * S
NT = T // P
NQ = T // 512
TB = S // P
PAIRS = H // 2
UNITS = B * PAIRS
EPS = 1e-5
ZONE_LOW = float(0.5 - np.log(4.0 / 3.0))
CENTER = float(1.0 / np.e)
Z_LOW = float(np.log(ZONE_LOW / (1.0 - ZONE_LOW)))
MAX_SCALE = 64.0


def rope_tables():
    inv_freq = 1.0 / 10000.0 ** (np.arange(0, DH, 2, dtype=np.float32) / DH)
    freqs = np.outer(np.arange(S, dtype=np.float32), inv_freq)
    cos = np.concatenate([np.cos(freqs), np.cos(freqs)], -1)[:, ::2]
    sin = np.concatenate([np.sin(freqs), np.sin(freqs)], -1)[:, ::2]
    sign = np.where(np.arange(DH) % 2 == 0, -1.0, 1.0)[:, None]
    c = np.repeat(cos.T, 2, axis=0)
    s = np.repeat(sin.T, 2, axis=0) * sign
    return np.stack([np.tile(c, (2, 1)), np.tile(s, (2, 1))], 1).astype(np.float32)


def up_columns(wq, wk):
    swap = np.arange(H * DH) ^ 1
    four = np.stack([w[:, i] for w in (np.transpose(wq), np.transpose(wk)) for i in (np.arange(H * DH), swap)], 1)
    return np.concatenate([four, four], 0)


def build(nc, x, wg, wu, wd, wr, temp, wdq, wdkv, wup_in, wuv, wo, lns, lnb, rope, out):
    with ExitStack() as ctx:
        def sb(name, shape, dt=F32):
            return ctx.enter_context(nc.sbuf_tensor(name, shape, dt))

        def sem(name):
            return ctx.enter_context(nc.semaphore(name))

        ps = ctx.enter_context(nc.psum_tensor("ps", [P, 8, 512], F32))

        xg = sb("xg", [P, B + 2, TB, D])
        xs = xg[:, 1:B + 1].rearrange("p b t d -> p (b t) d")
        ident = sb("ident", [P, P])
        ident16 = sb("ident16", [P, P], F16)
        rows_sum = sb("rows_sum", [P, E], F16)
        xt_hi = sb("xt_hi", [P, T], F16)
        xt_lo = sb("xt_lo", [P, T], F16)
        w_ffn = {n: (sb(n + "_hi", [P, E, P], F16), sb(n + "_lo", [P, E, P], F16)) for n in ("wg", "wu", "wd")}
        wr_hi, wr_lo = sb("wr_hi", [P, E], F16), sb("wr_lo", [P, E], F16)
        rtemp = sb("rtemp", [P, 1])
        rev = sb("rev", [P, E])
        GT = (B + 2) * TB
        stat6 = sb("stat6", [P, 2, TB, 6])
        mean, var, m_sum, m_dif, v_sum = (sb(n, [P, 2, TB]) for n in ("mean", "var", "mean_sum", "mean_dif", "var_sum"))
        tanh_bias = sb("tanh_bias", [P, 2])
        rs0, rs1, root_tmp, rstd, nmr, rstd2, rr, nmrr, rstd_1 = (
            sb(n, [P, GT]) for n in ("var_eps", "minus_half_var", "root_tmp", "rstd", "minus_mean_rstd", "rstd2", "rstd_both",
                                     "minus_mean_both", "rstd_plus_1"))
        cq_t, ckv_t = xt_hi, xt_lo
        CV = 2 * DH + 1
        cv_all = sb("cv_all", [P, NT, CV], F16)
        wc_hi = sb("wc_hi", [P, PAIRS, D], F16)
        wc_lo = sb("wc_lo", [P, PAIRS, D], F16)
        wup = sb("wup", [P, 4, 2, H * DH], F16)
        wd2 = sb("wd2", [P, 2, 3, P], F16)
        lnsb = sb("lnsb", [P, 2])
        cs = sb("cs", [P, 2, S])

        big = 26 * 1024
        area = sb("area", [P, big])
        area_at = [0]

        def carve(n, dt=F32):
            words = n if dt is F32 else n // 2
            a = area[:, area_at[0]:area_at[0] + words]
            area_at[0] += words
            assert area_at[0] <= big, area_at
            return a if dt is F32 else a.bitcast(dt)

        FFN_WORDS = 9 * 1024
        area_at[0] = FFN_WORDS
        st = {n: carve(E * P) for n in ("wg", "wu", "wd")}
        st_up = carve(4 * H * DH).rearrange("p (w n) -> p w n", w=4)
        st_v = carve(PAIRS * DH)
        st_o = carve(PAIRS * D)
        st_dn = carve(2 * P)
        st_r = carve(E)
        staging_end = area_at[0]
        s_x = [sem(f"x_loaded_{n}") for n in range(B)]
        s_w = [sem(n + "_loaded") for n in ("wr", "wg", "wu", "wd")]
        s_up, s_small, s_rope = sem("up_w_loaded"), sem("small_loaded"), sem("rope_loaded")
        s_id, s_idz, s_c0 = sem("ident_ready"), sem("ident_zeroed"), sem("consts_ready")
        s_hi, s_lo, s_wc = sem("w_hi_done"), sem("w_lo_done"), sem("wc_product")
        s_wch, s_wcr = sem("wc_hi_done"), sem("wc_read")
        s_uph, s_upl, s_dnh, s_dnl = sem("up_hi_done"), sem("up_lo_done"), sem("down_hi_done"), sem("down_lo_done")
        s_rt = sem("rtemp_done")
        x_v = x.rearrange("(n p) d -> p n d", p=P)
        split = [(st_r, wr_hi[:], wr_lo[:])] + [(st[n], *(t[:].rearrange("p e i -> p (e i)") for t in w_ffn[n]))
                                                for n in ("wg", "wu", "wd")]

        def load_sync(sp):
            def load_x(c):
                sp.dma_start(xs[:, 8 * c:8 * c + 8, :], x_v[:, 8 * c:8 * c + 8, :]).then_inc(s_x[c], 16)
            load_x(0)
            sp.dma_start(st_r, wr).then_inc(s_w[0], 16)
            sp.dma_start(st["wg"].rearrange("p (e i) -> p e i", e=E), wg.rearrange("e d i -> d e i")).then_inc(s_w[1], 16)
            sp.dma_start(st["wu"].rearrange("p (e i) -> p e i", e=E), wu.rearrange("e d i -> d e i")).then_inc(s_w[2], 16)
            load_x(1)
            sp.dma_start(st["wd"].rearrange("p (e i) -> p e i", e=E), wd.rearrange("e i d -> i e d")).then_inc(s_w[3], 16)
            load_x(2)
            load_x(3)
            sp.dma_start(st_up, wup_in).then_inc(s_up, 16)
            sp.dma_start(cs[:], rope).then_inc(s_rope, 16)

        def load_scalar(act):
            act.dma_start(st_v.rearrange("p (j r) -> p j r", j=PAIRS), wuv.rearrange("(j p) r -> p j r", p=P)).then_inc(s_small, 16)
            act.dma_start(st_o.rearrange("p (j d) -> p j d", j=PAIRS), wo.rearrange("(j p) d -> p j d", p=P)).then_inc(s_small, 16)
            act.dma_start(rtemp[:, 0:1], temp.rearrange("(p a) -> p a", a=1).broadcast_to([P, 1])).then_inc(s_small, 16)
            act.dma_start(st_dn[:, 0:64], wdq).then_inc(s_small, 16)
            act.dma_start(st_dn[:, 64:128], wdkv).then_inc(s_small, 16)
            act.dma_start(lnsb[:, 0:1], lns.rearrange("(p a) -> p a", a=1)).then_inc(s_small, 16)
            act.dma_start(lnsb[:, 1:2], lnb.rearrange("(p a) -> p a", a=1)).then_inc(s_small, 16)

        def high_halves(act):
            for n, (src, hi, _) in enumerate(split):
                act.wait_ge(s_w[n], 16)
                nc.scalar.copy(hi, src).then_inc(s_hi, 1)

        def low_halves(pool):
            for n, (src, hi, lo) in enumerate(split):
                pool.wait_ge(s_w[n], 16)
                pool.wait_ge(s_hi, n + 1)
                nc.gpsimd.tensor_tensor(lo, src, hi, ALU.subtract).then_inc(s_lo, 1)

        def identities(pool):
            nc.gpsimd.memset(ident[:], 0.0).then_inc(s_idz, 1)
            nc.gpsimd.memset(ident16[:], 0.0).then_inc(s_idz, 1)
            pool.wait_ge(s_idz, 2)
            for m in (ident, ident16):
                nc.gpsimd.affine_select(out=m[:], in_=m[:], compare_op=ALU.not_equal, fill=1.0, base=0,
                                        pattern=[[-1, P]], channel_multiplier=1).then_inc(s_id, 1)
            pool.wait_ge(s_id, 2)
            nc.gpsimd.tensor_tensor(rows_sum[:], ident16[:, 0:E], ident16[:, E:2 * E], ALU.add).then_inc(s_id, 1)
            nc.gpsimd.memset(cv_all[:, :, DH:DH + 1], 1.0).then_inc(s_c0, 1)

        def constants(v):
            nc.vector.memset(tanh_bias[:, 0:1], (0.5 - CENTER) * 0.5 / 0.1).then_inc(s_c0, 1)
            nc.vector.memset(tanh_bias[:, 1:2], (0.5 - CENTER) * 0.5 / 0.3).then_inc(s_c0, 1)
            for e in range(E):
                nc.vector.memset(rev[:, e:e + 1], float(E - e)).then_inc(s_c0, 1)
            nc.vector.memset(xg[:, 0], 0.0).then_inc(s_c0, 1)
            nc.vector.memset(xg[:, B + 1], 0.0).then_inc(s_c0, 1)

        def latent_out_product(pe):
            pe.wait_ge(s_small, 112)
            for hh in range(2):
                rows = slice(64 * hh, 64 * hh + 64)
                for j in range(PAIRS):
                    last = nc.tensor.matmul(ps[rows, 2 * hh + j // 4, D * (j % 4):D * (j % 4) + D],
                                            st_v[rows, DH * j:DH * j + DH], st_o[rows, D * j:D * j + D],
                                            start=True, stop=True)
            last.then_inc(s_wc, 1)
        wc_parts = [(slice(64 * hh, 64 * hh + 64), slice(4 * g, 4 * g + 4), 2 * hh + g) for hh in range(2) for g in range(2)]

        def latent_out_high(act):
            act.wait_ge(s_wc, 1)
            for rows, js, bank in wc_parts:
                nc.scalar.copy(wc_hi[rows, js, :], ps[rows, bank, :].rearrange("p (j d) -> p j d", d=D)).then_inc(s_wch, 1)

        def latent_out_low(v):
            for n, (rows, js, bank) in enumerate(wc_parts):
                v.wait_ge(s_wch, n + 1)
                nc.vector.tensor_tensor(wc_lo[rows, js, :], ps[rows, bank, :].rearrange("p (j d) -> p j d", d=D),
                                        wc_hi[rows, js, :], ALU.subtract).then_inc(s_wcr, 1)

        def up_high(act, w):
            act.wait_ge(s_up, 16)
            nc.scalar.copy(wup[:, w, 0, :], st_up[:, w, :]).then_inc(s_uph, 1)

        def up_low(pool, n):
            w, cols = n // 2, slice(512 * (n % 2), 512 * (n % 2) + 512)
            pool.wait_ge(s_uph, w + 1)
            nc.gpsimd.tensor_tensor(wup[:, w, 1, cols], st_up[:, w, cols], wup[:, w, 0, cols], ALU.subtract).then_inc(s_upl, 1)

        def down_high(act, n):
            k, r = n // 2, n % 2
            nc.scalar.copy(wd2[:, k, 0, 64 * r:64 * r + 64], st_dn[:, 64 * k:64 * k + 64]).then_inc(s_dnh, 1)

        def down_low(v, n):
            k, r = n // 2, n % 2
            v.wait_ge(s_dnh, n + 1)
            nc.vector.tensor_tensor(wd2[:, k, 1, 64 * r:64 * r + 64], st_dn[:, 64 * k:64 * k + 64],
                                    wd2[:, k, 0, 64 * r:64 * r + 64], ALU.subtract).then_inc(s_dnl, 1)

        def inverse_root(link, v_eps, minus_half, root, tmp):
            i32 = mybir.dt.int32
            link(lambda: nc.vector.tensor_scalar(root.bitcast(i32), v_eps.bitcast(i32), -0.5, float(0x5F3759DF), ALU.mult, ALU.add))
            link(lambda: nc.vector.tensor_scalar(minus_half, v_eps, -0.5, None, ALU.mult))
            for _ in range(3):
                link(lambda: nc.vector.tensor_tensor(tmp, root, root, ALU.mult))
                link(lambda: nc.vector.tensor_tensor(tmp, tmp, minus_half, ALU.mult))
                link(lambda: nc.vector.scalar_tensor_tensor(root, tmp, 1.5, root, ALU.add, ALU.mult))

        NORM_LINKS, NORM2_LINKS = 26, 42

        def chain(v, s, p, count):
            at = [0]

            def link(make, back=1):
                done = p * count + (at[0] + 1 - back)
                if not isinstance(done, int) or done > 0:
                    v.wait_ge(s, done)
                make().then_inc(s, 1)
                at[0] += 1
            return link, at

        def norm(v, g, s_chain, s_done, twice=False):
            count = NORM2_LINKS if twice else NORM_LINKS
            link, at = chain(v, s_chain, g, count)
            at_g = bass.ds(g * TB, TB)
            v_e, m_h, rt, tm, nm, rt2, both, nmb, plus1 = (
                t[:, at_g] for t in (rs0, rs1, rstd, root_tmp, nmr, rstd2, rr, nmrr, rstd_1))
            kind = 1 if twice else 0
            m_, var_, ms, md, vs = (t[:, kind, :] for t in (mean, var, m_sum, m_dif, v_sum))
            m_e, v_e_, m_o, v_o_ = (stat6[:, kind, :, c] for c in (1, 2, 4, 5))

            def stats(n):
                xj = xg[:, bass.ds(g, 1), n, :].rearrange("p b d -> p (b d)")
                at[0] += 1
                nc.vector.bn_stats(stat6[:, kind, n, :], xj).then_inc(s_chain, 1)

            made = [lambda: nc.vector.tensor_tensor(ms, m_e, m_o, ALU.add),
                    lambda: nc.vector.tensor_tensor(md, m_e, m_o, ALU.subtract),
                    lambda: nc.vector.tensor_tensor(vs, v_e_, v_o_, ALU.add),
                    lambda: nc.vector.scalar_tensor_tensor(md, md, 0.25, md, ALU.mult, ALU.mult),
                    lambda: nc.vector.tensor_scalar(m_, ms, 0.5, None, ALU.mult),
                    lambda: nc.vector.scalar_tensor_tensor(var_, vs, 1.0 / D, md, ALU.mult, ALU.add)]
            backs = [1, 2, 3, 2, 2, 2]
            made.append(lambda: nc.vector.tensor_scalar(v_e, var_, EPS, None, ALU.add))
            inverse_root(made.append, v_e, m_h, rt, tm)
            if twice:
                made += [lambda: nc.vector.tensor_tensor(v_e, var_, rt, ALU.mult),
                         lambda: nc.vector.tensor_tensor(v_e, v_e, rt, ALU.mult),
                         lambda: nc.vector.tensor_scalar(v_e, v_e, EPS, None, ALU.add)]
                inverse_root(made.append, v_e, m_h, rt2, tm)
                made += [lambda: nc.vector.tensor_tensor(both, rt, rt2, ALU.mult),
                         lambda: nc.vector.scalar_tensor_tensor(nmb, m_, -1.0, both, ALU.mult, ALU.mult)]

            def last():
                assert at[0] == count, at
                v.wait_ge(s_chain, g * count + count)
                if twice:
                    nc.vector.tensor_scalar(plus1, rt, 1.0, None, ALU.add)
                nc.vector.scalar_tensor_tensor(nm, m_, -1.0, rt, ALU.mult, ALU.mult).then_inc(s_done, 1)
            backs += [1] * (len(made) - len(backs))
            return ([lambda n=n: stats(n) for n in range(TB)]
                    + [lambda make=make, back=back: link(make, back) for make, back in zip(made, backs)] + [last])

        area_at[0] = 0
        qk = {n: carve(4 * S, F16).rearrange("p (u h n) -> p u h n", u=2, h=2) for n in ("Q1", "K1")}
        here, area_at[0] = area_at[0], big - (2 * 2 * S + TB * P)
        assert area_at[0] >= staging_end
        qk.update({n: carve(4 * S, F16).rearrange("p (u h n) -> p u h n", u=2, h=2) for n in ("Q2", "K2")})
        cx = carve(TB * P).rearrange("p (t n) -> p t n", t=TB)
        s_qz = sem("qk_zeroed")

        def clear(v, n):
            if n > 8:
                v.wait_ge(s_qz, 8)
                nc.vector.memset(qk["K2"][64:65, (n - 9) // 2, (n - 9) % 2, :], -MAX_SCALE).then_inc(s_qz, 1)
                return
            if n < 8:
                t_ = qk[("Q2", "K2")[n // 4]][:, (n // 2) % 2, n % 2, :]
            else:
                t_ = cx
            nc.vector.memset(t_, 0.0).then_inc(s_qz, 1)
        area_at[0] = here
        p32 = carve(2 * 1024).rearrange("p (s n) -> p s n", s=2)
        p_hi = carve(4 * 1024, F16).rearrange("p (s n) -> p s n", s=4)
        p_lo = carve(4 * 1024, F16).rearrange("p (s n) -> p s n", s=4)
        ra = carve(2 * 512).rearrange("p (s n) -> p s n", s=2)
        rb = carve(2 * 512).rearrange("p (s n) -> p s n", s=2)
        rc = carve(2 * 512).rearrange("p (s n) -> p s n", s=2)
        r_hi = carve(4 * 512, F16).rearrange("p (c n) -> p c n", c=4)
        r_lo = carve(4 * 512, F16).rearrange("p (c n) -> p c n", c=4)
        cxt_hi = carve(S, F16).rearrange("p (t n) -> p t n", t=TB)
        cxt_lo = carve(S, F16).rearrange("p (t n) -> p t n", t=TB)
        lat = carve(2 * S, F16).rearrange("p (k n) -> p k n", k=2)
        wu_cur = carve(2 * 8 * P, F16).rearrange("p (s w h n) -> p s w h n", s=2, w=4, h=2)
        cv_cur = carve(2 * TB * CV, F16).rearrange("p (s t r) -> p s t r", s=2, t=TB)
        wc_cur = carve(2 * 2 * D, F16).rearrange("p (s h d) -> p s h d", s=2, h=2)
        mx = carve(2 * 16).rearrange("p (a k q) -> p a k q", a=2, k=2)
        mm = carve(2 * 8).rearrange("p (a q) -> p a q", a=2)
        m16 = carve(2 * 8, F16).rearrange("p (a q) -> p a q", a=2)
        mt = carve(2 * P, F16).rearrange("p (a n) -> p a n", a=2)
        rsum = carve(4)
        s_op = sem("latents_loaded")
        s_cv, s_wcc, s_wu = ([sem(f"{n}_loaded_{k}") for k in range(2)] for n in ("cv", "wc", "wu"))
        s_mf, s_mr = sem("misc_filled"), sem("misc_read")
        s_rc, s_rh, s_rl = sem("rotated_sum"), sem("rotated_hi"), sem("rotated_lo")
        s_sq, s_sk = sem("q_stacked"), sem("k_stacked")
        s_mch, s_m16, s_mrow = sem("max_chain"), sem("max_f16"), sem("max_row_stored")
        s_s, s_e32, s_e16 = sem("scores"), sem("exp_f32"), sem("exp_hi")
        s_pd, s_pp = sem("p_lo_dve"), sem("p_lo_pool")
        s_pv, s_rs, s_cx = sem("pv"), sem("row_sums_inverted"), sem("context")
        s_oh = sem("context_T_hi")

        def latents_of(sp, w):
            b_ = w // PAIRS
            sp.dma_start(lat[:, 0, :], cq_t[:, bass.ds(b_ * S, S)]).then_inc(s_op, 16)
            sp.dma_start(lat[:, 1, :], ckv_t[:, bass.ds(b_ * S, S)]).then_inc(s_op, 16)

        def up_weights(sp, w, slot):
            j_ = w % PAIRS
            sp.dma_start(wu_cur[:, slot].rearrange("p w h n -> p (w h) n"),
                         wup[:].rearrange("p w h n -> p (w h) n")[:, :, bass.ds(j_ * P, P)]).then_inc(s_wu[slot], 16)

        def latent_rows(sp, w, slot):
            sp.dma_start(cv_cur[:, slot].rearrange("p t r -> p (t r)"),
                         cv_all[:].rearrange("p t r -> p (t r)")[:, bass.ds((w // PAIRS) * (TB * CV), TB * CV)]).then_inc(s_cv[slot], 16)

        def out_weights(sp, w, slot):
            j_ = w % PAIRS
            sp.dma_start(wc_cur[:, slot, 0, :], wc_hi[:].rearrange("p j d -> p (j d)")[:, bass.ds(j_ * D, D)]).then_inc(s_wcc[slot], 16)
            sp.dma_start(wc_cur[:, slot, 1, :], wc_lo[:].rearrange("p j d -> p (j d)")[:, bass.ds(j_ * D, D)]).then_inc(s_wcc[slot], 16)

        def ffn(name):
            area_at[0] = 0
            xn = carve(2 * 512).rearrange("p (s j d) -> p s j d", s=2, j=4)
            gate = carve(2 * 512).rearrange("p (s n) -> p s n", s=2)
            gu = carve(2 * 512).rearrange("p (s n) -> p s n", s=2)
            hw = carve(2 * 512).rearrange("p (s n) -> p s n", s=2)
            h_hi = carve(2 * 512, F16).rearrange("p (s n) -> p s n", s=2)
            h_lo = carve(2 * 512, F16).rearrange("p (s n) -> p s n", s=2)
            wt = carve(2 * 512, F16).rearrange("p (s n) -> p s n", s=2)
            z, th, w, fb, t0, t1, oh, fbm = (
                carve(TB * E).rearrange("p (t e) -> p t e", e=E) for _ in range(8))
            t01 = carve(2 * TB * E).rearrange("p (a n) -> p a n", a=2)
            ex = carve(2 * TB * E).rearrange("p (a n) -> p a n", a=2)
            abs01 = carve(2 * TB * E).rearrange("p (a n) -> p a n", a=2)
            r0, r1, r2, r3, r4, r5, r6, r7 = (carve(TB) for _ in range(8))
            whl = carve(TB * 2 * E, F16).rearrange("p (t h e) -> p t h e", h=2, e=E)
            assert area_at[0] <= FFN_WORDS
            first = name == "f1"
            s_ch, s_rstd = sem(name + "_norm_chain"), sem(name + "_rstd")
            s_xn, s_xT, s_xhi, s_xlo = (sem(name + n) for n in ("_xn", "_xT", "_xT_hi", "_xT_lo"))
            s_z, s_zr, s_th, s_tt, s_ex = (sem(name + n) for n in ("_logits", "_logits_read", "_tanh", "_tanh_dist", "_abs_tanh"))
            s_rc, s_routed = sem(name + "_route_chain"), sem(name + "_route_done")
            s_wr, s_wt, s_wz = sem(name + "_w_rows"), sem(name + "_w_rows_stored"), sem(name + "_w_rows_zeroed")
            s_g, s_u, s_wb = (sem(name + n) for n in ("_gate", "_up", "_wbcast"))
            s_si, s_gu, s_hw = sem(name + "_silu"), sem(name + "_gate_up"), sem(name + "_h")
            s_hh, s_hl, s_dn = sem(name + "_h_hi"), sem(name + "_h_lo"), sem(name + "_down")
            s_y0, s_y = sem(name + "_y_zeroed"), sem(name + "_y_added")
            (g_hi, g_lo), (u_hi, u_lo), (d_hi, d_lo) = (w_ffn[n] for n in ("wg", "wu", "wd"))
            ROUTE_LINKS = 27

            def turns(eng, body):
                with eng.Fori(0, B - 1) as it:
                    body(it, False)
                body(B - 1, True)

            with nc.Block() as block:
                @block.sync
                def _(sp):
                    if first:
                        load_sync(sp)
                        sp.wait_ge(s_rope, 16)
                    else:
                        o_v = out.rearrange("(n p) d -> p n d", p=P)
                        for b_ in range(B):
                            for a in range(2):
                                if b_ < B - 1 and a == 0:
                                    continue
                                sp.wait_ge(s_y, 2 * b_ + (3 if a else 2))
                                n0 = TB * b_ + (4 * a if b_ == B - 1 else 0)
                                n1 = TB * b_ + 4 * (a + 1)
                                sp.dma_start(o_v[:, n0:n1, :], xs[:, n0:n1, :]).then_inc(s_out, 16)
                        sp.wait_ge(s_out, (B + 1) * 16)

                @block.tensor
                def _(pe):
                    def transpose(p, a):
                        pe.wait_ge(s_xn, 2 * p + (a + 1))
                        if a == 1:
                            pe.wait_ge(s_xlo, 2 * p + 1)
                        elif not isinstance(p, int):
                            pe.wait_ge(s_y, 2 * p - 1)
                        for j in range(4):
                            last = nc.tensor.transpose(ps[:, 7, P * j:P * j + P], xn[:, a, j, :], ident[:])
                        last.then_inc(s_xT, 1)

                    def router(p):
                        pe.wait_ge(s_xlo, 2 * p + 2)
                        for j in range(TB):
                            cols = bass.ds(p * S + P * j, P)
                            for k, (a, b) in enumerate(((xt_hi, wr_hi), (xt_hi, wr_lo), (xt_lo, wr_hi))):
                                last = nc.tensor.matmul(ps[:, 7, E * j:E * j + E], a[:, cols], b[:],
                                                        start=(j == 0 and k == 0), stop=(k == 2), skip_group_check=True)
                        last.then_inc(s_z, 1)

                    def weight_rows(p, a):
                        if a == 0:
                            pe.wait_ge(s_routed, p + 1)
                            if not isinstance(p, int):
                                pe.wait_ge(s_y, 2 * p)
                        else:
                            pe.wait_ge(s_wt, 2 * p + 1)
                        for j in range(4):
                            last = nc.tensor.matmul(ps[0:2 * E, 6, P * j:P * j + P],
                                                    whl[:, 4 * a + j].rearrange("p h e -> p (h e)"), ident16[:],
                                                    start=(j == 0), stop=True, skip_group_check=True)
                        last.then_inc(s_wr, 1)

                    def gate_up(i, t, k):
                        e, b = k % E, k % 2
                        cols = bass.ds(t * S + 512 * (k // E), 512)
                        for w_h, w_l, bank, read, done in ((g_hi, g_lo, 0, s_si, s_g), (u_hi, u_lo, 2, s_gu, s_u)):
                            if not (isinstance(t, int) and t == 0 and k < 2):
                                pe.wait_ge(read, i - 1 if read is s_si else i)
                            o = ps[:, bank + b, :]
                            nc.tensor.matmul(o, w_h[:, e, :], xt_hi[:, cols], start=True, stop=False)
                            nc.tensor.matmul(o, w_h[:, e, :], xt_lo[:, cols], start=False, stop=False)
                            nc.tensor.matmul(o, w_l[:, e, :], xt_hi[:, cols], start=False, stop=True).then_inc(done, 1)

                    def weight(i, t, k):
                        if not (isinstance(t, int) and t == 0 and k < 2):
                            pe.wait_ge(s_hw, i - 1)
                        if k % E == 0:
                            pe.wait_ge(s_wt, 2 * t + (k // E + 1))
                        nc.tensor.matmul(ps[:, 4 + k % 2, :], rows_sum[:, k % E:k % E + 1].broadcast_to([P, P]),
                                         wt[:, k // E, :], start=True, stop=True).then_inc(s_wb, 1)

                    def down(i, t, k, last_turn):
                        e, b = k % E, k % 2
                        if k == 0:
                            pe.wait_ge(s_wt, 2 * t + 2)
                        if k == E:
                            if last_turn:
                                pe.wait_ge(s_y, 2 * t + 1)
                            else:
                                pe.wait_ge(s_zr, t + 2)
                        pe.wait_ge(s_hh, i + 1)
                        pe.wait_ge(s_hl, i + 3)
                        for j in range(4):
                            o = ps[:, 6 + k // E, P * j:P * j + P]
                            cols = slice(P * j, P * j + P)
                            nc.tensor.matmul(o, h_hi[:, b, cols], d_hi[:, e, :], start=(e == 0 and j == 0), stop=False,
                                             skip_group_check=True)
                            nc.tensor.matmul(o, h_hi[:, b, cols], d_lo[:, e, :], start=False, stop=False, skip_group_check=True)
                            last = nc.tensor.matmul(o, h_lo[:, b, cols], d_hi[:, e, :], start=False, stop=(e == E - 1),
                                                    skip_group_check=True)
                        last.then_inc(s_dn, 1)

                    def turn(t, last):
                        for k in range(16):
                            i = t * 16 + k
                            t2, k2 = (t, k + 2) if k < 14 else (t + 1, k - 14)
                            ahead = k < 14 or not last
                            if ahead:
                                gate_up(i + 2, t2, k2)
                            if not last and k == 5:
                                router(t + 1)
                            down(i, t, k, last)
                            if not last and k in (1, 3):
                                transpose(t + 1, (k - 1) // 2)
                            if not last and k in (13, 14):
                                weight_rows(t + 1, k - 13)
                            if ahead:
                                weight(i + 2, t2, k2)
                    pe.sem_inc(s_dn, 2)
                    if first:
                        pe.wait_ge(s_id, 3)
                    transpose(0, 0)
                    transpose(0, 1)
                    if first:
                        pe.wait_ge(s_lo, 1)
                    router(0)
                    if first:
                        latent_out_product(pe)
                        pe.wait_ge(s_lo, 4)
                        pe.wait_ge(s_wcr, len(wc_parts))
                    gate_up(0, 0, 0)
                    gate_up(1, 0, 1)
                    weight_rows(0, 0)
                    weight_rows(0, 1)
                    pe.wait_ge(s_wz, 1)
                    weight(0, 0, 0)
                    weight(1, 0, 1)
                    turns(pe, turn)

                @block.scalar
                def _(act):
                    def normed(p, a):
                        act.wait_ge(s_rstd, p + 1)
                        if not isinstance(p, int):
                            act.wait_ge(s_xT, 2 * p + (a - 1))
                        for j in range(4):
                            n = 4 * a + j
                            xj = xg[:, bass.ds(p + 1, 1), n, :].rearrange("p b d -> p (b d)")
                            at_n = bass.ds((p + 1) * TB + n, 1)
                            last = nc.scalar.activation(xn[:, a, j, :], xj, ACT.Identity, scale=rstd[:, at_n], bias=nmr[:, at_n])
                        last.then_inc(s_xn, 1)

                    def hi(p, a):
                        act.wait_ge(s_xT, 2 * p + (a + 1))
                        nc.scalar.copy(xt_hi[:, bass.ds(p * S + 512 * a, 512)], ps[:, 7, :]).then_inc(s_xhi, 1)

                    def tanh_z(p):
                        act.wait_ge(s_zr, p + 1)
                        nc.scalar.activation(th, z, ACT.Tanh, scale=0.5).then_inc(s_th, 1)

                    def tanh_dist(p):
                        act.wait_ge(s_th, p + 1)
                        th_ = th.rearrange("p t e -> p (t e)")
                        for m, width in enumerate((0.1, 0.3)):
                            nc.scalar.activation(t01[:, m], th_, ACT.Tanh, scale=0.5 * 0.5 / width,
                                                 bias=tanh_bias[:, m:m + 1]).then_inc(s_tt, 1)
                        act.wait_ge(s_tt, 2 * p + 2)
                        nc.scalar.activation(abs01, t01, ACT.Abs, scale=0.5).then_inc(s_ex, 1)

                    def rows(p, a):
                        act.wait_ge(s_wr, 2 * p + (a + 1))
                        nc.scalar.copy(wt[0:2 * E, a, :], ps[0:2 * E, 6, :]).then_inc(s_wt, 1)

                    def silu(i, t, k):
                        act.wait_ge(s_g, i + 1)
                        if not (isinstance(t, int) and t == 0 and k == 0):
                            act.wait_ge(s_gu, i)
                        nc.scalar.activation(gate[:, k % 2, :], ps[:, k % 2, :], ACT.Silu).then_inc(s_si, 1)

                    def turn(t, last):
                        for k in range(16):
                            i = t * 16 + k
                            if not (last and k == 15):
                                silu(i + 1, *((t, k + 1) if k < 15 else (t + 1, 0)))
                            act.wait_ge(s_hw, i + 1)
                            act.wait_ge(s_dn, i + 1)
                            nc.scalar.copy(h_hi[:, k % 2, :], hw[:, k % 2, :]).then_inc(s_hh, 1)
                            if not last:
                                if k in (0, 1):
                                    normed(t + 1, k)
                                if k in (2, 4):
                                    hi(t + 1, (k - 2) // 2)
                                if k == 6:
                                    tanh_z(t + 1)
                                    tanh_dist(t + 1)
                                if k in (14, 15):
                                    rows(t + 1, k - 14)
                            elif first:
                                if k in (1, 3, 5, 7):
                                    up_high(act, k // 2)
                                if k in (8, 9, 10, 11):
                                    down_high(act, k - 8)
                    if first:
                        load_scalar(act)
                    normed(0, 0)
                    normed(0, 1)
                    hi(0, 0)
                    hi(0, 1)
                    if first:
                        high_halves(act)
                        act.wait_ge(s_c0, 2)
                    tanh_z(0)
                    tanh_dist(0)
                    if first:
                        latent_out_high(act)
                    act.wait_ge(s_wz, 1)
                    silu(0, 0, 0)
                    rows(0, 0)
                    rows(0, 1)
                    turns(act, turn)

                @block.gpsimd
                def _(pool):
                    def turn(t, last):
                        for k in range(16):
                            i = t * 16 + k
                            pool.wait_ge(s_hh, i + 1)
                            pool.wait_ge(s_dn, i + 1)
                            nc.gpsimd.tensor_tensor(h_lo[:, k % 2, :], hw[:, k % 2, :], h_hi[:, k % 2, :],
                                                    ALU.subtract).then_inc(s_hl, 1)
                            if first and last and 3 <= k < 11:
                                up_low(pool, k - 3)
                    if first:
                        identities(pool)
                    nc.gpsimd.memset(wt, 0.0).then_inc(s_wz, 1)
                    if first:
                        low_halves(pool)
                    pool.sem_inc(s_hl, 2)
                    turns(pool, turn)

                @block.vector
                def _(v):
                    def lo(p, a):
                        v.wait_ge(s_xhi, 2 * p + (a + 1))
                        cols = bass.ds(p * S + 512 * a, 512)
                        nc.vector.tensor_tensor(xt_lo[:, cols], ps[:, 7, :], xt_hi[:, cols], ALU.subtract).then_inc(s_xlo, 1)

                    def logits(p):
                        v.wait_ge(s_z, p + 1)
                        nc.vector.tensor_scalar(z, ps[:, 7, 0:TB * E].rearrange("p (t e) -> p t e", e=E), rtemp[:, 0:1],
                                                None, ALU.mult).then_inc(s_zr, 1)

                    def wide(t):
                        return t.unsqueeze(2).broadcast_to([P, TB, E])

                    def flat(t):
                        return t.rearrange("p t e -> p (t e)")

                    def route(p):
                        link, at = chain(v, s_rc, p, ROUTE_LINKS)
                        tt, stt, ts, tr = (nc.vector.tensor_tensor, nc.vector.scalar_tensor_tensor,
                                           nc.vector.tensor_scalar, nc.vector.tensor_reduce)
                        w_all, fb_all = (ex[:, m].rearrange("p (t e) -> p t e", e=E) for m in range(2))
                        idx = rev[:].unsqueeze(1).broadcast_to([P, TB, E])
                        parts = []

                        def do(make, back=1):
                            parts.append(lambda: link(make, back))
                        parts.append(lambda: v.wait_ge(s_ex, p + 1))
                        do(lambda: ts(abs01, abs01, 0.5, None, ALU.add))
                        do(lambda: nc.vector.reciprocal(ex, abs01))
                        do(lambda: ts(ex, ex, -1.0, None, ALU.add))
                        parts.append(lambda: v.wait_ge(s_zr, p + 1))
                        do(lambda: tr(r2, fb_all, AX.X, ALU.max))
                        do(lambda: stt(w, z, Z_LOW, w_all, ALU.is_ge, ALU.mult), 2)
                        do(lambda: tt(t0, fb_all, wide(r2), ALU.is_equal), 2)
                        do(lambda: stt(w, z, 0.0, w, ALU.is_le, ALU.mult), 2)
                        do(lambda: tt(t0, t0, idx, ALU.mult), 2)
                        do(lambda: tr(r0, w, AX.X, ALU.add), 2)
                        do(lambda: tr(r3, t0, AX.X, ALU.max), 2)
                        do(lambda: ts(r1, r0, 1e-8, None, ALU.is_lt), 2)
                        do(lambda: tt(oh, t0, wide(r3), ALU.is_equal), 2)
                        do(lambda: stt(fbm, oh, -4.0, fb_all, ALU.mult, ALU.add))
                        do(lambda: tr(r4, fbm, AX.X, ALU.max))
                        do(lambda: tt(fb, fb_all, wide(r1), ALU.mult), 2)
                        do(lambda: tt(t1, fbm, wide(r4), ALU.is_equal), 2)
                        do(lambda: tt(t1, t1, idx, ALU.mult))
                        do(lambda: tr(r5, t1, AX.X, ALU.max))
                        do(lambda: tt(t1, t1, wide(r5), ALU.is_equal))
                        do(lambda: tt(oh, oh, t1, ALU.add))
                        do(lambda: tt(fb, fb, oh, ALU.mult))
                        do(lambda: tt(w, w, fb, ALU.add))
                        do(lambda: tr(r6, w, AX.X, ALU.add))
                        do(lambda: ts(r6, r6, 1e-8, None, ALU.max))
                        do(lambda: nc.vector.reciprocal(r7, r6))
                        do(lambda: tt(w, w, wide(r7), ALU.mult))
                        do(lambda: nc.vector.tensor_copy(whl[:, :, 0, :], w))

                        def low_half():
                            assert at[0] == ROUTE_LINKS, at
                            v.wait_ge(s_rc, p * ROUTE_LINKS + ROUTE_LINKS)
                            tt(whl[:, :, 1, :], w, whl[:, :, 0, :], ALU.subtract).then_inc(s_routed, 1)
                        return parts + [low_half]

                    def add_y(t, a):
                        v.wait_ge(s_dn, t * 16 + (10 if a == 0 else 2))
                        xq = xg[:, bass.ds(t + (1 - a), 1), 4 * a:4 * a + 4, :].rearrange("p b t d -> p (b t) d")
                        y_ = ps[:, 6 + a, :].rearrange("p (t d) -> p t d", d=D)
                        nc.vector.scalar_tensor_tensor(xq, y_, 0.5, xq, ALU.mult, ALU.add).then_inc(s_y, 1)

                    def turn(t, last):
                        spread = [0] * 16
                        between, after_ = ({k: [] for k in range(16)} for _ in range(2))
                        after_[1].append(lambda: add_y(t, 1))
                        after_[9].append(lambda: add_y(t, 0))
                        if not last:
                            between[3].append(lambda: lo(t + 1, 0))
                            between[5].append(lambda: lo(t + 1, 1))
                            after_[6].append(lambda: logits(t + 1))
                            for parts, n_between, n_after in (
                                    (norm(v, t + 3, s_ch, s_rstd), {k: 1 for k in (2, 3, 4, 5, 6, 7, 14, 15)}, {k: 4 for k in range(2, 8)}),
                                    (route(t + 1), {k: 1 for k in range(8, 13)}, {k: 5 for k in range(8, 13)})):
                                for k in range(16):
                                    for part_list, count in ((between, n_between), (after_, n_after)):
                                        for _ in range(count.get(k, 0)):
                                            if parts:
                                                part_list[k].append(parts.pop(0))
                                assert not parts, len(parts)
                        if first:
                            parts = norm(v, t + 0, s_an, s_ann, True)
                            for k in range(1, 16):
                                mine, others = [parts.pop(0) for _ in range(min(3, len(parts)))], after_[k]
                                after_[k] = []
                                if k == 1:
                                    after_[k].append(others.pop(0))
                                while mine or others:
                                    for some in (others, mine):
                                        if some:
                                            after_[k].append(some.pop(0))
                            assert not parts
                        if first and last:
                            for k in range(4):
                                after_[9 + k].append(lambda k=k: down_low(v, k))
                            for k in range(13):
                                after_[2 + k].append(lambda k=k: clear(v, k))
                        for k in range(16):
                            i, b = t * 16 + k, k % 2
                            v.wait_ge(s_si, i + 1)
                            v.wait_ge(s_u, i + 1)
                            nc.vector.tensor_tensor(gu[:, b, :], gate[:, b, :], ps[:, 2 + b, :], ALU.mult).then_inc(s_gu, 1)
                            for f in between[k]:
                                f()
                            v.wait_ge(s_gu, i + 2)
                            v.wait_ge(s_wb, i + 1)
                            v.wait_ge(s_hl, i + 1)
                            nc.vector.tensor_tensor(hw[:, b, :], gu[:, b, :], ps[:, 4 + b, :], ALU.mult).then_inc(s_hw, 1)
                            for f in after_[k]:
                                f()
                    v.sem_inc(s_gu, 1)
                    if first:
                        constants(v)
                        v.wait_ge(s_x[0], 16)
                    v.sem_inc(s_ch, NORM_LINKS)
                    for f in norm(v, 1, s_ch, s_rstd):
                        f()
                    if first:
                        v.wait_ge(s_small, 112)
                        nc.vector.reciprocal(rtemp[:], rtemp[:]).then_inc(s_rt, 1)
                        v.wait_ge(s_rt, 1)
                    lo(0, 0)
                    lo(0, 1)
                    logits(0)
                    v.wait_ge(s_zr, 1)
                    nc.vector.memset(ps[:, 7, :], 0.0).then_inc(s_y0, 1)
                    if first:
                        v.wait_ge(s_x[1], 16)
                        v.wait_ge(s_c0, 13)
                    norm_parts, route_parts = norm(v, 2, s_ch, s_rstd), route(0)
                    for f in norm_parts[:TB]:
                        f()
                    norm_parts = norm_parts[TB:]
                    while norm_parts or route_parts:
                        for parts in (route_parts, norm_parts):
                            if parts:
                                parts.pop(0)()
                    if first:
                        latent_out_low(v)
                        for c in (2, 3):
                            v.wait_ge(s_x[c], 16)
                    v.wait_ge(s_y0, 1)
                    turns(v, turn)
                    add_y(B, 1)

        s_out = sem("out_written")
        s_an, s_ann = sem("attention_norm_chain"), sem("attention_norms")
        ffn("f1")
        area_at[0] = 0
        yn = carve(2 * 512).rearrange("p (s j d) -> p s j d", s=2, j=4)
        h32 = carve(2 * 512).rearrange("p (s n) -> p s n", s=2)
        hh_hi = carve(2 * 512, F16).rearrange("p (s n) -> p s n", s=2)
        hh_lo = carve(2 * 512, F16).rearrange("p (s n) -> p s n", s=2)
        assert area_at[0] <= 2 * 2 * S
        s_yr, s_yn, s_yT = sem("y_residual"), sem("yn_done"), sem("yT_done")
        s_h32, s_hhi, s_hlo = sem("h32_done"), sem("hT_hi"), sem("hT_lo")
        s_lat, s_lhi, s_llo = sem("latents_product"), sem("latents_hi"), sem("latents_lo")
        with nc.Block() as block:
            @block.sync
            def _(sp):
                sp.wait_ge(s_lhi, 6)
                sp.wait_ge(s_llo, 6)
                up_weights(sp, 0, 0)
                latents_of(sp, 0)
                up_weights(sp, 1, 1)
                latent_rows(sp, 0, 0)
                out_weights(sp, 0, 1)

            @block.vector
            def _(v):
                norm_parts = norm(v, B, s_an, s_ann, True)

                def some_norm(n):
                    for f in norm_parts[:n]:
                        f()
                    del norm_parts[:n]
                for q in range(NQ + 1):
                    some_norm(3)
                    if q < NQ:
                        v.wait_ge(s_yT, q + 1)
                        if q >= 2:
                            v.wait_ge(s_hlo, q - 1)
                        nc.vector.tensor_scalar(h32[:, q % 2, :], ps[:, q % 2, :], lnsb[:, 0:1], lnsb[:, 1:2],
                                                ALU.mult, ALU.add).then_inc(s_h32, 1)
                        some_norm(3)
                        v.wait_ge(s_yn, q + 1)
                        for n in range(4 * q, 4 * q + 4):
                            nc.vector.tensor_scalar(xs[:, n, :], xs[:, n, :], rstd_1[:, TB + n:TB + n + 1], nmr[:, TB + n:TB + n + 1],
                                                    ALU.mult, ALU.add).then_inc(s_yr, 1)
                            some_norm(1)
                    if q >= 1:
                        p, cols, bank = q - 1, slice(512 * q - 512, 512 * q), 2 + 3 * ((q - 1) % 2)
                        for k, dst in enumerate((cq_t, ckv_t)):
                            v.wait_ge(s_lhi, 3 * p + k + 1)
                            nc.vector.tensor_tensor(dst[64:128, cols], ps[64:128, bank + k, :], dst[64:128, cols],
                                                    ALU.subtract).then_inc(s_llo, 1)
                        v.wait_ge(s_lhi, 3 * p + 3)
                        cvt = cv_all[:, 4 * p:4 * p + 4, :]
                        nc.vector.tensor_tensor(cvt[:, :, DH + 1:CV], ps[:, bank + 2, 0:256].rearrange("p (t r) -> p t r", r=DH),
                                                cvt[:, :, 0:DH], ALU.subtract).then_inc(s_llo, 1)

            @block.gpsimd
            def _(pool):
                for q in range(NQ):
                    pool.wait_ge(s_h32, q + 1)
                    pool.wait_ge(s_hhi, q + 1)
                    if q >= 2:
                        pool.wait_ge(s_lat, 3 * (q - 1))
                    nc.gpsimd.tensor_tensor(hh_lo[:, q % 2, :], h32[:, q % 2, :], hh_hi[:, q % 2, :],
                                            ALU.subtract).then_inc(s_hlo, 1)

            @block.scalar
            def _(act):
                def normed(q):
                    if q >= 2:
                        act.wait_ge(s_yT, q - 1)
                    if q == NQ - 2:
                        act.wait_ge(s_ann, B + 1)
                    for j in range(4):
                        n = 4 * q + j
                        last = nc.scalar.activation(yn[:, q % 2, j, :], xs[:, n, :], ACT.Identity,
                                                    scale=rr[:, TB + n:TB + n + 1], bias=nmrr[:, TB + n:TB + n + 1])
                    last.then_inc(s_yn, 1)

                def latents(q):
                    cols, bank = slice(512 * q, 512 * q + 512), 2 + 3 * (q % 2)
                    for k, dst in enumerate((cq_t, ckv_t)):
                        act.wait_ge(s_lat, 3 * q + k + 1)
                        nc.scalar.copy(dst[:, cols], ps[:, bank + k, :]).then_inc(s_lhi, 1)
                    act.wait_ge(s_lat, 3 * q + 3)
                    nc.scalar.copy(cv_all[:, 4 * q:4 * q + 4, 0:DH],
                                   ps[:, bank + 2, 0:256].rearrange("p (t r) -> p t r", r=DH)).then_inc(s_lhi, 1)
                normed(0)
                for q in range(NQ):
                    if q + 1 < NQ:
                        normed(q + 1)
                    act.wait_ge(s_h32, q + 1)
                    if q >= 2:
                        act.wait_ge(s_lat, 3 * (q - 1))
                    nc.scalar.copy(hh_hi[:, q % 2, :], h32[:, q % 2, :]).then_inc(s_hhi, 1)
                    if q >= 1:
                        latents(q - 1)
                latents(NQ - 1)

            @block.tensor
            def _(pe):
                def transposes(q):
                    pe.wait_ge(s_yn, q + 1)
                    if q >= 2:
                        pe.wait_ge(s_h32, q - 1)
                    for j in range(4):
                        last = nc.tensor.transpose(ps[:, q % 2, P * j:P * j + P], yn[:, q % 2, j, :], ident[:])
                    last.then_inc(s_yT, 1)
                transposes(0)
                for q in range(NQ):
                    if q + 1 < NQ:
                        transposes(q + 1)
                    bank = 2 + 3 * (q % 2)
                    pe.wait_ge(s_hlo, q + 1)
                    if q >= 2:
                        pe.wait_ge(s_llo, 3 * (q - 1))
                    a_hi, a_lo = hh_hi[:, q % 2, :], hh_lo[:, q % 2, :]
                    for k in range(2):
                        for m, (w_, a_) in enumerate(((0, a_hi), (0, a_lo), (1, a_hi))):
                            last = nc.tensor.matmul(ps[:, bank + k, :], wd2[:, k, w_, :], a_, start=(m == 0), stop=(m == 2))
                        last.then_inc(s_lat, 1)
                    for j in range(4):
                        cols = slice(P * j, P * j + P)
                        for m, (a_, w_) in enumerate(((a_hi, 0), (a_hi, 1), (a_lo, 0))):
                            last = nc.tensor.matmul(ps[:, bank + 2, DH * j:DH * j + DH], a_[:, cols], wd2[:, 1, w_, 0:DH],
                                                    start=(j == 0 and m == 0), stop=(m == 2), skip_group_check=True)
                    last.then_inc(s_lat, 1)

        DC = 400
        ROT_SUM, ROT_HI, ROT_LO = 7, 8, 9
        STEPS = 16
        IT = UNITS // 2

        def tiles(kind, off, hd, *span):
            return [(kind, off, hd, i) for i in range(*span)]
        letters = {"a": tiles("A", 0, 1, 8, 16), "b": tiles("A", 1, 0, 16), "c": tiles("A", 1, 1, 8), "r": tiles("R", 2, 0, 8),
                   "T": tiles("OT", -1, 0, 2), "P": tiles("OP", -1, 0, 2), "m": tiles("M", 0, 1, 1), "n": tiles("M", 1, 0, 1)}
        plan = {s: [letters[c].pop(0) for c in step] for s, step in enumerate(
            "aaa aaa aaTT bmP bb bbPr bbr bbr bbr bbr bbbr cr nrc cc cc cc".split())}
        assert not any(letters.values())
        letters = {"r": tiles("R", 0, 0, 8), "s": tiles("R", 1, 0, 8), "a": tiles("A", 0, 0, 16), "m": tiles("M", 0, 0, 1),
                   "b": tiles("A", 0, 1, 8)}
        before = [letters[c].pop(0) for c in "rrrrrrrrssssaaaaaassaaaaaassaaaambbbbbbbb"]
        assert not any(letters.values())
        read_before = {item: n + 1 for n, item in enumerate(before)}

        after = [("OT", -1, 0, 0), ("OT", -1, 0, 1), ("OP", -1, 0, 0), ("OP", -1, 0, 1)]

        def items(s, left):
            return [i for i in plan[s] if i[1] <= left]
        per_unit = sum(len(p) for p in plan.values())

        def read_by(item, left=9):
            return [i for s in range(STEPS) for i in items(s, left)].index(item) + 1

        def run_units(eng, prologue, unit):
            prologue()
            n0 = len(before)
            with eng.Fori(0, IT - 1) as it:
                for k in range(2):
                    unit(it * 2 + k, k, 9, it * (2 * per_unit) + (n0 + k * per_unit), (n0 + k * per_unit) % 2)
            n = n0 + (IT - 1) * 2 * per_unit
            for k in range(2):
                unit(UNITS - 2 + k, k, 1 - k, n, n % 2)
                n += sum(len(items(s, 1 - k)) for s in range(STEPS))
            return n

        with nc.Block() as block:
            @block.tensor
            def _(pe):
                def misc(item, u, k, n, par, ot_read=None):
                    kind, off, hd, i = item
                    w, slot = u + off, (k + off) % 2
                    bank = ps[:, 6 + par, :]
                    if not (isinstance(n, int) and n < 2):
                        pe.wait_ge(s_mr, n - 1)
                    if kind == "R":
                        c, half_, sw = i // 2, (i // 2) % 2, i % 2
                        if i == 0:
                            pe.wait_ge(s_op, 32 if isinstance(w, int) and w == 0 else w * 32)
                            pe.wait_ge(s_wu[slot], (w + (2 - slot)) * 8)
                        which = 2 * (c // 2) + sw
                        src = lat[:, c // 2, 512 * half_:512 * half_ + 512]
                        nc.tensor.matmul(bank, wu_cur[:, slot, which, 0, :], src, start=True, stop=False)
                        last = nc.tensor.matmul(bank, wu_cur[:, slot, which, 1, :], src, start=False, stop=True)
                    elif kind == "A":
                        if i == 0 and hd == 0:
                            pe.wait_ge(s_sq, (w + 1) * 96)
                            pe.wait_ge(s_sk, (w + 1) * 96)
                        qt, kh = i // 2, i % 2
                        last = nc.tensor.matmul(bank, qk["Q1"][:, slot, hd, P * qt:P * qt + P],
                                                qk["K1"][:, slot, hd, 512 * kh:512 * kh + 512], start=True, stop=True)
                    elif kind == "M":
                        pe.wait_ge(s_m16, w * 2 + (hd + 1))
                        last = nc.tensor.matmul(bank[0:8, 0:P], m16[:, hd, :], ident16[:], start=True, stop=True)
                    elif kind == "OT":
                        pe.wait_ge(s_cx, u * 4 + 2)
                        for t in range(4):
                            last = nc.tensor.transpose(bank[:, P * t:P * t + P], cx[:, 4 * i + t, :], ident[:])
                    else:
                        pe.wait_ge(s_oh, u * 2 + (i + 1))
                        pe.wait_ge(s_mr, ot_read[i])
                        if i == 0:
                            pe.wait_ge(s_wcc[slot], (u + (2 - k)) * 16)
                        for t in range(4):
                            a = [c_[:, 4 * i + t, :] for c_ in (cxt_hi, cxt_lo)]
                            for m, (x_, y_) in enumerate(((0, 0), (0, 1), (1, 0))):
                                last = nc.tensor.matmul(bank[:, P * t:P * t + P], a[x_], wc_cur[:, slot, y_, :],
                                                        start=(t == 0 and m == 0), stop=(m == 2), skip_group_check=True)
                    last.then_inc(s_mf, 1)

                def scores(u, k, s, kk):
                    hd, qh, kt = s // 8, (s // 4) % 2, 2 * (s % 4) + kk
                    if s % 8 == 0 and kk == 0:
                        pe.wait_ge(s_mrow, (u * 2 + (hd + 2)) * 16)
                    o = ps[:, 2 * (s % 2) + kk, :]
                    keys, qs = slice(P * kt, P * kt + P), slice(512 * qh, 512 * qh + 512)
                    nc.tensor.matmul(o, qk["K1"][:, k, hd, keys], qk["Q1"][:, k, hd, qs], start=True, stop=False)
                    return nc.tensor.matmul(o, qk["K2"][:, k, hd, keys], qk["Q2"][:, k, hd, qs], start=False, stop=True)

                def pv(u, k, s, kk):
                    kt = 2 * (s % 4) + kk
                    g = u * STEPS + s
                    if kk == 0:
                        if s == 0:
                            pe.wait_ge(s_cv[k], (u + (2 - k)) * 8)
                        if s % 4 == 0:
                            pe.wait_ge(s_cx, u * 4 + (s // 4 + 1))
                        pe.wait_ge(s_pd, g + 2)
                        pe.wait_ge(s_pp, g + 2)
                    for j in range(4):
                        c = 512 * kk + P * j
                        o = ps[:, 4 + (s // 4) % 2, (DH + 1) * j:(DH + 1) * (j + 1)]
                        first = kt == 0 and j == 0
                        nc.tensor.matmul(o, p_hi[:, s % 4, c:c + P], cv_cur[:, k, kt, 0:DH + 1], start=first, stop=False,
                                         skip_group_check=True)
                        nc.tensor.matmul(o[:, 0:DH], p_hi[:, s % 4, c:c + P], cv_cur[:, k, kt, DH + 1:CV], start=False,
                                         stop=False, skip_group_check=True)
                        last = nc.tensor.matmul(o, p_lo[:, s % 4, c:c + P], cv_cur[:, k, kt, 0:DH + 1], start=False,
                                                stop=(kt == 7), skip_group_check=True)
                    return last

                def prologue():
                    pe.sem_inc(s_pv, 3)
                    for n, item in enumerate(before):
                        misc(item, 0, 0, n, n % 2)
                    for s in range(2):
                        scores(0, 0, s, 0)
                        scores(0, 0, s, 1).then_inc(s_s, 1)

                def unit(u, k, left, n, par):
                    ot_read = [n + read_by(("OT", -1, 0, i), left) for i in range(2)]
                    for s in range(STEPS):
                        work = []
                        if s + 2 < STEPS or left >= 1:
                            t, v_, k_ = ((s + 2), u, k) if s + 2 < STEPS else (s + 2 - STEPS, u + 1, 1 - k)

                            def half0(t=t, v_=v_, k_=k_, s=s):
                                pe.wait_ge(s_e16, u * STEPS + (s + 1))
                                scores(v_, k_, t, 0)

                            def half1(t=t, v_=v_, k_=k_):
                                scores(v_, k_, t, 1).then_inc(s_s, 1)
                            work += [half0, half1]
                        work += [lambda s=s: pv(u, k, s, 0), lambda s=s: pv(u, k, s, 1).then_inc(s_pv, 1)]
                        todo = items(s, left)
                        todo = list(todo)
                        for c in "wiwiwiwiii":
                            if c == "i" and todo:
                                misc(todo.pop(0), u, k, n, par, ot_read)
                                n, par = n + 1, 1 - par
                            if c == "w" and work:
                                work.pop(0)()
                n = run_units(pe, prologue, unit)
                for m, item in enumerate(after):
                    misc(item, UNITS, 0, n + m, (n + m) % 2, [n + 1, n + 2])

            @block.vector
            def _(v):
                def misc(item, u, k, n, par):
                    kind, off, hd, i = item
                    w = u + off
                    bank = ps[:, 6 + par, :]
                    v.wait_ge(s_mf, n + 1)
                    if kind == "R":
                        c, half_, sw = i // 2, (i // 2) % 2, i % 2
                        if not (isinstance(w, int) and w == 0 and c < 2):
                            v.wait_ge(s_rc, w * 4 + (c - 1))
                        nc.vector.tensor_tensor((ra, rb)[sw][:, c % 2, :], bank, cs[:, sw, 512 * half_:512 * half_ + 512],
                                                ALU.mult).then_inc(s_mr, 1)
                    elif kind == "A":
                        qt, kh = i // 2, i % 2
                        nc.vector.tensor_reduce(mx[:, hd, kh, qt:qt + 1], bank, AX.X, ALU.max).then_inc(s_mr, 1)
                        if i == 15:
                            v.wait_ge(s_mr, n + 1)
                            nc.vector.tensor_tensor(mm[:, hd, :], mx[:, hd, 0, :], mx[:, hd, 1, :], ALU.max).then_inc(s_mch, 1)
                            v.wait_ge(s_mch, w * 2 + (hd + 1))
                            nc.vector.tensor_scalar(m16[:, hd, :], mm[:, hd, :], 1.0 / MAX_SCALE, None, ALU.mult).then_inc(s_m16, 1)
                    elif kind == "M":
                        if not (isinstance(w, int) and w == 0):
                            v.wait_ge(s_mrow, (w * 2 + hd) * 16)
                        nc.vector.tensor_copy(mt[0:8, hd, :], bank[0:8, 0:P]).then_inc(s_mr, 1)
                    elif kind == "OT":
                        v.wait_ge(s_oh, u * 2 + (i + 1))
                        c_ = slice(4 * i, 4 * i + 4)
                        nc.vector.tensor_tensor(cxt_lo[:, c_, :], bank.rearrange("p (t n) -> p t n", t=4), cxt_hi[:, c_, :],
                                                ALU.subtract).then_inc(s_mr, 1)
                    else:
                        grp = (u + (off + PAIRS)) // PAIRS
                        xo = xg[:, bass.ds(grp, 1), 4 * i:4 * i + 4, :].rearrange("p b t d -> p (b t) d")
                        nc.vector.tensor_tensor(xo, xo, bank.rearrange("p (t d) -> p t d", d=D), ALU.add).then_inc(s_mr, 1)

                def low(g, s):
                    v.wait_ge(s_e32, g + 1)
                    v.wait_ge(s_e16, g + 1)
                    if not (isinstance(g, int) and g == 0):
                        v.wait_ge(s_pv, g)
                    nc.vector.tensor_tensor(p_lo[:, s % 4, 0:DC], p32[:, s % 2, 0:DC], p_hi[:, s % 4, 0:DC],
                                            ALU.subtract).then_inc(s_pd, 1)

                def prologue():
                    v.sem_inc(s_cx, 2)
                    v.sem_inc(s_pd, 1)
                    for n, item in enumerate(before):
                        misc(item, 0, 0, n, n % 2)
                        if n % 2 == 1 and 3 <= n < 11:
                            c = (n - 3) // 2
                            v.wait_ge(s_rh, c + 1)
                            nc.vector.tensor_tensor(r_lo[:, c, :], rc[:, c % 2, :], r_hi[:, c, :], ALU.subtract).then_inc(s_rl, 1)
                    low(0, 0)

                def context(u, grp):
                    hd, qh = grp // 2, grp % 2
                    o = ps[:, 4 + grp % 2, 0:4 * (DH + 1)].rearrange("p (t r) -> p t r", r=DH + 1)
                    v.wait_ge(s_pv, u * STEPS + (4 * grp + 7))
                    nc.vector.reciprocal(rsum, o[:, :, DH]).then_inc(s_rs, 1)
                    v.wait_ge(s_rs, u * 4 + (grp + 1))
                    nc.vector.tensor_tensor(cx[:, 4 * qh:4 * qh + 4, DH * hd:DH * hd + DH], o[:, :, 0:DH],
                                            rsum.unsqueeze(2).broadcast_to([P, 4, DH]), ALU.mult).then_inc(s_cx, 1)

                def unit(u, k, left, n, par):
                    for s in range(STEPS):
                        todo = items(s, left)
                        more = s + 1 < STEPS or left >= 1
                        for m, item in enumerate(todo):
                            misc(item, u, k, n, par)
                            n, par = n + 1, 1 - par
                            if m == min(1, len(todo) - 1) and more:
                                low(u * STEPS + (s + 1), (s + 1) % STEPS)
                        if not todo and more:
                            low(u * STEPS + (s + 1), (s + 1) % STEPS)
                        if s % 4 == 3:
                            context(u, s // 4)
                n = run_units(v, prologue, unit)
                for m, item in enumerate(after):
                    misc(item, UNITS, 0, n + m, (n + m) % 2)

            @block.scalar
            def _(act):
                def exps(g, s):
                    act.wait_ge(s_s, g + 1)
                    if not (isinstance(g, int) and g == 0):
                        act.wait_ge(s_pd, g)
                        act.wait_ge(s_pp, g)
                    sc = ps[:, 2 * (s % 2):2 * (s % 2) + 2, :].rearrange("p b n -> p (b n)")
                    nc.scalar.activation(p32[:, s % 2, :], sc, ACT.Exp, scale=0.125).then_inc(s_e32, 1)
                    if not (isinstance(g, int) and g == 0):
                        act.wait_ge(s_pv, g)
                    nc.scalar.activation(p_hi[:, s % 4, :], sc, ACT.Exp, scale=0.125).then_inc(s_e16, 1)

                def rot_hi(w, c):
                    act.wait_ge(s_rc, w * 4 + (c + 1))
                    if not (isinstance(w, int) and w == 0):
                        act.wait_ge((s_sq, s_sk)[c // 2], w * 96)
                    nc.scalar.copy(r_hi[:, c, :], rc[:, c % 2, :]).then_inc(s_rh, 1)

                def context_hi(i, n, par):
                    act.wait_ge(s_mf, n + 1)
                    bank = ps[:, 6 + par, :].rearrange("p (t n) -> p t n", t=4)
                    nc.scalar.copy(cxt_hi[:, 4 * i:4 * i + 4, :], bank).then_inc(s_oh, 1)

                def prologue():
                    for w in range(2):
                        for c in range(4):
                            rot_hi(w, c)
                    exps(0, 0)

                def unit(u, k, left, n, par):
                    for s in range(STEPS):
                        if s + 1 < STEPS or left >= 1:
                            exps(u * STEPS + (s + 1), (s + 1) % STEPS)
                        for item in items(s, left):
                            if item[0] == "OT":
                                context_hi(item[3], n, par)
                            n, par = n + 1, 1 - par
                        if left >= 2 and s >= ROT_HI and (s - ROT_HI) % 2 == 0 and s < ROT_HI + 8:
                            rot_hi(u + 2, (s - ROT_HI) // 2)
                n = run_units(act, prologue, unit)
                for i in range(2):
                    context_hi(i, n + i, (n + i) % 2)

            @block.gpsimd
            def _(pool):
                def low(g, s):
                    pool.wait_ge(s_e32, g + 1)
                    pool.wait_ge(s_e16, g + 1)
                    if not (isinstance(g, int) and g == 0):
                        pool.wait_ge(s_pv, g)
                    nc.gpsimd.tensor_tensor(p_lo[:, s % 4, DC:], p32[:, s % 2, DC:], p_hi[:, s % 4, DC:],
                                            ALU.subtract).then_inc(s_pp, 1)

                def rot_sum(w, c, read):
                    pool.wait_ge(s_mr, read)
                    if not (isinstance(w, int) and w == 0 and c < 2):
                        pool.wait_ge(s_rl, 4 if isinstance(w, int) and w == 1 and c == 0 else w * 4 + (c - 1))
                    nc.gpsimd.tensor_tensor(rc[:, c % 2, :], ra[:, c % 2, :], rb[:, c % 2, :], ALU.add).then_inc(s_rc, 1)

                def rot_lo(w, c):
                    pool.wait_ge(s_rh, w * 4 + (c + 1))
                    nc.gpsimd.tensor_tensor(r_lo[:, c, :], rc[:, c % 2, :], r_hi[:, c, :], ALU.subtract).then_inc(s_rl, 1)

                def prologue():
                    pool.sem_inc(s_pp, 1)
                    for w in range(2):
                        for c in range(4):
                            rot_sum(w, c, read_before[("R", w, 0, 2 * c + 1)])
                            if w == 1:
                                rot_lo(w, c)
                    low(0, 0)

                def unit(u, k, left, n, par):
                    for s in range(STEPS):
                        if s + 1 < STEPS or left >= 1:
                            low(u * STEPS + (s + 1), (s + 1) % STEPS)
                        if left >= 2:
                            if s >= ROT_SUM and (s - ROT_SUM) % 2 == 0 and s < ROT_SUM + 8:
                                c = (s - ROT_SUM) // 2
                                rot_sum(u + 2, c, n + read_by(("R", 2, 0, 2 * c + 1), left))
                            if s >= ROT_LO and (s - ROT_LO) % 2 == 0 and s < ROT_LO + 8:
                                rot_lo(u + 2, (s - ROT_LO) // 2)
                run_units(pool, prologue, unit)

            @block.sync
            def _(sp):
                def stack(w, slot):
                    for kind, done in ((0, s_sq), (2, s_sk)):
                        for sm in (s_rh, s_rl):
                            sp.wait_ge(sm, w * 4 + (kind + 2))
                        for hd in range(2):
                            rows = slice(64 * hd, 64 * hd + 64)
                            hi, lo = (t[rows, kind:kind + 2, :].rearrange("p c n -> p (c n)") for t in (r_hi, r_lo))
                            if kind == 0:
                                moves = (("Q1", 0, hi), ("Q1", 64, lo), ("Q2", 0, hi))
                            else:
                                moves = (("K1", 0, hi), ("K1", 64, hi), ("K2", 0, lo))
                            for name_, row, src in moves:
                                sp.dma_start(qk[name_][row:row + 64, slot, hd, :], src).then_inc(done, 16)

                def max_row(slot, hd, read):
                    sp.wait_ge(s_mr, read)
                    sp.dma_start(qk["Q2"][64:65, slot, hd, :], mt[0:8, hd, :]).then_inc(s_mrow, 16)

                def prologue():
                    sp.sem_inc(s_mrow, 16)
                    stack(0, 0)
                    stack(1, 1)
                    max_row(0, 0, read_before[("M", 0, 0, 0)])

                def unit(u, k, left, n, par):
                    sp.wait_ge(s_mr, n)
                    if left >= 2:
                        latents_of(sp, u + 2)
                        up_weights(sp, u + 2, k)
                    out_weights(sp, u, k)
                    if left >= 1:
                        sp.wait_ge(s_pv, u * STEPS + 3)
                        latent_rows(sp, u + 1, 1 - k)
                    max_row(k, 1, n + read_by(("M", 0, 1, 0), left))
                    if left >= 1:
                        max_row(1 - k, 0, n + read_by(("M", 1, 0, 0), left))
                    if left >= 2:
                        sp.wait_ge(s_s, (u + 1) * STEPS)
                        stack(u + 2, k)
                run_units(sp, prologue, unit)
        ffn("f2")


_INS = ["x", "wg", "wu", "wd", "wr", "temp", "wdq", "wdkv", "wup", "wuv", "wo", "lns", "lnb", "rope"]


def kernel(L0_attn_x, L0_attn_w_down_q, L0_attn_w_down_kv, L0_attn_w_up_q, L0_attn_w_up_k, L0_attn_w_up_v, L0_attn_w_out,
           L0_attn_ln_scale, L0_attn_ln_bias, L0_ffn_Wg, L0_ffn_Wu, L0_ffn_Wd, L0_ffn_Wr, L0_ffn_temperature):
    import concourse.bacc as bacc
    from concourse.bass_utils import run_bass_kernel_spmd

    given = {
        "x": np.reshape(L0_attn_x, (T, D)), "wg": L0_ffn_Wg, "wu": L0_ffn_Wu, "wd": L0_ffn_Wd, "wr": L0_ffn_Wr,
        "temp": L0_ffn_temperature, "wdq": np.transpose(L0_attn_w_down_q), "wdkv": np.transpose(L0_attn_w_down_kv),
        "wup": up_columns(L0_attn_w_up_q, L0_attn_w_up_k), "wuv": L0_attn_w_up_v,
        "wo": np.transpose(L0_attn_w_out), "lns": L0_attn_ln_scale, "lnb": L0_attn_ln_bias, "rope": rope_tables(),
    }
    nc = bacc.Bacc("TRN2", target_bir_lowering=False, num_devices=1)
    arrays, args = {}, []
    for n in _INS:
        a = np.ascontiguousarray(given[n])
        arrays["in_" + n] = a
        args.append(nc.dram_tensor("in_" + n, a.shape, mybir.dt.from_np(a.dtype), kind="ExternalInput").ap())
    args.append(nc.dram_tensor("out_x", (T, D), F32, kind="ExternalOutput").ap())
    build(nc, *args)
    r = run_bass_kernel_spmd(nc, [arrays], core_ids=[0])
    return np.reshape(r.results[0]["out_x"], (B, S, D))
```
